# Optimizing a Trainium2 kernel written in Bass

```python
import numpy as np
import jax
import jax.numpy as jnp

def _softmax(x, axis=-1):
    return jax.nn.softmax(x, axis=axis)

def _gelu(x):
    return jax.nn.gelu(x, approximate=True)

def _silu(x):
    return jax.nn.silu(x)

def _sigmoid(x):
    return jax.nn.sigmoid(x)

def _layernorm(x, axis=-1, eps=1e-05):
    m = jnp.mean(x, axis=axis, keepdims=True)
    v = jnp.var(x, axis=axis, keepdims=True)
    return (x - m) / jnp.sqrt(v + eps)

def _scatter_add(tgt, idx, src, axis=0):
    return tgt.at[idx].add(src)

def _segment_sum(src, seg, n):
    return jax.ops.segment_sum(src, seg, n)
kernel_name = 'mk_cond_resid_d4_seqx_r8_2f5918'

def setup_inputs(seed: int=0):
    np.random.seed(seed)
    _w = jnp.asarray

    def _rec_inputs():
        import jax
        import jax.numpy as jnp
        _rk = jax.random.key(seed)
        x = -0.003407 + 1.001 * jax.random.normal(jax.random.fold_in(_rk, 1), (32, 32, 256), jnp.float32)
        _lenS = 32 - jax.random.randint(jax.random.fold_in(_rk, 7), (32,), 0, max(1, 32 // 4) + 1, jnp.int32)
        _lenS2 = 32 - jax.random.randint(jax.random.fold_in(_rk, 8), (32,), 0, max(1, 32 // 4) + 1, jnp.int32)
        itok_Bx257_0_4111 = jax.random.randint(jax.random.fold_in(_rk, 11), (32, 257), 0, 514, jnp.int32)
        itok_B_37_3939 = jax.random.randint(jax.random.fold_in(_rk, 12), (32,), 37, 3940, jnp.int32)
        itok_B_1_198 = jax.random.randint(jax.random.fold_in(_rk, 13), (32,), 1, 199, jnp.int32)
        itok_B_0_7 = jax.random.randint(jax.random.fold_in(_rk, 14), (32,), 0, 8, jnp.int32)
        fside_8xS_0 = -0.00162727 + 0.0609077 * jax.random.normal(jax.random.fold_in(_rk, 15), (8, 32), jnp.float32)
        return (x, itok_Bx257_0_4111, itok_B_37_3939, itok_B_1_198, itok_B_0_7, fside_8xS_0)
    x, itok_Bx257_0_4111, itok_B_37_3939, itok_B_1_198, itok_B_0_7, fside_8xS_0 = _rec_inputs()

    def _L0_cond_setup():
        import jax, jax.numpy as jnp
        import numpy as np
        H, G, HD = (8, 4, 32)
        GSZ = H // G
        BLOCK = 16
        WINDOW = 128
        SCALE = 256.0 ** (-0.5)
        EPS = 1e-06
        THETA = 10000.0
        B, T, D = (16, 4, 256)
        NBLK = 257

        def _rms(x, scale):
            var = jnp.mean(x * x, axis=-1, keepdims=True)
            return x * jax.lax.rsqrt(var + EPS) * (1.0 + scale)

        def _rope(x, pos):
            half = HD // 2
            inv = 1.0 / THETA ** (jnp.arange(half, dtype=jnp.float32) / half)
            ang = pos[:, :, None].astype(jnp.float32) * inv
            cos = jnp.cos(ang)[:, None, :, :]
            sin = jnp.sin(ang)[:, None, :, :]
            x1, x2 = (x[..., :half], x[..., half:])
            return jnp.concatenate([x1 * cos - x2 * sin, x2 * cos + x1 * sin], axis=-1)
        key = jax.random.key(seed)
        ks = jax.random.split(key, 10)
        inv_d = 1.0 / np.sqrt(D)
        return {'x': jax.random.normal(ks[0], (B, T, D), jnp.float32), 'Wq': jax.random.normal(ks[1], (H * HD, D), jnp.float32) * inv_d, 'Wk': jax.random.normal(ks[2], (G * HD, D), jnp.float32) * inv_d, 'Wv': jax.random.normal(ks[3], (G * HD, D), jnp.float32) * inv_d, 'Wo': jax.random.normal(ks[4], (D, H * HD), jnp.float32) * inv_d, 'q_norm_scale': jax.random.normal(ks[5], (HD,), jnp.float32) * 0.02, 'k_norm_scale': jax.random.normal(ks[6], (HD,), jnp.float32) * 0.02, 'k_blocks': jax.random.normal(ks[7], (B * NBLK, G, BLOCK, HD), jnp.float32), 'v_blocks': jax.random.normal(ks[8], (B * NBLK, G, BLOCK, HD), jnp.float32), 'block_tables': jnp.arange(B * NBLK, dtype=jnp.int32).reshape(B, NBLK), 'kv_lens': jax.random.randint(ks[9], (B,), 0, 512, dtype=jnp.int32)}
    _L0_cond_all = _L0_cond_setup()
    _L0_cond_in = {k: v for k, v in _L0_cond_all.items() if k in ('Wq', 'Wk', 'Wv', 'Wo', 'q_norm_scale', 'k_norm_scale', 'k_blocks', 'v_blocks')}
    del _L0_cond_all

    def _L1_cond_setup():
        import jax, jax.numpy as jnp
        import numpy as np
        B, C, T = (128, 32, 256)
        S, D = (200, 32)
        key = jax.random.key(seed)
        k1, k2, k3 = jax.random.split(key, 3)
        x = jax.random.normal(k1, (B, C, T), dtype=jnp.float32)
        conditions = jax.random.randint(k2, (B,), 0, S, dtype=jnp.int64)
        weights = jax.random.normal(k3, (S, C, D), dtype=jnp.float32) / jnp.sqrt(jnp.float32(C))
        return {'x': x, 'conditions': conditions, 'weights': weights}
    _L1_cond_all = _L1_cond_setup()
    _L1_cond_in = {k: v for k, v in _L1_cond_all.items() if k in ('weights',)}
    del _L1_cond_all

    def _L2_cond_setup():
        import jax, jax.numpy as jnp
        import numpy as np
        B, C, T = (64, 32, 256)
        D, N = (32, 8)
        key = jax.random.key(seed)
        k_x, k_s, k_w, k_b = jax.random.split(key, 4)
        scale = 1.0 / np.sqrt(C)
        x = jax.random.normal(k_x, (B, C, T), dtype=jnp.float32)
        subjects = jax.random.randint(k_s, (B,), 0, N, dtype=jnp.int64)
        weights = jax.random.normal(k_w, (N, C, D), dtype=jnp.float32) * scale
        bias = jax.random.normal(k_b, (N, D), dtype=jnp.float32) * scale
        return {'x': x, 'subjects': subjects, 'weights': weights, 'bias': bias}
    _L2_cond_all = _L2_cond_setup()
    _L2_cond_in = {k: v for k, v in _L2_cond_all.items() if k in ('weights',)}
    del _L2_cond_all

    def _L3_cond_setup():
        import jax, jax.numpy as jnp
        import numpy as np

        def _lora_linear(x, W, A, B, adapter_indices):
            base = jnp.einsum('bsd,df->bsf', x, W)
            Ai = A[adapter_indices]
            Bi = B[adapter_indices]
            lora = jnp.einsum('bsr,brf->bsf', jnp.einsum('bsd,bdr->bsr', x, Ai), Bi)
            return base + lora
        key = jax.random.key(seed)
        ks = jax.random.split(key, 10)
        H, I, N, R = (256, 1024, 8, 16)
        B, S = (4, 256)
        std_h = 1.0 / np.sqrt(H)
        std_i = 1.0 / np.sqrt(I)
        x = jax.random.normal(ks[0], (B, S, H), dtype=jnp.float32)
        adapter_indices = jax.random.randint(ks[1], (B,), 0, N, dtype=jnp.int32)
        Wg = jax.random.normal(ks[2], (H, I), dtype=jnp.float32) * std_h
        Wu = jax.random.normal(ks[3], (H, I), dtype=jnp.float32) * std_h
        Wd = jax.random.normal(ks[4], (I, H), dtype=jnp.float32) * std_i
        Ag = jax.random.normal(ks[5], (N, H, R), dtype=jnp.float32) * std_h
        Bg = jnp.zeros((N, R, I), dtype=jnp.float32) + 0.01
        Au = jax.random.normal(ks[6], (N, H, R), dtype=jnp.float32) * std_h
        Bu = jnp.zeros((N, R, I), dtype=jnp.float32) + 0.01
        Ad = jax.random.normal(ks[7], (N, I, R), dtype=jnp.float32) * std_i
        Bd = jnp.zeros((N, R, H), dtype=jnp.float32) + 0.01
        return {'x': x, 'Wg': Wg, 'Wu': Wu, 'Wd': Wd, 'Ag': Ag, 'Bg': Bg, 'Au': Au, 'Bu': Bu, 'Ad': Ad, 'Bd': Bd, 'adapter_indices': adapter_indices}
    _L3_cond_all = _L3_cond_setup()
    _L3_cond_in = {k: v for k, v in _L3_cond_all.items() if k in ('Wg', 'Wu', 'Wd', 'Ag', 'Bg', 'Au', 'Bu', 'Ad', 'Bd')}
    del _L3_cond_all
    return {'x': x, 'itok_Bx257_0_4111': itok_Bx257_0_4111, 'itok_B_37_3939': itok_B_37_3939, 'itok_B_1_198': itok_B_1_198, 'itok_B_0_7': itok_B_0_7, 'fside_8xS_0': fside_8xS_0, 'L0_cond_Wq': _L0_cond_in['Wq'], 'L0_cond_Wk': _L0_cond_in['Wk'], 'L0_cond_Wv': _L0_cond_in['Wv'], 'L0_cond_Wo': _L0_cond_in['Wo'], 'L0_cond_q_norm_scale': _L0_cond_in['q_norm_scale'], 'L0_cond_k_norm_scale': _L0_cond_in['k_norm_scale'], 'L0_cond_k_blocks': _L0_cond_in['k_blocks'], 'L0_cond_v_blocks': _L0_cond_in['v_blocks'], 'L1_cond_weights': _L1_cond_in['weights'], 'L2_cond_weights': _L2_cond_in['weights'], 'L3_cond_Wg': _L3_cond_in['Wg'], 'L3_cond_Wu': _L3_cond_in['Wu'], 'L3_cond_Wd': _L3_cond_in['Wd'], 'L3_cond_Ag': _L3_cond_in['Ag'], 'L3_cond_Bg': _L3_cond_in['Bg'], 'L3_cond_Au': _L3_cond_in['Au'], 'L3_cond_Bu': _L3_cond_in['Bu'], 'L3_cond_Ad': _L3_cond_in['Ad'], 'L3_cond_Bd': _L3_cond_in['Bd']}

def reference(x, itok_Bx257_0_4111, itok_B_37_3939, itok_B_1_198, itok_B_0_7, fside_8xS_0, L0_cond_Wq, L0_cond_Wk, L0_cond_Wv, L0_cond_Wo, L0_cond_q_norm_scale, L0_cond_k_norm_scale, L0_cond_k_blocks, L0_cond_v_blocks, L1_cond_weights, L2_cond_weights, L3_cond_Wg, L3_cond_Wu, L3_cond_Wd, L3_cond_Ag, L3_cond_Bg, L3_cond_Au, L3_cond_Bu, L3_cond_Ad, L3_cond_Bd):
    import jax
    import jax.numpy as jnp

    def _L0_cond_ref(x, Wq, Wk, Wv, Wo, q_norm_scale, k_norm_scale, k_blocks, v_blocks, block_tables, kv_lens):
        import jax, jax.numpy as jnp
        import numpy as np
        H, G, HD = (8, 4, 32)
        GSZ = H // G
        BLOCK = 16
        WINDOW = 128
        SCALE = 256.0 ** (-0.5)
        EPS = 1e-06
        THETA = 10000.0
        B, T, D = (16, 4, 256)
        NBLK = 257

        def _rms(x, scale):
            var = jnp.mean(x * x, axis=-1, keepdims=True)
            return x * jax.lax.rsqrt(var + EPS) * (1.0 + scale)

        def _rope(x, pos):
            half = HD // 2
            inv = 1.0 / THETA ** (jnp.arange(half, dtype=jnp.float32) / half)
            ang = pos[:, :, None].astype(jnp.float32) * inv
            cos = jnp.cos(ang)[:, None, :, :]
            sin = jnp.sin(ang)[:, None, :, :]
            x1, x2 = (x[..., :half], x[..., half:])
            return jnp.concatenate([x1 * cos - x2 * sin, x2 * cos + x1 * sin], axis=-1)
        Bx, Tx, _ = x.shape
        q = jnp.einsum('btd,od->bto', x, Wq).reshape(Bx, Tx, H, HD).transpose(0, 2, 1, 3)
        k = jnp.einsum('btd,od->bto', x, Wk).reshape(Bx, Tx, G, HD).transpose(0, 2, 1, 3)
        v = jnp.einsum('btd,od->bto', x, Wv).reshape(Bx, Tx, G, HD).transpose(0, 2, 1, 3)
        q = _rms(q, q_norm_scale)
        k = _rms(k, k_norm_scale)
        pos = kv_lens[:, None] + jnp.arange(Tx, dtype=jnp.int32)
        q = _rope(q, pos)
        k = _rope(k, pos)
        slot = pos // BLOCK
        off = pos % BLOCK
        blk = jnp.take_along_axis(block_tables, slot, axis=1)
        k_blocks = k_blocks.at[blk, :, off, :].set(k.transpose(0, 2, 1, 3))
        v_blocks = v_blocks.at[blk, :, off, :].set(v.transpose(0, 2, 1, 3))
        k_all = k_blocks[block_tables].transpose(0, 2, 1, 3, 4).reshape(Bx, G, -1, HD)
        v_all = v_blocks[block_tables].transpose(0, 2, 1, 3, 4).reshape(Bx, G, -1, HD)
        S = k_all.shape[2]
        qg = q.reshape(Bx, G, GSZ, Tx, HD)
        scores = jnp.einsum('bghtd,bgsd->bghts', qg, k_all) * SCALE
        kpos = jnp.arange(S, dtype=jnp.int32)
        allowed = (kpos[None, None, :] <= pos[:, :, None]) & (kpos[None, None, :] > pos[:, :, None] - WINDOW)
        scores = jnp.where(allowed[:, None, None, :, :], scores, -jnp.inf)
        p = jax.nn.softmax(scores, axis=-1)
        o = jnp.einsum('bghts,bgsd->bghtd', p, v_all).reshape(Bx, H, Tx, HD)
        o = o.transpose(0, 2, 1, 3).reshape(Bx, Tx, H * HD)
        return jnp.einsum('bto,do->btd', o, Wo)

    def _L1_cond_ref(x, conditions, weights):
        import jax, jax.numpy as jnp
        import numpy as np
        B, C, T = (128, 32, 256)
        S, D = (200, 32)
        w = weights[conditions]
        return jnp.einsum('bct,bcd->bdt', x, w)

    def _L2_cond_ref(x, subjects, weights, bias):
        import jax, jax.numpy as jnp
        import numpy as np
        B, C, T = (64, 32, 256)
        D, N = (32, 8)
        w = weights[subjects]
        b = bias[subjects]
        out = jnp.einsum('bct,bcd->bdt', x, w)
        out = out + b[:, :, None]
        return out

    def _L3_cond_ref(x, Wg, Wu, Wd, Ag, Bg, Au, Bu, Ad, Bd, adapter_indices):
        import jax, jax.numpy as jnp
        import numpy as np

        def _lora_linear(x, W, A, B, adapter_indices):
            base = jnp.einsum('bsd,df->bsf', x, W)
            Ai = A[adapter_indices]
            Bi = B[adapter_indices]
            lora = jnp.einsum('bsr,brf->bsf', jnp.einsum('bsd,bdr->bsr', x, Ai), Bi)
            return base + lora
        gate = _lora_linear(x, Wg, Ag, Bg, adapter_indices)
        up = _lora_linear(x, Wu, Au, Bu, adapter_indices)
        h = jax.nn.silu(gate) * up
        return _lora_linear(h, Wd, Ad, Bd, adapter_indices)
    x = x + _L0_cond_ref(x, L0_cond_Wq, L0_cond_Wk, L0_cond_Wv, L0_cond_Wo, L0_cond_q_norm_scale, L0_cond_k_norm_scale, L0_cond_k_blocks, L0_cond_v_blocks, itok_Bx257_0_4111, itok_B_37_3939)
    x = x + _L1_cond_ref(x, itok_B_1_198, L1_cond_weights)
    x = x + _L2_cond_ref(x, itok_B_0_7, L2_cond_weights, fside_8xS_0)
    x = x + _L3_cond_ref(x, L3_cond_Wg, L3_cond_Wu, L3_cond_Wd, L3_cond_Ag, L3_cond_Bg, L3_cond_Au, L3_cond_Bu, L3_cond_Ad, L3_cond_Bd, itok_B_0_7)
    return x

_drawn_inputs = setup_inputs


def setup_inputs(seed=0):
    import zlib

    import numpy as np

    out = dict(_drawn_inputs(seed))
    spreads = {'L3_cond_Bg': (0.009999999776482582, 0.6),
     'L3_cond_Bu': (0.009999999776482582, 0.6),
     'L3_cond_Bd': (0.009999999776482582, 0.6)}
    factors = {'L0_cond_q_norm_scale': 59.049, 'L0_cond_k_norm_scale': 64.0}
    for name, (base, spread) in spreads.items():
        noise = np.random.default_rng([zlib.crc32(name.encode()), seed]).standard_normal(out[name].shape)
        drawn = base * np.exp(spread * noise) if base else spread * noise
        out[name] = jnp.asarray(drawn.astype(out[name].dtype))
    for name, factor in factors.items():
        out[name] = (out[name] * factor).astype(out[name].dtype)
    return out
```

```python
from contextlib import ExitStack

import concourse.bass as bass
import numpy as np
from concourse import mybir

F32 = mybir.dt.float32
F16 = mybir.dt.float16
I32 = mybir.dt.int32
ALU = mybir.AluOpType
ACT = mybir.ActivationFunctionType
AX = mybir.AxisListType

P = 128
B, T, D = 32, 32, 256
H, G, HD = 8, 4, 32
GS = H // G
HALF = HD // 2
BLOCK, WINDOW = 16, 128
NBLK = 257
CACHE_BLOCKS = 16 * NBLK
GB = P // T
NG = B // GB
NPAIR = NG // 2
KD = D // P
SPAN = WINDOW + T
SLOTS = 12
BT = 8
NT = B // BT
BP = BT * SLOTS
BACK = WINDOW // BLOCK
WS = 3
NW = B * WS
KV = 2 * G * HD
BELEMS = G * BLOCK * HD
OLD_ROWS = B * SLOTS * BLOCK
NEW_ROWS = B * T
FF = 1024
NF = FF // P
NR = 128
RANK = 16
SCALE = 256.0 ** -0.5
EPS = 1e-6
THETA = 10000.0
BIG = 2.0 ** 100
TWO_PI = 2.0 * np.pi
PI_PARTS = (6.28125, 0.0019350051879882812, 3.019915981956753e-07)
MAGIC = 1.5 * 2.0 ** 23
PAIR_TOK = 2 * P


def layout(fields):
    at, where = 0, {}
    for name, n in fields:
        where[name] = (at, at + n)
        at += n
    return where, at


C128, C128_N = layout([("ident", P), ("hide", SPAN), ("posbig", SPAN), ("pair", 2), ("sample", GB),
                       ("tok", 1), ("adapter", 1), ("freq", HALF)])
C96, C96_N = layout([("slot", 1), ("table", NT), ("own", NT * BLOCK), ("writer", BT * WS), ("off", BLOCK),
                     ("wslot", 1), ("wrow", 1)])
C32, C32_N = layout([("tok_b", P), ("blk_b", BP), ("wrt_b", NW), ("of_len", NG + NT + 1 + B), ("group", GB * NG)])


def tables():
    p = np.arange(P)
    a = np.zeros((P, C128_N), np.float32)

    def put(arr, where, name, v):
        lo, hi = where[name]
        arr[:, lo:hi] = v

    i = np.arange(SPAN)[None, :]
    t = (p % T)[:, None]
    put(a, C128, "ident", np.eye(P))
    put(a, C128, "hide", np.where((i > t) & (i <= WINDOW + t), 0.0, -BIG))
    put(a, C128, "posbig", i * BIG)
    put(a, C128, "pair", (p[:, None] // HD) % 2 == np.arange(2)[None, :])
    put(a, C128, "sample", p[:, None] // T == np.arange(GB)[None, :])
    put(a, C128, "tok", t)
    put(a, C128, "adapter", p[:, None] // RANK)
    half = np.arange(HALF, dtype=np.float32) / np.float32(HALF)
    put(a, C128, "freq", (np.float32(1.0) / np.power(np.float32(THETA), half))[None, :])
    q = np.arange(BP)
    b = np.zeros((BP, C96_N), np.float32)
    tile = np.arange(NT)[None, :]
    put(b, C96, "slot", (q % SLOTS - BACK)[:, None])
    put(b, C96, "table", (tile * BT + (q // SLOTS)[:, None]) * NBLK)
    own = ((tile[:, :, None] * BT + (q // SLOTS)[:, None, None]) * SLOTS + (q % SLOTS)[:, None, None]) * BLOCK
    put(b, C96, "own", (own + np.arange(BLOCK)[None, None, :]).reshape(BP, -1))
    w = np.arange(BT * WS)[None, :]
    put(b, C96, "writer", q[:, None] == (w // WS) * SLOTS + BACK + w % WS)
    put(b, C96, "off", np.arange(BLOCK)[None, :])
    put(b, C96, "wslot", ((q % WS) * BLOCK)[:, None])
    put(b, C96, "wrow", ((q // WS) * T + 1)[:, None])
    s = np.arange(B)[:, None]
    c = np.zeros((B, C32_N), np.float32)
    put(c, C32, "tok_b", s % GB == p[None, :] // T)
    put(c, C32, "blk_b", s % BT == q[None, :] // SLOTS)
    put(c, C32, "wrt_b", s == np.arange(NW)[None, :] // WS)
    put(c, C32, "of_len", np.concatenate([s // GB == np.arange(NG)[None, :], s // BT == np.arange(NT)[None, :],
                                          np.ones((B, 1)), np.eye(B)], axis=1))
    g = np.arange(GB * NG)[None, :]
    put(c, C32, "group", s == (g % NG) * GB + g // NG)
    return a, b, c


FFN_PIECES = (["lora"] + [f"{k}{f}" for f in range(NF) for k in ("gate", "up")] + ["down_lora"]
              + [f"down{r}{k}" for r in range(2) for k in range(3)])
STAGES = ["kt", "scores", "pt", "pv", "wo", "mix1", "mix2", "xt"]
LOOP_ORDER = (
    ["lora", "gate0", "up0", "gate1", "up1", ("kt", 0), "gate2", ("scores", 0), "up2", "gate3", "up3", "gate4",
     ("pt", 0), "up4", ("pv", 0), "gate5", ("wo", 0), "up5", ("mix1", 0), "gate6", ("mix2", 0), "up6",
     ("xt", 0), ("kt", 1), "gate7", ("scores", 1), "up7", "down_lora", "down00", ("pt", 1), "down01",
     ("pv", 1), "down02", ("wo", 1), "down10", ("mix1", 1), "down11", ("mix2", 1), ("xt", 1), "down12"])


def build(nc, x, table, lens, cond, subj, side, Wq, Wk, Wv, Wo, qs, ks, kb, vb, w1, w2,
          Wg, Wu, Wd, Ag, Bg, Au, Bu, Ad, Bd, c128, c96, c32, out):
    ctx = ExitStack()
    with ctx:
        def sb(name, shape, dt=F32):
            return ctx.enter_context(nc.sbuf_tensor(name, shape, dt))

        def sem(name):
            return ctx.enter_context(nc.semaphore(name))

        kv_rows = nc.dram_tensor("kv_rows", (OLD_ROWS + NEW_ROWS, KV), F32, kind="Internal").ap()
        row_table = nc.dram_tensor("row_table", (B, SLOTS * BLOCK), F32, kind="Internal").ap()
        mix_rows = nc.dram_tensor("mix_rows", (2, B, T * T), F32, kind="Internal").ap()

        k128 = sb("k128", [P, C128_N])
        k96 = sb("k96", [BP, C96_N])
        k32 = sb("k32", [B, C32_N])
        ones = sb("ones", [P, P])
        ones16 = sb("ones16", [BP, BP], F16)

        def c1(name):
            return k128[:, C128[name][0]:C128[name][1]]

        def c9(name):
            return k96[:, C96[name][0]:C96[name][1]]

        def c3(name):
            return k32[:, C32[name][0]:C32[name][1]]

        ident = c1("ident")

        wq_raw = sb("wq_raw", [P, 2, D])
        wk_raw = sb("wk_raw", [P, D])
        wv_raw = sb("wv_raw", [P, D])
        wo_raw = sb("wo_raw", [P, 2, GS, G * HD])
        w_vkq = sb("w_vkq", [P, KD, 512])
        w_o = sb("w_o", [P, GS, D])
        early = sb("early", [P, 2 * BELEMS])
        moved = sb("moved", [P, BLOCK * KV])
        wg = early[:, 0:KD * FF].rearrange("p (k f) -> p k f", k=KD)
        wu = early[:, KD * FF:2 * KD * FF].rearrange("p (k f) -> p k f", k=KD)
        wd = sb("wd", [P, NF, D])
        ag = sb("ag", [P, KD, NR])
        au = sb("au", [P, KD, NR])
        ad = moved[:, 0:NF * NR].rearrange("p (k n) -> p k n", k=NF)
        bg = moved[:, NF * NR:NF * NR + FF]
        bu = moved[:, NF * NR + FF:NF * NR + 2 * FF]
        bd = sb("bd", [NR, D])
        len_i = sb("len_i", [B, 1], I32)
        cond_i = sb("cond_i", [B, 1], I32)
        subj_i = sb("subj_i", [B, 1], I32)
        len_f = sb("len_f", [B, 1])
        subj_f = sb("subj_f", [B, 1])
        scale_qk = sb("scale_qk", [P, 2, HD])
        scale_sw = sb("scale_sw", [P, 2, HD])
        len_sel = sb("len_sel", [B, NG + NT + 1 + B])
        ad_sel = sb("ad_sel", [B, B])
        len_all = sb("len_all", [P, 80])
        adapt = sb("adapt", [NR, B])
        thresh = sb("thresh", [P, B])
        xs = sb("xs", [P, NG, D])
        x_t = sb("x_t", [P, KD, NG, P])
        angle = sb("angle", [P, NG, HALF])
        turn = sb("turn", [P, 2, NG, HALF])
        rest = sb("rest", [P, 2, NG, HALF])
        sincos = sb("sincos", [P, 2, NG, HALF])
        pos = sb("pos", [P, NG])
        rope_c = sb("rope_c", [P, 2, NG, HD])
        rope_s = sb("rope_s", [P, 2, NG, HD])
        NH = G + H
        raw = sb("raw", [P, 2, NH * HD])
        sq = sb("sq", [P, 2, NH * HD])
        roped = sb("roped", [P, 2, NH * HD])
        ssum = sb("ssum", [P, 2 * NH])
        meansq = sb("meansq", [P, 2 * NH])
        minus_half = sb("minus_half", [P, 2 * NH])
        rstd = sb("rstd", [P, 2 * NH])
        far_probs = sb("far_probs", [P, 2 * GB, 2 * P])
        new_kv = far_probs[:, :, :]
        q_rot = sb("q_rot", [P, 2, GS, G * HD])
        q_t = sb("q_t", [P, NG, GS, P])
        slot_i = sb("slot_i", [BP, NT], I32)
        slot_f = sb("slot_f", [BP, NT])
        tidx = sb("tidx", [BP, NT], I32)
        blk_i = sb("blk_i", [BP, NT], I32)
        blk_f = sb("blk_f", [BP, NT])
        k_raw = early[0:BP, 0:BELEMS]
        v_raw = early[0:BP, BELEMS:2 * BELEMS]
        kv_blk = moved[0:BP, :].rearrange("p (o c) -> p o c", c=KV)
        wr_i = sb("wr_i", [BP, 1], I32)
        wr_off = sb("wr_off", [BP, 1])
        wr_d = sb("wr_d", [BP, BLOCK])
        wr_e = sb("wr_e", [BP, BLOCK])
        wr_f = sb("wr_f", [BP, BLOCK])
        wr_diag = sb("wr_diag", [BP, BLOCK, NW], F16)
        wr_all = sb("wr_all", [BP, BLOCK, NW], F16)
        wid_sel = sb("wid_sel", [BP, NT, BT * WS])
        wid_all = sb("wid_all", [BP, NW])
        same = sb("same", [BP, NW], F16)
        cand = sb("cand", [BP, BLOCK, NW], F16)
        winner = sb("winner", [BP, NT * BLOCK])
        won = sb("won", [BP, NT * BLOCK])
        rows = sb("rows", [BP, NT * BLOCK])
        bits_i = sb("bits_i", [B, 4], I32)
        bits = sb("bits", [B, 4])
        row_b = sb("row_b", [B, SLOTS * BLOCK])
        row_d = sb("row_d", [B, SLOTS * BLOCK])
        far_i = sb("far_i", [P, B], I32)
        near_i = sb("near_i", [P, NG], I32)
        mix_raw = sb("mix_raw", [B, 2, T * T])
        mix_w = sb("mix_w", [P, 2, NG, T])
        side_b = sb("side_b", [B, T])
        bias = sb("bias", [P, NG])
        R = range(2)
        idx = [sb(f"idx{r}", [P, GB + 1], I32) for r in R]
        far = [sb(f"far{r}", [P, GB, KV]) for r in R]
        near = [sb(f"near{r}", [P, KV]) for r in R]
        k_t = [sb(f"k_t{r}", [P, GB, SPAN]) for r in R]
        q_bd = [sb(f"q_bd{r}", [P, GB, 2, GS, T]) for r in R]
        mask = [sb(f"mask{r}", [P, GB, SPAN]) for r in R]
        prob = [sb(f"prob{r}", [P, GB, 2, SPAN]) for r in R]
        prob_near = [sb(f"prob_near{r}", [P, 2, GB, T]) for r in R]
        top = [sb(f"top{r}", [P, GB * 2]) for r in R]
        ntop = [sb(f"ntop{r}", [P, GB * 2]) for r in R]
        den = [sb(f"den{r}", [P, GB * 2]) for r in R]
        rden = [sb(f"rden{r}", [P, GB * 2]) for r in R]
        p_far = [far_probs[:, GB * r:GB * (r + 1), :] for r in R]
        p_near = [sb(f"p_near{r}", [P, GB, 2 * P]) for r in R]
        o_t = [sb(f"o_t{r}", [P, GS, GB, T]) for r in R]
        w_mix = [sb(f"w_mix{r}", [P, 2, GB, T]) for r in R]
        x1 = [sb(f"x1_{r}", [P, D]) for r in R]
        x2 = [sb(f"x2_{r}", [P, D]) for r in R]
        x3 = [sb(f"x3_{r}", [P, D]) for r in R]
        x3_t = sb("x3_t", [P, KD, 2, P])
        xf = sb("xf", [P, KD, PAIR_TOK])
        low = sb("low", [NR, 2, PAIR_TOK])
        th = [sb(f"th{r}", [P, PAIR_TOK]) for r in range(3)]
        gs = [sb(f"gs{r}", [P, PAIR_TOK]) for r in R]
        h_t = x_t[:, :, :, :].rearrange("p k g t -> p (k g t)").rearrange("p (f t) -> p f t", t=PAIR_TOK)
        low_d = sb("low_d", [NR, PAIR_TOK])
        bank = [ctx.enter_context(nc.psum_tensor(f"bank{n}", [P, 512], F32)) for n in range(8)]

        small_in = sem("small_in")
        k128_in = sem("k128_in")
        scale_in = sem("scale_in")
        x_in = sem("x_in")
        wvkq_in = sem("wvkq_in")
        wo_in = sem("wo_in")
        ffn_in = sem("ffn_in")
        mix_idx_in = sem("mix_idx_in")
        ones_set = sem("ones_set")
        sel_ready = sem("sel_ready")
        len_psum = sem("len_psum")
        len_ready = sem("len_ready")
        tidx_ready = sem("tidx_ready")
        blk_in = sem("blk_in")
        blk_ready = sem("blk_ready")
        k_in = sem("k_in")
        v_in = sem("v_in")
        k_moved = sem("k_moved")
        v_moved = sem("v_moved")
        blk_out = sem("blk_out")
        new_out = sem("new_out")
        xt_psum = sem("xt_psum")
        xt_ready = sem("xt_ready")
        w_psum = sem("w_psum")
        w_ready = sem("w_ready")
        arg_ready = sem("arg_ready")
        sin_ready = sem("sin_ready")
        rope_ready = sem("rope_ready")
        vkq_psum = sem("vkq_psum")
        raw_ready = sem("raw_ready")
        cos_part = sem("cos_part")
        meansq_ready = sem("meansq_ready")
        rstd_ready = sem("rstd_ready")
        kq_ready = sem("kq_ready")
        qt_psum = sem("qt_psum")
        qt_ready = sem("qt_ready")
        diag_ready = sem("diag_ready")
        wr_psum = sem("wr_psum")
        wr_ready = sem("wr_ready")
        widsel_ready = sem("widsel_ready")
        wid_psum = sem("wid_psum")
        rows_ready = sem("rows_ready")
        rows_out = sem("rows_out")
        rows_in = sem("rows_in")
        shift_ready = sem("shift_ready")
        place_psum = sem("place_psum")
        place_ready = sem("place_ready")
        mix_in = sem("mix_in")
        side_in = sem("side_in")
        mix_out = sem("mix_out")
        mix_back = sem("mix_back")
        vector_order = sem("vector_order")
        idx_ready = sem("idx_ready")
        kv_in = [sem(f"kv_in{r}") for r in R]
        qbd_ready = sem("qbd_ready")
        mask_ready = sem("mask_ready")
        wmix_ready = sem("wmix_ready")
        kt_psum = sem("kt_psum")
        far_kt_ready = sem("far_kt_ready")
        near_kt_ready = sem("near_kt_ready")
        scores_psum = sem("scores_psum")
        top_ready = sem("top_ready")
        ntop_ready = sem("ntop_ready")
        exp_ready = sem("exp_ready")
        rden_ready = sem("rden_ready")
        prob_ready = sem("prob_ready")
        pfar_psum = sem("pfar_psum")
        pnear_psum = sem("pnear_psum")
        pfar0_ready = sem("pfar0_ready")
        pfar1_ready = sem("pfar1_ready")
        pnear_ready = sem("pnear_ready")
        o_psum = sem("o_psum")
        o_ready = sem("o_ready")
        wo_psum = sem("wo_psum")
        x1_ready = sem("x1_ready")
        mix1_psum = sem("mix1_psum")
        x2_ready = sem("x2_ready")
        mix2_psum = sem("mix2_psum")
        x3_ready = sem("x3_ready")
        x3_kept = sem("x3_kept")
        x3t_psum = sem("x3t_psum")
        x3t_ready = sem("x3t_ready")
        xf_ready = sem("xf_ready")
        low_psum = sem("low_psum")
        low_ready = sem("low_ready")
        gu_psum = sem("gu_psum")
        tanh_ready = sem("tanh_ready")
        gs_ready = sem("gs_ready")
        h_ready = sem("h_ready")
        lowd_psum = sem("lowd_psum")
        lowd_ready = sem("lowd_ready")
        down_psum = sem("down_psum")
        y_ready = sem("y_ready")
        y_out = sem("y_out")

        def over(ap, axis, n):
            ap = ap.unsqueeze(axis)
            shape = list(ap.shape)
            shape[axis] = n
            return ap.broadcast_to(shape)

        LOW_BANKS, HIGH_BANKS = bank[0:4], bank[4:8]
        FFN_BANKS = bank[4:8]
        SCORE = slice(0, 2 * SPAN)

        block = ctx.enter_context(nc.Block())

        @block.sync
        def _(sp):
            sp.dma_start(len_i[:, :], lens.rearrange("(b o) -> b o", o=1)).then_inc(small_in, 16)
            sp.dma_start(k32[:, :], c32).then_inc(small_in, 16)
            sp.dma_start(k96[:, :], c96).then_inc(small_in, 16)
            sp.dma_start(k128[:, :], c128).then_inc(k128_in, 16)
            sp.dma_start(xs[:, :, :], x.rearrange("(g s) t d -> (s t) g d", s=GB)).then_inc(x_in, 16)
            sp.dma_start(wv_raw[:, :], Wv).then_inc(wvkq_in, 16)
            sp.dma_start(wk_raw[:, :], Wk).then_inc(wvkq_in, 16)
            sp.dma_start(wq_raw[:, :, :], Wq.rearrange("(a p) d -> p a d", p=P)).then_inc(wvkq_in, 16)
            for a in range(2):
                for h in range(GS):
                    sp.dma_start(wo_raw[:, a, h, :].rearrange("p (g d) -> p g d", g=G),
                                 Wo[a * P:(a + 1) * P, :].rearrange("p (g h d) -> p g h d", g=G, h=GS)[:, :, h, :]
                                 ).then_inc(wo_in, 16)
            for t in range(NT):
                sp.wait_ge(raw_ready, t + 1)
                sp.wait_ge(kq_ready, 2 * t + 1)
                lo = OLD_ROWS + 2 * t * P
                sp.dma_start(kv_rows[lo:lo + 2 * P, :].rearrange("(g p) c -> p g c", p=P),
                             new_kv[:, 2 * t:2 * t + 2, :]).then_inc(new_out, 16)
                sp.wait_ge(k_moved, t + 1)
                sp.wait_ge(v_moved, t + 1)
                sp.dma_start(kv_rows[t * BP * BLOCK:(t + 1) * BP * BLOCK, :].rearrange("(p o) c -> p (o c)", o=BLOCK),
                             kv_blk[:, :, :].rearrange("p o c -> p (o c)")).then_inc(blk_out, 16)
            sp.dma_start(wd[:, :, :], Wd.rearrange("(k p) f -> p k f", p=P)).then_inc(ffn_in, 16)
            for dst, src in ((ag[:, :, :], Ag), (au[:, :, :], Au)):
                for k in range(KD):
                    sp.dma_start(dst[:, k, :].rearrange("p (n r) -> p n r", r=RANK),
                                 src[:, k * P:(k + 1) * P, :].rearrange("n p r -> p n r")).then_inc(ffn_in, 16)
            sp.dma_start(wg[:, :, :], Wg.rearrange("(k p) f -> p k f", p=P)).then_inc(ffn_in, 16)
            sp.dma_start(wu[:, :, :], Wu.rearrange("(k p) f -> p k f", p=P)).then_inc(ffn_in, 16)
            sp.wait_ge(blk_out, 16 * NT)
            sp.dma_start(bg[:, :], Bg.rearrange("n r f -> (n r) f")).then_inc(ffn_in, 16)
            sp.dma_start(bu[:, :], Bu.rearrange("n r f -> (n r) f")).then_inc(ffn_in, 16)
            for k in range(NF):
                sp.dma_start(ad[:, k, :].rearrange("p (n r) -> p n r", r=RANK),
                             Ad[:, k * P:(k + 1) * P, :].rearrange("n p r -> p n r")).then_inc(ffn_in, 16)
            sp.dma_start(bd[:, :], Bd.rearrange("n r f -> (n r) f")).then_inc(ffn_in, 16)

            def store(m):
                for r in R:
                    sp.wait_ge(y_ready, 2 * m + r + 1)
                    sp.dma_start(out[bass.ds(m * 2 * GB + GB * r, GB), :, :].rearrange("s t d -> (s t) d"),
                                 xs[:, bass.ds(2 * m + r, 1), :].rearrange("p a d -> p (a d)")).then_inc(y_out, 16)

            with sp.Fori(0, NPAIR) as m:
                store(m)
            sp.wait_ge(y_out, 16 * NG)

        FFN_LOADS = 2 * KD + 4 + NF + 2

        @block.gpsimd
        def _(pool):
            pool.memset(ones[:, :], 1.0).then_inc(ones_set, 1)
            pool.memset(ones16[:, :], 1.0).then_inc(ones_set, 1)
            pool.memset(minus_half[:, :], -0.5).then_inc(ones_set, 1)
            pool.wait_ge(tidx_ready, 1)
            for t in range(NT):
                pool.indirect_dma_start(
                    blk_i[:, t:t + 1], None, table.rearrange("b (n o) -> (b n) o", o=1),
                    bass.IndirectOffsetOnAxis(ap=tidx[:, t:t + 1], axis=0)).then_inc(blk_in, 16)
            pool.wait_ge(mix_idx_in, 32)
            for n, (w, i) in enumerate(((w1, cond_i), (w2, subj_i))):
                pool.indirect_dma_start(mix_raw[:, n, :], None, w.rearrange("n c d -> n (c d)"),
                                        bass.IndirectOffsetOnAxis(ap=i[:, :], axis=0)).then_inc(mix_in, 16)
            pool.indirect_dma_start(side_b[:, :], None, side,
                                    bass.IndirectOffsetOnAxis(ap=subj_i[:, :], axis=0)).then_inc(side_in, 16)
            pool.wait_ge(blk_in, 16 * NT)

            def load_blocks(t):
                if t:
                    pool.wait_ge(k_moved, t)
                pool.indirect_dma_start(k_raw[:, :], None, kb.rearrange("n g o d -> n (g o d)"),
                                        bass.IndirectOffsetOnAxis(ap=blk_i[:, t:t + 1], axis=0)).then_inc(k_in, 16)
                if t:
                    pool.wait_ge(v_moved, t)
                pool.indirect_dma_start(v_raw[:, :], None, vb.rearrange("n g o d -> n (g o d)"),
                                        bass.IndirectOffsetOnAxis(ap=blk_i[:, t:t + 1], axis=0)).then_inc(v_in, 16)

            def cos_half(i):
                pool.wait_ge(raw_ready, i + 1)
                if i == 0:
                    pool.wait_ge(rope_ready, 1)
                else:
                    pool.wait_ge(kq_ready, 2 * i)
                for n, (lo, nh) in enumerate(((0, G), (G, H))):
                    cols = slice(lo * HD, (lo + nh) * HD)
                    pool.tensor_tensor(roped[:, :, cols].rearrange("p t (h d) -> p t h d", d=HD),
                                       raw[:, :, cols].rearrange("p t (h d) -> p t h d", d=HD),
                                       over(rope_c[:, n, 2 * i:2 * i + 2, :], 2, nh), ALU.mult).then_inc(cos_part, 1)
                pool.wait_ge(ones_set, 3)
                pool.wait_ge(meansq_ready, i + 1)
                pool.tensor_tensor(rstd[:, :], meansq[:, :], minus_half[:, :], ALU.pow).then_inc(rstd_ready, 1)

            for t in range(NT):
                load_blocks(t)
                cos_half(t)

            def prepare(n, r, pair):
                if pair is not None:
                    pool.wait_ge(kv_in[r], pair * (GB + 1) * 16)
                pool.tensor_copy(idx[r][:, 0:GB], far_i[:, bass.ds(GB * n, GB)]).then_inc(idx_ready, 1)
                pool.tensor_copy(idx[r][:, GB:GB + 1], near_i[:, bass.ds(n, 1)]).then_inc(idx_ready, 1)
                pool.wait_ge(idx_ready, 2 * n + 2)
                if pair is not None:
                    pool.wait_ge(o_psum, n - 1)
                pool.nop(nofuse=True)
                for s in range(GB):
                    pool.indirect_dma_start(far[r][:, s, :], None, kv_rows,
                                            bass.IndirectOffsetOnAxis(ap=idx[r][:, s:s + 1], axis=0)
                                            ).then_inc(kv_in[r], 16)
                pool.indirect_dma_start(near[r][:, :], None, kv_rows,
                                        bass.IndirectOffsetOnAxis(ap=idx[r][:, GB:GB + 1], axis=0)
                                        ).then_inc(kv_in[r], 16)
                for h in range(GS):
                    src = q_t[:, bass.ds(n, 1), h, :].rearrange("p a (s t) -> p (a s) t", s=GB)
                    pool.tensor_tensor(q_bd[r][:, :, :, h, :], over(src, 2, 2),
                                       over(over(c1("pair"), 1, GB), 3, T), ALU.mult).then_inc(qbd_ready, 1)
                for w in range(2):
                    src = mix_w[:, w, bass.ds(n, 1), :].rearrange("p a d -> p (a d)")
                    pool.tensor_tensor(w_mix[r][:, w, :, :], over(src, 1, GB), over(c1("sample"), 2, T),
                                       ALU.mult).then_inc(wmix_ready, 1)

            def normalise(n, r):
                for half in range(2):
                    pool.wait_ge(rden_ready, 2 * n + half + 1)
                    s = slice(2 * half, 2 * half + 2)
                    v = prob[r][:, s, :, 0:P].rearrange("p s c i -> p (s c) i")
                    scale = rden[r][:, 4 * half:4 * half + 4]
                    pool.tensor_tensor(v, v, over(scale, 2, P), ALU.mult).then_inc(prob_ready, 1)
                    pool.tensor_tensor(prob_near[r][:, :, s, :].rearrange("p c s i -> p s c i"),
                                       prob[r][:, s, :, P:SPAN],
                                       over(scale.rearrange("p (s c) -> p s c", c=2), 3, T),
                                       ALU.mult).then_inc(prob_ready, 1)

            def keep(n, r):
                pool.wait_ge(x3_ready, n + 1)
                pool.tensor_copy(xs[:, bass.ds(n, 1), :].rearrange("p a d -> p (a d)"), x3[r][:, :]).then_inc(x3_kept, 1)

            pool.wait_ge(place_ready, 3)
            pool.wait_ge(blk_out, 16 * NT)
            pool.wait_ge(new_out, 16 * NT)
            pool.wait_ge(qt_ready, NT)
            pool.wait_ge(mix_back, 32)
            for r in R:
                prepare(r, r, None)
            for r in R:
                normalise(r, r)
            for r in R:
                keep(r, r)

            with pool.Fori(0, NPAIR - 1) as m:
                for r in R:
                    prepare(2 * m + 2 + r, r, m + 1)
                for step in LOOP_ORDER:
                    if step[0] == "scores":
                        normalise(2 * m + 2 + step[1], step[1])
                    elif step[0] == "mix2":
                        keep(2 * m + 2 + step[1], step[1])

        @block.scalar
        def _(act):
            act.dma_start(cond_i[:, :], cond.rearrange("(b o) -> b o", o=1)).then_inc(mix_idx_in, 16)
            act.dma_start(subj_i[:, :], subj.rearrange("(b o) -> b o", o=1)).then_inc(mix_idx_in, 16)
            for n, s in enumerate((ks, qs)):
                act.dma_start(scale_qk[:, n, :], s.partition_broadcast(P)).then_inc(scale_in, 16)
            for n in range(2):
                act.wait_ge(xt_psum, 2 * n + 1)
                act.copy(x_t[:, n, 0:4, :].rearrange("p g t -> p (g t)"), bank[1 + 2 * n][:, :]).then_inc(xt_ready, 1)
            act.wait_ge(w_psum, 1)
            act.copy(w_vkq[:, 0, :], bank[5][:, :]).then_inc(w_ready, 1)
            act.wait_ge(arg_ready, 1)
            act.activation(sincos[:, :, :, :].rearrange("p a g f -> p (a g f)"),
                           rest[:, :, :, :].rearrange("p a g f -> p (a g f)"), ACT.Sin).then_inc(sin_ready, 1)
            act.wait_ge(wr_psum, 1)
            for n in range(3):
                act.copy(wr_all[:, :, :].rearrange("p o w -> p (o w)")[:, 512 * n:512 * (n + 1)],
                         bank[1 + n][0:BP, :]).then_inc(wr_ready, 1)

            def evacuate(i):
                act.wait_ge(vkq_psum, i + 1)
                if i:
                    act.wait_ge(kq_ready, 2 * i)
                for t in range(2):
                    src = bank[4 + 2 * (i % 2) + t]
                    act.copy(new_kv[:, 2 * i + t, G * HD:KV], src[:, 0:G * HD])
                    last = act.copy(raw[:, t, :], src[:, G * HD:512])
                last.then_inc(raw_ready, 1)

            def move_k(t):
                act.wait_ge(k_in, 16 * (t + 1))
                if t:
                    act.wait_ge(blk_out, 16 * t)
                act.copy(kv_blk[:, :, 0:G * HD].rearrange("p o (g d) -> p o g d", d=HD),
                         k_raw[:, :].rearrange("p (g o d) -> p o g d", g=G, d=HD)).then_inc(k_moved, 1)

            for i in range(NT):
                evacuate(i)
                move_k(i)
                act.wait_ge(qt_psum, i + 1)
                act.copy(q_t[:, 2 * i:2 * i + 2, :, :].rearrange("p g h t -> p (g h t)"),
                         bank[i % 2 + 2][:, :]).then_inc(qt_ready, 1)
            act.wait_ge(mix_in, 32)
            for n in range(2):
                act.dma_start(mix_rows[n, :, :], mix_raw[:, n, :]).then_inc(mix_out, 16)
            act.wait_ge(mix_out, 32)
            for n in range(2):
                act.dma_start(mix_w[:, n, :, :],
                              mix_rows[n, :, :].rearrange("(g s) (c d) -> (s c) g d", s=GB, d=T)).then_inc(mix_back, 16)

            act.wait_ge(rows_ready, 1)
            act.dma_start(row_table.rearrange("(t b) (j o) -> (b j) t o", t=NT, o=BLOCK),
                          rows[:, :].rearrange("p (t o) -> p t o", t=NT)).then_inc(rows_out, 16)
            act.wait_ge(rows_out, 16)
            act.dma_start(row_b[:, :], row_table).then_inc(rows_in, 16)

            def attention(stage, n, r, b, pair):
                if stage == "kt":
                    act.wait_ge(kt_psum, n + 1)
                    act.copy(k_t[r][:, :, 0:P], b[0][:, :].rearrange("p (s i) -> p s i", s=GB)).then_inc(far_kt_ready, 1)
                elif stage == "scores":
                    for half in range(2):
                        act.wait_ge(ntop_ready, 2 * n + half + 1)
                        for j in range(4 * half, 4 * half + 4):
                            v = prob[r][:, j // 2, j % 2, :]
                            last = act.activation(v, v, ACT.Exp, bias=ntop[r][:, j:j + 1], scale=SCALE,
                                                  accum_out=den[r][:, j:j + 1])
                        last.then_inc(exp_ready, 1)
                elif stage == "pt":
                    act.wait_ge(pfar_psum, 2 * n + 1)
                    act.copy(p_far[r][:, 0:2, :].rearrange("p s c -> p (s c)"), b[2][:, :]).then_inc(pfar0_ready, 1)
                elif stage == "pv":
                    act.wait_ge(o_psum, n + 1)
                    act.copy(o_t[r][:, :, :, :].rearrange("p h s t -> p s h t"),
                             b[1][:, 0:2 * P].rearrange("p (s h t) -> p s h t", s=GB, h=GS)).then_inc(o_ready, 1)
                elif stage == "xt":
                    act.wait_ge(x3t_psum, n + 1)
                    act.copy(x3_t[:, :, r, :], b[0][:, 0:2 * P].rearrange("p (k t) -> p k t", k=KD)
                             ).then_inc(x3t_ready, 1)

            def ffn(piece, m):
                if piece.startswith("up"):
                    f = int(piece[2:])
                    act.wait_ge(gu_psum, NF * m + f + 1)
                    act.activation(th[f % 3][:, :], FFN_BANKS[f % 3][:, 0:PAIR_TOK], ACT.Tanh,
                                   scale=0.5).then_inc(tanh_ready, 1)

            for stage in STAGES:
                for r in R:
                    attention(stage, r, r, (LOW_BANKS, HIGH_BANKS)[r], 0)
            with act.Fori(0, NPAIR - 1) as m:
                for step in LOOP_ORDER:
                    if isinstance(step, str):
                        ffn(step, m)
                    else:
                        stage, r = step
                        attention(stage, 2 * m + 2 + r, r, LOW_BANKS, m + 1)
            for piece in FFN_PIECES:
                ffn(piece, NPAIR - 1)

        @block.vector
        def _(dve):
            count = [0]

            def then(ins):
                count[0] += 1
                ins.then_inc(vector_order, 1)
                dve.wait_ge(vector_order, count[0])

            dve.wait_ge(small_in, 48)
            then(dve.tensor_copy(len_f[:, :], len_i[:, :]))
            then(dve.tensor_scalar(len_sel[:, :], c3("of_len"), len_f[:, 0:1], None, ALU.mult))
            dve.wait_ge(mix_idx_in, 32)
            then(dve.tensor_copy(subj_f[:, :], subj_i[:, :]))
            dve.tensor_scalar(ad_sel[:, :], c3("of_len")[:, NG + NT + 1:], subj_f[:, 0:1], None,
                              ALU.mult).then_inc(sel_ready, 1)
            dve.wait_ge(len_psum, 1)
            then(dve.tensor_copy(len_all[:, 0:NG], bank[0][:, 0:NG]))
            then(dve.tensor_copy(len_all[0:BP, NG:NG + NT + 1], bank[0][0:BP, NG:NG + NT + 1]))
            then(dve.tensor_copy(len_all[:, 16:80], bank[0][:, 16:80]))
            then(dve.tensor_copy(slot_i[:, :], len_all[0:BP, NG:NG + NT]))
            then(dve.tensor_scalar(slot_i[:, :], slot_i[:, :], 4, None, ALU.logical_shift_right))
            then(dve.tensor_scalar(slot_f[:, :], slot_i[:, :], c9("slot"), 0.0, ALU.add, ALU.max))
            dve.scalar_tensor_tensor(tidx[:, :], slot_f[:, :], float(NBLK - 1), c9("table"), ALU.min,
                                     ALU.add).then_inc(tidx_ready, 1)
            then(dve.tensor_copy(wr_i[:, :], len_all[0:BP, NG + NT:NG + NT + 1]))
            then(dve.tensor_scalar(wr_i[:, :], wr_i[:, :], BLOCK - 1, None, ALU.bitwise_and))
            then(dve.tensor_copy(wr_off[:, :], wr_i[:, :]))
            then(dve.tensor_tensor(wr_off[:, :], c9("wslot"), wr_off[:, :], ALU.subtract))
            then(dve.tensor_scalar(wr_d[:, :], c9("off"), wr_off[:, 0:1], None, ALU.add))
            then(dve.tensor_scalar(wr_e[:, :], wr_d[:, :], c9("wrow"), None, ALU.add))
            then(dve.scalar_tensor_tensor(wr_f[:, :], wr_d[:, :], 0.0, wr_e[:, :], ALU.is_ge, ALU.mult))
            then(dve.scalar_tensor_tensor(wr_e[:, :], wr_d[:, :], float(T - 1), wr_f[:, :], ALU.is_le, ALU.mult))
            dve.wait_ge(k128_in, 16)
            dve.tensor_tensor(wr_diag[:, :, :], over(ident[0:BP, 0:NW], 1, BLOCK), over(wr_e[:, :], 2, NW),
                              ALU.mult).then_inc(diag_ready, 1)
            then(dve.tensor_scalar(pos[:, :], len_all[:, 0:NG], c1("tok"), None, ALU.add))
            then(dve.tensor_tensor(angle[:, :, :], over(pos[:, :], 2, HALF), over(c1("freq"), 1, NG), ALU.mult))
            flat = angle[:, :, :].rearrange("p g f -> p (g f)")
            t2 = turn[:, :, :, :].rearrange("p a g f -> p a (g f)")
            r2 = rest[:, :, :, :].rearrange("p a g f -> p a (g f)")
            then(dve.tensor_scalar(t2[:, 0, :], flat, 1.0 / TWO_PI, None, ALU.mult))
            then(dve.tensor_scalar(t2[:, 1, :], flat, 1.0 / TWO_PI, 0.25, ALU.mult, ALU.add))
            then(dve.tensor_scalar(t2, t2, MAGIC, None, ALU.add))
            then(dve.tensor_scalar(t2, t2, -MAGIC, None, ALU.add))
            then(dve.scalar_tensor_tensor(r2, t2, -PI_PARTS[0], over(flat, 1, 2), ALU.mult, ALU.add))
            then(dve.scalar_tensor_tensor(r2, t2, -PI_PARTS[1], r2, ALU.mult, ALU.add))
            then(dve.scalar_tensor_tensor(r2, t2, -PI_PARTS[2], r2, ALU.mult, ALU.add))
            then(dve.tensor_scalar(r2[:, 1, :], r2[:, 1, :], float(np.pi / 2), None, ALU.add))
            dve.tensor_scalar(r2, r2, 3.1415925, -3.1415925, ALU.min, ALU.max).then_inc(arg_ready, 1)
            for n in range(2):
                dve.wait_ge(xt_psum, 2 * n + 2)
                dve.tensor_copy(x_t[:, n, 4:8, :].rearrange("p g t -> p (g t)"), bank[2 + 2 * n][:, :]
                                ).then_inc(xt_ready, 1)
            dve.wait_ge(w_psum, 2)
            dve.tensor_copy(w_vkq[:, 1, :], bank[6][:, :]).then_inc(w_ready, 1)
            dve.wait_ge(w_psum, 3)
            dve.tensor_copy(w_o[:, :, :].rearrange("p h d -> p (h d)"), bank[7][:, :]).then_inc(w_ready, 1)
            dve.wait_ge(scale_in, 32)
            then(dve.tensor_scalar(scale_qk[:, :, :], scale_qk[:, :, :], 1.0, None, ALU.add))
            then(dve.tensor_scalar(scale_sw[:, :, 0:HALF], scale_qk[:, :, HALF:HD], -1.0, None, ALU.mult))
            then(dve.tensor_copy(scale_sw[:, :, HALF:HD], scale_qk[:, :, 0:HALF]))
            dve.wait_ge(sin_ready, 1)
            for n in range(2):
                for dst, trig, s in ((rope_c, 1, scale_qk), (rope_s, 0, scale_sw)):
                    last = dve.tensor_tensor(dst[:, n, :, :].rearrange("p g (a f) -> p g a f", a=2),
                                             over(sincos[:, trig, :, :], 2, 2),
                                             over(s[:, n, :].rearrange("p (a f) -> p a f", a=2), 1, NG), ALU.mult)
                    if (n, trig) != (1, 0):
                        then(last)
            last.then_inc(rope_ready, 1)
            then(dve.tensor_scalar(thresh[:, :], len_all[:, 16:16 + B], -BIG, BIG * WINDOW, ALU.mult, ALU.add))
            then(dve.tensor_scalar(adapt[:, :], len_all[:, 48:48 + B], c1("adapter"), None, ALU.is_equal))
            dve.wait_ge(blk_in, 16 * NT)
            then(dve.tensor_copy(blk_f[:, :], blk_i[:, :]))
            dve.tensor_tensor(wid_sel[:, :, :], over(c9("writer"), 1, NT), over(blk_f[:, :], 2, BT * WS),
                              ALU.mult).then_inc(widsel_ready, 1)

            def move_v(t):
                dve.wait_ge(v_in, 16 * (t + 1))
                if t:
                    dve.wait_ge(blk_out, 16 * t)
                dve.tensor_copy(kv_blk[:, :, G * HD:KV].rearrange("p o (g d) -> p o g d", d=HD),
                                v_raw[:, :].rearrange("p (g o d) -> p o g d", g=G, d=HD)).then_inc(v_moved, 1)

            def norm_rope(i):
                dve.wait_ge(raw_ready, i + 1)
                NC = NH * HD
                h4 = [a[:, :, :].rearrange("p t (h d) -> p (t h) d", d=HD) for a in (raw, sq, roped)]
                then(dve.tensor_tensor(sq[:, :, :], raw[:, :, :], raw[:, :, :], ALU.mult))
                then(dve.tensor_reduce(ssum[:, :], h4[1], AX.X, ALU.add))
                dve.tensor_scalar(meansq[:, :], ssum[:, :], 1.0 / HD, EPS, ALU.mult, ALU.add).then_inc(meansq_ready, 1)
                for n, (lo, nh) in enumerate(((0, G), (G, H))):
                    cols = slice(lo * HD, (lo + nh) * HD)
                    src = raw[:, :, cols].rearrange("p t (h d) -> p t h d", d=HD)
                    dst = sq[:, :, cols].rearrange("p t (h d) -> p t h d", d=HD)
                    for a in range(2):
                        mine, other = slice(a * HALF, (a + 1) * HALF), slice((1 - a) * HALF, (2 - a) * HALF)
                        then(dve.tensor_tensor(dst[:, :, :, mine], src[:, :, :, other],
                                               over(rope_s[:, n, 2 * i:2 * i + 2, mine], 2, nh), ALU.mult))
                dve.wait_ge(cos_part, 2 * i + 2)
                then(dve.tensor_tensor(sq[:, :, :], sq[:, :, :], roped[:, :, :], ALU.add))
                dve.wait_ge(rstd_ready, i + 1)
                r4 = rstd[:, :].rearrange("p (t h) -> p t h", t=2)
                dve.tensor_tensor(new_kv[:, 2 * i:2 * i + 2, 0:G * HD].rearrange("p t (h d) -> p t h d", d=HD),
                                  sq[:, :, 0:G * HD].rearrange("p t (h d) -> p t h d", d=HD),
                                  over(r4[:, :, 0:G], 3, HD), ALU.mult).then_inc(kq_ready, 1)
                if i:
                    dve.wait_ge(qt_psum, i)
                for h in range(GS):
                    last = dve.tensor_tensor(q_rot[:, :, h, :].rearrange("p t (g d) -> p t g d", d=HD),
                                             sq[:, :, G * HD:].rearrange("p t (g h d) -> p t g h d", h=GS, d=HD)
                                             [:, :, :, h, :],
                                             over(r4[:, :, G:].rearrange("p t (g h) -> p t g h", h=GS)[:, :, :, h],
                                                  3, HD), ALU.mult)
                last.then_inc(kq_ready, 1)
                dve.wait_ge(kq_ready, 2 * i + 2)

            def find_winners(t):
                then(dve.tensor_scalar(same[:, :], wid_all[:, :], blk_f[:, t:t + 1], None, ALU.is_equal))
                then(dve.tensor_tensor(cand[:, :, :], wr_all[:, :, :], over(same[:, :], 1, BLOCK), ALU.mult))
                then(dve.tensor_reduce(winner[:, t * BLOCK:(t + 1) * BLOCK], cand[:, :, :], AX.X, ALU.max))

            for t in range(NT):
                norm_rope(t)
                move_v(t)
                if t == 0:
                    dve.wait_ge(wid_psum, 1)
                    then(dve.tensor_copy(wid_all[:, :], bank[0][0:BP, 0:NW]))
                    dve.wait_ge(wr_ready, 3)
                find_winners(t)
            then(dve.tensor_scalar(won[:, :], winner[:, :], 0.0, None, ALU.is_gt))
            then(dve.scalar_tensor_tensor(winner[:, :], winner[:, :], float(OLD_ROWS - 1), c9("own"), ALU.add,
                                          ALU.subtract))
            then(dve.tensor_tensor(winner[:, :], winner[:, :], won[:, :], ALU.mult))
            dve.tensor_tensor(rows[:, :], winner[:, :], c9("own"), ALU.add).then_inc(rows_ready, 1)
            for k in range(4):
                then(dve.tensor_scalar(bits_i[:, k:k + 1], len_i[:, :], k, 1, ALU.logical_shift_right,
                                       ALU.bitwise_and))
            then(dve.tensor_copy(bits[:, :], bits_i[:, :]))
            dve.wait_ge(rows_in, 16)
            width = SLOTS * BLOCK
            for k in (3, 2, 1, 0):
                width -= 1 << k
                then(dve.tensor_tensor(row_d[:, 0:width], row_b[:, 1 << k:width + (1 << k)], row_b[:, 0:width],
                                       ALU.subtract))
                last = dve.scalar_tensor_tensor(row_b[:, 0:width], row_d[:, 0:width], bits[:, k:k + 1],
                                                row_b[:, 0:width], ALU.mult, ALU.add)
                if k:
                    then(last)
            last.then_inc(shift_ready, 1)
            dve.wait_ge(place_psum, 1)
            dve.tensor_copy(far_i[:, :], bank[0][:, 0:B]).then_inc(place_ready, 1)
            dve.tensor_copy(near_i[:, :], bank[0][:, B:B + NG]).then_inc(place_ready, 1)
            dve.tensor_copy(bias[:, :], bank[0][:, B + NG:B + 2 * NG]).then_inc(place_ready, 1)

            def row(ap, n):
                return ap[:, bass.ds(n, 1), :].rearrange("p a d -> p (a d)")

            def attention(stage, n, r, b, pair):
                if stage == "kt":
                    for s in range(GB):
                        last = dve.scalar_tensor_tensor(mask[r][:, s, :], c1("posbig"),
                                                        thresh[:, bass.ds(GB * n + s, 1)], c1("hide"),
                                                        ALU.subtract, ALU.min)
                    last.then_inc(mask_ready, 1)
                    dve.wait_ge(kt_psum, n + 1)
                    dve.tensor_copy(k_t[r][:, :, P:SPAN], b[1][:, 0:P].rearrange("p (s i) -> p s i", s=GB)
                                    ).then_inc(near_kt_ready, 1)
                elif stage == "scores":
                    dve.wait_ge(mask_ready, n + 1)
                    for half in range(2):
                        dve.wait_ge(scores_psum, 2 * n + half + 1)
                        dve.nop(nofuse=True)
                        for j in range(4 * half, 4 * half + 4):
                            s = (j // 2) % 2
                            last = dve.tensor_tensor_reduce(
                                prob[r][:, j // 2, j % 2, :], b[(2, 0)[half] + j % 2][:, s * SPAN:(s + 1) * SPAN],
                                mask[r][:, j // 2, :], 1.0, -3.0e38, ALU.add, ALU.max, top[r][:, j:j + 1])
                        last.then_inc(top_ready, 1)
                        dve.wait_ge(top_ready, 2 * n + half + 1)
                        q = slice(4 * half, 4 * half + 4)
                        dve.tensor_scalar(ntop[r][:, q], top[r][:, q], -SCALE, None, ALU.mult).then_inc(ntop_ready, 1)
                    for half in range(2):
                        dve.wait_ge(exp_ready, 2 * n + half + 1)
                        q = slice(4 * half, 4 * half + 4)
                        dve.reciprocal(rden[r][:, q], den[r][:, q]).then_inc(rden_ready, 1)
                elif stage == "pt":
                    dve.wait_ge(pfar_psum, 2 * n + 2)
                    dve.tensor_copy(p_far[r][:, 2:4, :].rearrange("p s c -> p (s c)"), b[3][:, :]
                                    ).then_inc(pfar1_ready, 1)
                    dve.wait_ge(pnear_psum, n + 1)
                    dve.tensor_tensor(p_near[r][:, :, :], over(b[0][:, 0:2 * P], 1, GB),
                                      over(c1("sample"), 2, 2 * P), ALU.mult).then_inc(pnear_ready, 1)
                elif stage == "wo":
                    dve.wait_ge(wo_psum, n + 1)
                    dve.tensor_tensor(x1[r][:, :], b[0][:, 0:D], row(xs, n), ALU.add).then_inc(x1_ready, 1)
                elif stage == "mix1":
                    dve.wait_ge(mix1_psum, n + 1)
                    dve.tensor_tensor(x2[r][:, :], b[2][:, 0:D], x1[r][:, :], ALU.add).then_inc(x2_ready, 1)
                elif stage == "mix2":
                    dve.wait_ge(mix2_psum, n + 1)
                    dve.wait_ge(x2_ready, n + 1)
                    if not isinstance(pair, int):
                        dve.wait_ge(x3_kept, n - 1)
                    dve.scalar_tensor_tensor(x3[r][:, :], b[3][:, 0:D], bias[:, bass.ds(n, 1)], x2[r][:, :],
                                             ALU.add, ALU.add).then_inc(x3_ready, 1)

            def ffn(piece, m):
                if piece == "lora":
                    dve.wait_ge(x3t_ready, 2 * m + 2)
                    dve.tensor_copy(xf[:, :, :].rearrange("p k t -> p (k t)"),
                                    x3_t[:, :, :, :].rearrange("p k r t -> p (k r t)")).then_inc(xf_ready, 1)
                    dve.wait_ge(low_psum, m + 1)
                    for a in range(2):
                        last = dve.tensor_tensor(
                            low[:, a, :].rearrange("p (s t) -> p s t", t=T),
                            FFN_BANKS[3][:, a * PAIR_TOK:(a + 1) * PAIR_TOK].rearrange("p (s t) -> p s t", t=T),
                            over(adapt[:, bass.ds(2 * GB * m, 2 * GB)], 2, T), ALU.mult)
                    last.then_inc(low_ready, 1)
                elif piece.startswith("up"):
                    f = int(piece[2:])
                    b = FFN_BANKS[f % 3]
                    at = NF * m + f + 1
                    dve.wait_ge(tanh_ready, at)
                    dve.scalar_tensor_tensor(gs[f % 2][:, :], th[f % 3][:, :], 1.0, b[:, 0:PAIR_TOK], ALU.add,
                                             ALU.mult).then_inc(gs_ready, 1)
                    dve.wait_ge(gs_ready, at)
                    dve.scalar_tensor_tensor(h_t[:, f, :], b[:, PAIR_TOK:], 0.5, gs[f % 2][:, :], ALU.mult,
                                             ALU.mult).then_inc(h_ready, 1)
                elif piece == "down_lora":
                    dve.wait_ge(lowd_psum, m + 1)
                    dve.tensor_tensor(low_d[:, :].rearrange("p (s t) -> p s t", t=T),
                                      FFN_BANKS[3][:, 0:PAIR_TOK].rearrange("p (s t) -> p s t", t=T),
                                      over(adapt[:, bass.ds(2 * GB * m, 2 * GB)], 2, T), ALU.mult
                                      ).then_inc(lowd_ready, 1)
                elif piece in ("down02", "down12"):
                    r = int(piece[4])
                    dve.wait_ge(down_psum, 2 * m + r + 1)
                    dve.wait_ge(x3_kept, 2 * m + r + 1)
                    dve.tensor_tensor(row(xs, 2 * m + r), FFN_BANKS[r][:, 0:D], row(xs, 2 * m + r), ALU.add
                                      ).then_inc(y_ready, 1)

            for stage in STAGES:
                for r in R:
                    attention(stage, r, r, (LOW_BANKS, HIGH_BANKS)[r], 0)
            with dve.Fori(0, NPAIR - 1) as m:
                for step in LOOP_ORDER:
                    if isinstance(step, str):
                        ffn(step, m)
                    else:
                        stage, r = step
                        attention(stage, 2 * m + 2 + r, r, LOW_BANKS, m + 1)
            for piece in FFN_PIECES:
                ffn(piece, NPAIR - 1)

        @block.tensor
        def _(pe):
            pe.wait_ge(sel_ready, 1)
            pe.wait_ge(ones_set, 2)
            o = NG + NT + 1
            pe.matmul(bank[0][:, 0:NG], c3("tok_b"), len_sel[:, 0:NG], start=True, stop=True)
            pe.matmul(bank[0][0:BP, NG:NG + NT], c3("blk_b"), len_sel[:, NG:NG + NT], start=True, stop=True)
            pe.matmul(bank[0][0:BP, NG + NT:o], c3("wrt_b"), len_f[:, :], start=True, stop=True)
            pe.matmul(bank[0][:, 16:16 + B], ones[0:B, :], len_sel[:, o:o + B], start=True, stop=True)
            pe.matmul(bank[0][:, 48:48 + B], ones[0:B, :], ad_sel[:, :], start=True, stop=True).then_inc(len_psum, 1)
            pe.wait_ge(k128_in, 16)
            pe.wait_ge(x_in, 16)
            for k in range(KD):
                for hf in range(2):
                    for g in range(4):
                        last = pe.transpose(bank[1 + 2 * k + hf][:, g * P:(g + 1) * P],
                                            xs[:, 4 * hf + g, k * P:(k + 1) * P], ident)
                    last.then_inc(xt_psum, 1)
            pe.wait_ge(wvkq_in, 48)
            for k in range(KD):
                c = slice(k * P, (k + 1) * P)
                for j, w in enumerate((wv_raw[:, c], wk_raw[:, c], wq_raw[:, 0, c], wq_raw[:, 1, c])):
                    last = pe.transpose(bank[5 + k][:, j * P:(j + 1) * P], w, ident)
                last.then_inc(w_psum, 1)
            pe.wait_ge(wo_in, 64)
            for h in range(GS):
                for a in range(2):
                    last = pe.transpose(bank[7][:, h * D + a * P:h * D + (a + 1) * P], wo_raw[:, a, h, :], ident)
            last.then_inc(w_psum, 1)
            pe.wait_ge(diag_ready, 1)
            pe.wait_ge(xt_ready, 4)
            for n in range(3):
                last = pe.matmul(bank[1 + n][0:BP, :], ones16[:, :],
                                 wr_diag[:, :, :].rearrange("p o w -> p (o w)")[:, 512 * n:512 * (n + 1)],
                                 start=True, stop=True)
            last.then_inc(wr_psum, 1)
            pe.wait_ge(w_ready, 3)

            def project(i):
                if i >= 2:
                    pe.wait_ge(raw_ready, i - 1)
                for t in range(2):
                    for k in range(KD):
                        last = pe.matmul(bank[4 + 2 * (i % 2) + t][:, :], x_t[:, k, 2 * i + t, :], w_vkq[:, k, :],
                                         start=(k == 0), stop=(k == KD - 1))
                last.then_inc(vkq_psum, 1)

            def turn_q(i):
                pe.wait_ge(kq_ready, 2 * i + 2)
                if i >= 2:
                    pe.wait_ge(qt_ready, i - 1)
                for t in range(2):
                    for h in range(GS):
                        last = pe.transpose(bank[2 + i % 2][:, (t * GS + h) * P:(t * GS + h + 1) * P],
                                            q_rot[:, t, h, :], ident)
                last.then_inc(qt_psum, 1)

            project(0)
            project(1)
            pe.wait_ge(widsel_ready, 1)
            pe.matmul(bank[0][0:BP, 0:NW], ones[0:BP, 0:BP], wid_sel[:, :, :].rearrange("p t w -> p (t w)"),
                      start=True, stop=True).then_inc(wid_psum, 1)
            pe.wait_ge(wr_ready, 3)
            turn_q(0)
            project(2)
            turn_q(1)
            project(3)
            turn_q(2)
            turn_q(3)
            pe.wait_ge(shift_ready, 1)
            pe.wait_ge(side_in, 16)
            pe.transpose(bank[0][:, 0:B], row_b[:, 0:P], ident[0:B, 0:B])
            for s in range(GB):
                q = slice(s * T, (s + 1) * T)
                sel = c3("group")[:, s * NG:(s + 1) * NG]
                pe.matmul(bank[0][q, B:B + NG], row_b[:, P:SPAN], sel, start=True, stop=True, tile_position=(0, s * T))
                last = pe.matmul(bank[0][q, B + NG:B + 2 * NG], side_b[:, :], sel, start=True, stop=True,
                                 tile_position=(0, s * T))
            last.then_inc(place_psum, 1)
            pe.wait_ge(place_ready, 3)

            def attention(stage, n, r, b, pair):
                first = isinstance(pair, int)
                if stage == "kt":
                    pe.wait_ge(kv_in[r], (pair + 1) * (GB + 1) * 16)
                    if first:
                        pe.wait_ge(qt_ready, NT)
                    else:
                        pe.wait_ge(x3t_ready, n)
                    for s in range(GB):
                        pe.transpose(b[0][:, s * P:(s + 1) * P], far[r][:, s, 0:G * HD], ident)
                    pe.transpose(b[1][:, 0:P], near[r][:, 0:G * HD], ident).then_inc(kt_psum, 1)
                elif stage == "scores":
                    pe.wait_ge(far_kt_ready, n + 1)
                    pe.wait_ge(near_kt_ready, n + 1)
                    pe.wait_ge(qbd_ready, 2 * n + 2)
                    for half in range(2):
                        for s in range(2):
                            for c in range(2):
                                q = slice(64 * c, 64 * c + 64)
                                last = pe.matmul(b[(2, 0)[half] + c][:, s * SPAN:(s + 1) * SPAN],
                                                 q_bd[r][q, 2 * half + s, :, :, :].rearrange("p g h t -> p (g h t)"),
                                                 k_t[r][q, 2 * half + s, :], start=True, stop=True)
                        last.then_inc(scores_psum, 1)
                elif stage == "pt":
                    for half in range(2):
                        pe.wait_ge(prob_ready, 4 * n + 2 * half + 1)
                        for j in range(4):
                            last = pe.transpose(b[2 + half][:, j * P:(j + 1) * P],
                                                prob[r][:, 2 * half + j // 2, j % 2, 0:P], ident)
                        last.then_inc(pfar_psum, 1)
                    pe.wait_ge(prob_ready, 4 * n + 4)
                    for c in range(2):
                        last = pe.transpose(b[0][:, c * P:(c + 1) * P],
                                            prob_near[r][:, c, :, :].rearrange("p s i -> p (s i)"), ident)
                    last.then_inc(pnear_psum, 1)
                elif stage == "pv":
                    pe.wait_ge(pfar0_ready, n + 1)
                    pe.wait_ge(pfar1_ready, n + 1)
                    pe.wait_ge(pnear_ready, n + 1)
                    for s in range(GB):
                        for v_rows, pr, st in ((far[r][:, s, :], p_far[r], True), (near[r][:, :], p_near[r], False)):
                            for g in range(G):
                                last = pe.matmul(b[1][g * HD:(g + 1) * HD, s * 2 * T:(s + 1) * 2 * T],
                                                 v_rows[:, G * HD + g * HD:G * HD + (g + 1) * HD],
                                                 pr[:, s, g * 2 * T:(g + 1) * 2 * T], start=st, stop=not st,
                                                 tile_position=(0, g * HD))
                    last.then_inc(o_psum, 1)
                elif stage == "wo":
                    pe.wait_ge(o_ready, n + 1)
                    for h in range(GS):
                        last = pe.matmul(b[0][:, 0:D], o_t[r][:, h, :, :].rearrange("p s t -> p (s t)"), w_o[:, h, :],
                                         start=(h == 0), stop=(h == GS - 1))
                    last.then_inc(wo_psum, 1)
                elif stage == "mix1":
                    pe.wait_ge(x1_ready, n + 1)
                    pe.wait_ge(wmix_ready, 2 * n + 2)
                    pe.matmul(b[2][:, 0:D], w_mix[r][:, 0, :, :].rearrange("p s d -> p (s d)"), x1[r][:, :],
                              start=True, stop=True).then_inc(mix1_psum, 1)
                elif stage == "mix2":
                    pe.wait_ge(x2_ready, n + 1)
                    pe.matmul(b[3][:, 0:D], w_mix[r][:, 1, :, :].rearrange("p s d -> p (s d)"), x2[r][:, :],
                              start=True, stop=True).then_inc(mix2_psum, 1)
                elif stage == "xt":
                    pe.wait_ge(x3_ready, n + 1)
                    if not first:
                        pe.wait_ge(xf_ready, pair)
                    for k in range(KD):
                        last = pe.transpose(b[0][:, k * P:(k + 1) * P], x3[r][:, k * P:(k + 1) * P], ident)
                    last.then_inc(x3t_psum, 1)

            def ffn(piece, m):
                if piece == "lora":
                    pe.wait_ge(xf_ready, m + 1)
                    for a, w in enumerate((ag, au)):
                        for k in range(KD):
                            last = pe.matmul(FFN_BANKS[3][:, a * PAIR_TOK:(a + 1) * PAIR_TOK], w[:, k, :],
                                             xf[:, k, :], start=(k == 0), stop=(k == KD - 1))
                    last.then_inc(low_psum, 1)
                elif piece.startswith("gate") or piece.startswith("up"):
                    a = int(piece.startswith("up"))
                    f = int(piece[-1])
                    fs = slice(f * P, (f + 1) * P)
                    w, lo = ((wg, bg), (wu, bu))[a]
                    if a == 0:
                        if f >= 3:
                            pe.wait_ge(h_ready, NF * m + f - 2)
                        if f == 0:
                            pe.wait_ge(low_ready, m + 1)
                    dst = FFN_BANKS[f % 3][:, a * PAIR_TOK:(a + 1) * PAIR_TOK]
                    for k in range(KD):
                        pe.matmul(dst, w[:, k, fs], xf[:, k, :], start=(k == 0), stop=False)
                    last = pe.matmul(dst, lo[:, fs], low[:, a, :], start=False, stop=True)
                    if a:
                        last.then_inc(gu_psum, 1)
                elif piece == "down_lora":
                    pe.wait_ge(h_ready, NF * m + NF)
                    for k in range(NF):
                        last = pe.matmul(FFN_BANKS[3][:, 0:PAIR_TOK], ad[:, k, :], h_t[:, k, :],
                                         start=(k == 0), stop=(k == NF - 1))
                    last.then_inc(lowd_psum, 1)
                else:
                    r, third = int(piece[4]), int(piece[5])
                    ts = slice(r * P, (r + 1) * P)
                    dst = FFN_BANKS[r][:, 0:D]
                    if third == 2:
                        pe.wait_ge(lowd_ready, m + 1)
                    for k in range(3 * third, 3 * third + 3):
                        lhs, rhs = (h_t[:, k, ts], wd[:, k, :]) if k < NF else (low_d[:, ts], bd[:, :])
                        last = pe.matmul(dst, lhs, rhs, start=(k == 0), stop=(k == NF))
                    if third == 2:
                        last.then_inc(down_psum, 1)

            for stage in STAGES:
                for r in R:
                    attention(stage, r, r, (LOW_BANKS, HIGH_BANKS)[r], 0)
            pe.wait_ge(ffn_in, 16 * FFN_LOADS)
            with pe.Fori(0, NPAIR - 1) as m:
                for step in LOOP_ORDER:
                    if isinstance(step, str):
                        ffn(step, m)
                    else:
                        stage, r = step
                        attention(stage, 2 * m + 2 + r, r, LOW_BANKS, m + 1)
            for piece in FFN_PIECES:
                ffn(piece, NPAIR - 1)


NAMES = [("x", "x"), ("itok_Bx257_0_4111", "table"), ("itok_B_37_3939", "lens"), ("itok_B_1_198", "cond"),
         ("itok_B_0_7", "subj"), ("fside_8xS_0", "side"), ("L0_cond_Wq", "Wq"), ("L0_cond_Wk", "Wk"),
         ("L0_cond_Wv", "Wv"), ("L0_cond_Wo", "Wo"), ("L0_cond_q_norm_scale", "qs"), ("L0_cond_k_norm_scale", "ks"),
         ("L0_cond_k_blocks", "kb"), ("L0_cond_v_blocks", "vb"), ("L1_cond_weights", "w1"), ("L2_cond_weights", "w2"),
         ("L3_cond_Wg", "Wg"), ("L3_cond_Wu", "Wu"), ("L3_cond_Wd", "Wd"), ("L3_cond_Ag", "Ag"),
         ("L3_cond_Bg", "Bg"), ("L3_cond_Au", "Au"), ("L3_cond_Bu", "Bu"), ("L3_cond_Ad", "Ad"), ("L3_cond_Bd", "Bd")]


def kernel(**inputs):
    import concourse.bacc as bacc
    from concourse.bass_utils import run_bass_kernel_spmd

    nc = bacc.Bacc("TRN2", target_bir_lowering=False, num_devices=1)
    arrays, args = {}, {}

    def give(name, a):
        a = np.ascontiguousarray(a)
        arrays[f"in_{name}"] = a
        args[name] = nc.dram_tensor(f"in_{name}", a.shape, mybir.dt.from_np(a.dtype), kind="ExternalInput").ap()

    for name, short in NAMES:
        give(short, inputs[name])
    for name, a in zip(("c128", "c96", "c32"), tables()):
        give(name, a)
    args["out"] = nc.dram_tensor("out", (B, T, D), F32, kind="ExternalOutput").ap()
    build(nc, **args)
    r = run_bass_kernel_spmd(nc, [arrays], core_ids=[0])
    return r.results[0]["out"]
```

```python
from contextlib import ExitStack

import concourse.bass as bass
import numpy as np
from concourse import mybir

F32 = mybir.dt.float32
F16 = mybir.dt.float16
F32R = mybir.dt.float32r
I32 = mybir.dt.int32
ALU = mybir.AluOpType
ACT = mybir.ActivationFunctionType
AX = mybir.AxisListType

P = 128
B, T, D = 32, 32, 256
H, G, HD = 8, 4, 32
GS = H // G
HALF = HD // 2
BLOCK, WINDOW = 16, 128
NBLK = 257
CACHE_BLOCKS = 16 * NBLK
GB = P // T
NG = B // GB
NPAIR = NG // 2
KD = D // P
SPAN = WINDOW + T
SLOTS = 12
BT = 8
NT = B // BT
BP = BT * SLOTS
BACK = WINDOW // BLOCK
WS = 3
NW = B * WS
KV = 2 * G * HD
BELEMS = G * BLOCK * HD
OLD_ROWS = B * SLOTS * BLOCK
NEW_ROWS = B * T
TILE_ROWS = BP * BLOCK
FF = 1024
NF = FF // P
NR = 128
RANK = 16
SCALE = 256.0 ** -0.5
EPS = 1e-6
THETA = 10000.0
BIG = 2.0 ** 100
TWO_PI = 2.0 * np.pi
PI_PARTS = (6.28125, 0.0019350051879882812, 3.019915981956753e-07)
MAGIC = 1.5 * 2.0 ** 23
PAIR_TOK = 2 * P
JOB = 4 * G * HD


def layout(fields):
    at, where = 0, {}
    for name, n in fields:
        where[name] = (at, at + n)
        at += n
    return where, at


C128, C128_N = layout([("ident", P), ("hide", SPAN), ("posbig", SPAN), ("pair", 2), ("sample", GB),
                       ("tok", 1), ("adapter", 1), ("freq", HALF)])
C96, C96_N = layout([("slot", 1), ("table", NT), ("own", NT * BLOCK), ("writer", BT * WS), ("off", BLOCK),
                     ("wslot", 1), ("wrow", 1)])
C32, C32_N = layout([("tok_b", P), ("blk_b", BP), ("wrt_b", NW), ("of_len", NG + NT + 1 + B), ("group", GB * NG)])


def tables():
    p = np.arange(P)
    a = np.zeros((P, C128_N), np.float32)

    def put(arr, where, name, v):
        lo, hi = where[name]
        arr[:, lo:hi] = v

    i = np.arange(SPAN)[None, :]
    t = (p % T)[:, None]
    put(a, C128, "ident", np.eye(P))
    put(a, C128, "hide", np.where((i > t) & (i <= WINDOW + t), 0.0, -BIG))
    put(a, C128, "posbig", i * BIG)
    put(a, C128, "pair", (p[:, None] // HD) % 2 == np.arange(2)[None, :])
    put(a, C128, "sample", p[:, None] // T == np.arange(GB)[None, :])
    put(a, C128, "tok", t)
    put(a, C128, "adapter", p[:, None] // RANK)
    half = np.arange(HALF, dtype=np.float32) / np.float32(HALF)
    put(a, C128, "freq", (np.float32(1.0) / np.power(np.float32(THETA), half))[None, :])
    q = np.arange(BP)
    b = np.zeros((BP, C96_N), np.float32)
    tile = np.arange(NT)[None, :]
    put(b, C96, "slot", (q % SLOTS - BACK)[:, None])
    put(b, C96, "table", (tile * BT + (q // SLOTS)[:, None]) * NBLK)
    own = ((tile[:, :, None] * BT + (q // SLOTS)[:, None, None]) * SLOTS + (q % SLOTS)[:, None, None]) * BLOCK
    own += np.where(tile > 0, NEW_ROWS, 0)[:, :, None]
    put(b, C96, "own", (own + np.arange(BLOCK)[None, None, :]).reshape(BP, -1))
    w = np.arange(BT * WS)[None, :]
    put(b, C96, "writer", q[:, None] == (w // WS) * SLOTS + BACK + w % WS)
    put(b, C96, "off", np.arange(BLOCK)[None, :])
    put(b, C96, "wslot", ((q % WS) * BLOCK)[:, None])
    put(b, C96, "wrow", ((q // WS) * T + 1)[:, None])
    s = np.arange(B)[:, None]
    c = np.zeros((B, C32_N), np.float32)
    put(c, C32, "tok_b", s % GB == p[None, :] // T)
    put(c, C32, "blk_b", s % BT == q[None, :] // SLOTS)
    put(c, C32, "wrt_b", s == np.arange(NW)[None, :] // WS)
    put(c, C32, "of_len", np.concatenate([s // GB == np.arange(NG)[None, :], s // BT == np.arange(NT)[None, :],
                                          np.ones((B, 1)), np.eye(B)], axis=1))
    g = np.arange(GB * NG)[None, :]
    put(c, C32, "group", s == (g % NG) * GB + g // NG)
    return a, b, c


FFN_PIECES = (["lora", "adapt"] + [f"{k}{f}" for f in range(NF) for k in ("gate", "up")]
              + ["down00", "down01", "down10", "down11", "down_lora", "tail"])
STAGES = ["kt", "scores", "pt", "pv", "wo", "mix1", "mix2", "xt", "xf"]
LOOP_ORDER = (
    ["lora", "adapt", "gate0", "up0", "gate1", "up1", ("kt", 0), "gate2", "up2", ("scores", 0), "gate3", "up3",
     "gate4", "up4", ("pt", 0), "gate5", "up5", ("pv", 0), "gate6", ("wo", 0), "up6", ("mix1", 0),
     "gate7", ("mix2", 0), "up7", ("xt", 0), ("kt", 1), ("xf", 0), "down00", ("scores", 1), "down01", "down10",
     "down11", ("pt", 1), "down_lora", ("pv", 1), ("wo", 1), ("mix1", 1), ("mix2", 1), ("xt", 1), ("xf", 1), "tail"])

START_ORDER = (
    [("kt", 0), ("kt", 1), ("move", 2), ("load", 3), ("scores", 0), ("scores", 1), ("split", "a"),
     ("pt", 0), ("pt", 1), ("move", 3), ("winner", 2), ("winner", 3), ("rows", 1), ("pv", 0), ("pv", 1), ("wo", 0),
     ("wo", 1), ("split", "gu0"), ("mix1", 0), ("mix1", 1), ("split", "gu1"), ("mix2", 0), ("mix2", 1), ("split", "b"),
     ("xt", 0), ("xt", 1), ("xf", 0), ("xf", 1)])
FIRST_ORDER = (
    [("use", "a"), "lora", ("shift", 1), "adapt", ("place", 1), ("use", "b"), ("use", "gu0"), "gate0", "up0", "gate1",
     "up1", "gate2", "up2", ("split", "ad"), "gate3", "up3", ("kt", 0), ("use", "gu1"), "gate4", ("scores", 0), "up4",
     "gate5", ("split", "d"), "up5", ("pt", 0), "gate6", "up6", ("pv", 0), ("split", "bd"), ("wo", 0),
     "gate7", ("mix1", 0), "up7", ("mix2", 0), ("use", "d"), "down00", ("xt", 0), ("kt", 1), ("xf", 0), "down01",
     ("scores", 1), "down10", "down11", ("pt", 1), ("use", "ad"), "down_lora", ("pv", 1), ("wo", 1), ("mix1", 1), ("mix2", 1),
     ("xt", 1), ("xf", 1), ("use", "bd"), "tail"])
SPLITS = {"a": "pool", "gu0": "dve", "gu1": "pool", "b": "dve", "ad": "pool", "d": "dve", "bd": "pool"}
JOBS = [("k", 0), ("k", 4), ("q", 0), ("q", 2), ("q", 4), ("q", 6)]
POOL_JOBS = 3


def build(nc, x, table, lens, cond, subj, side, Wq, Wk, Wv, Wo, qs, ks, kb, vb, w1, w2,
          Wg, Wu, Wd, Ag, Bg, Au, Bu, Ad, Bd, c128, c96, c32, out):
    ctx = ExitStack()
    with ctx:
        def sb(name, shape, dt=F32):
            return ctx.enter_context(nc.sbuf_tensor(name, shape, dt))

        def share(*layers):
            sizes, made = [], []
            for layer in layers:
                with ExitStack() as inner:
                    made.append([inner.enter_context(nc.sbuf_tensor(name, shape, dt)) for name, shape, dt in layer])
                sizes.append(sum(-(-int(np.prod(shape[1:])) * (2 if dt == F16 else 4) // 32) * 8
                                 for _, shape, dt in layer))
            sb(f"place_of_{layers[0][0][0]}", [P, max(sizes)])
            return made

        def sem(name):
            return ctx.enter_context(nc.semaphore(name))

        kv_rows = nc.dram_tensor("kv_rows", (OLD_ROWS + NEW_ROWS, KV), F32, kind="Internal").ap()
        row_table = nc.dram_tensor("row_table", (B, SLOTS * BLOCK), F32, kind="Internal").ap()
        mix_rows = nc.dram_tensor("mix_rows", (2, B, T * T), F32, kind="Internal").ap()

        k128 = sb("k128", [P, C128_N])
        k96 = sb("k96", [BP, C96_N])
        k32 = sb("k32", [B, C32_N])
        ones = sb("ones", [P, P])
        ones16 = sb("ones16", [BP, BP], F16)

        def c1(name):
            return k128[:, C128[name][0]:C128[name][1]]

        def c9(name):
            return k96[:, C96[name][0]:C96[name][1]]

        def c3(name):
            return k32[:, C32[name][0]:C32[name][1]]

        ident = c1("ident")

        ((q_in_f, k_in_f, sq, cos_x, sin_x, q_rot, wq_raw, wk_raw, wv_raw, w_vkq), (gu_raw, b_raw, ad_raw),
         (gu_low, b_low, ad_low)) = share(
            [("q_in_f", [P, NG, H * HD], F32), ("k_in_f", [P, NG, G * HD], F32),
             ("sq", [P, JOB], F32), ("cos_x", [P, JOB], F32), ("sin_x", [P, JOB], F32),
             ("q_rot", [P, 2, GS, G * HD], F32), ("wq_raw", [P, 2, D], F32), ("wk_raw", [P, D], F32),
             ("wv_raw", [P, D], F32), ("w_vkq", [P, KD, 512], F32)],
            [("gu_raw", [P, 2 * KD, FF], F32), ("b_raw", [NR, 2 * FF], F32), ("ad_raw", [P, NF * NR], F32)],
            [("gu_low", [P, 2 * KD, FF], F32R), ("b_low", [NR, 2 * FF], F32R), ("ad_low", [P, NF * NR], F32R)])
        (wo_raw,), (a_high,) = share([("wo_raw", [P, 2, GS, G * HD], F32)],
                                     [("a_high", [P, 2 * KD * NR], F32R)])
        w_o = sb("w_o", [P, GS, D])
        (early,), (gu_high,) = share([("early", [P, 2 * BELEMS], F32)],
                                     [("gu_high", [P, 2 * KD, FF], F32R)])
        (angle, turn, rest, sincos), (moved,), (d_high, b_high) = share(
            [("angle", [P, NG, HALF], F32), ("turn", [P, 2, NG, HALF], F32), ("rest", [P, 2, NG, HALF], F32),
             ("sincos", [P, 2, NG, HALF], F32)],
            [("moved", [P, BLOCK * KV], F32)],
            [("d_high", [P, NF * D], F32R), ("b_high", [NR, 2 * FF], F32R)])
        (rope_c, rope_s), (ad_high,) = share(
            [("rope_c", [P, 2, NG, HD], F32), ("rope_s", [P, 2, NG, HD], F32)],
            [("ad_high", [P, NF * NR], F32R)])
        (a_raw,), (a_low,) = share([("a_raw", [P, 2 * KD * NR], F32)], [("a_low", [P, 2 * KD * NR], F32R)])
        (d_raw,), (d_low,) = share([("d_raw", [P, NF * D], F32)], [("d_low", [P, NF * D], F32R)])
        (bd_raw,), (bd_low,) = share([("bd_raw", [NR, D], F32)], [("bd_low", [NR, D], F32R)])
        bd_high = sb("bd_high", [NR, D], F32R)
        lower, upper = slice(0, FF // 2), slice(FF // 2, FF)
        WEIGHTS = {"a": (a_raw[:, :], a_high[:, :], a_low[:, :]), "b": (b_raw[:, :], b_high[:, :], b_low[:, :]),
                   "gu0": (gu_raw[:, :, lower], gu_high[:, :, lower], gu_low[:, :, lower]),
                   "gu1": (gu_raw[:, :, upper], gu_high[:, :, upper], gu_low[:, :, upper]),
                   "ad": (ad_raw[:, :], ad_high[:, :], ad_low[:, :]), "d": (d_raw[:, :], d_high[:, :], d_low[:, :]),
                   "bd": (bd_raw[:, :], bd_high[:, :], bd_low[:, :])}
        w_gu = [t[:, :, :].rearrange("p (g k) f -> p g k f", g=2) for t in (gu_high, gu_low)]
        w_b = [t[:, :].rearrange("p (g f) -> p g f", g=2) for t in (b_high, b_low)]
        w_ad = [t[:, :].rearrange("p (k n) -> p k n", k=NF) for t in (ad_high, ad_low)]
        w_a = [t[:, :].rearrange("p (g k n) -> p g k n", g=2, k=KD) for t in (a_high, a_low)]
        w_d = [t[:, :].rearrange("p (k d) -> p k d", k=NF) for t in (d_high, d_low)]
        w_bd = [t[:, :] for t in (bd_high, bd_low)]
        len_i = sb("len_i", [B, 1], I32)
        cond_i = sb("cond_i", [B, 1], I32)
        subj_i = sb("subj_i", [B, 1], I32)
        len_f = sb("len_f", [B, 1])
        subj_f = sb("subj_f", [B, 1])
        scale_qk = sb("scale_qk", [P, 2, HD])
        scale_sw = sb("scale_sw", [P, 2, HD])
        len_sel = sb("len_sel", [B, NG + NT + 1 + B])
        ad_sel = sb("ad_sel", [B, B])
        len_all = sb("len_all", [P, 80])
        adapt = sb("adapt", [NR, B])
        thresh = sb("thresh", [P, B])
        xs = sb("xs", [P, NG, D])
        (x_t,), (h_high,) = share([("x_t", [P, KD, NG, P], F32)], [("h_high", [P, NF, PAIR_TOK], F32R)])
        pos = sb("pos", [P, NG])
        ssum = sb("ssum", [P, JOB // HD])
        meansq = sb("meansq", [P, JOB // HD])
        rms = sb("rms", [P, JOB // HD])
        rstd = sb("rstd", [P, JOB // HD])
        far_probs = sb("far_probs", [P, 2 * GB, 2 * P])
        new_kv = far_probs[:, :, :]
        q_t = sb("q_t", [P, NG, GS, P])
        slot_i = sb("slot_i", [BP, NT], I32)
        slot_f = sb("slot_f", [BP, NT])
        tidx = sb("tidx", [BP, NT], I32)
        blk_i = sb("blk_i", [BP, NT], I32)
        blk_f = sb("blk_f", [BP, NT])
        k_raw = early[0:BP, 0:BELEMS]
        v_raw = early[0:BP, BELEMS:2 * BELEMS]
        kv_blk = moved[0:BP, :].rearrange("p (o c) -> p o c", c=KV)
        wr_i = sb("wr_i", [BP, 1], I32)
        wr_off = sb("wr_off", [BP, 1])
        wr_d = sb("wr_d", [BP, BLOCK])
        wr_e = sb("wr_e", [BP, BLOCK])
        wr_f = sb("wr_f", [BP, BLOCK])
        (wr_diag, wr_all), (th0, th1, th2, gs0, gs1, lowd_high) = share(
            [("wr_diag", [BP, BLOCK, NW], F16), ("wr_all", [BP, BLOCK, NW], F16)],
            [(f"th{n}", [P, PAIR_TOK], F32) for n in range(3)]
            + [(f"gs{n}", [P, PAIR_TOK], F32) for n in range(2)] + [("lowd_high", [NR, PAIR_TOK], F32R)])
        wid_sel = sb("wid_sel", [BP, NT, BT * WS])
        wid_all = sb("wid_all", [BP, NW])
        same = sb("same", [BP, NW], F16)
        cand = wr_diag
        winner = sb("winner", [BP, NT * BLOCK])
        won = sb("won", [BP, NT * BLOCK])
        rows = sb("rows", [BP, NT * BLOCK])
        bits_i = sb("bits_i", [B, 4], I32)
        bits = sb("bits", [B, 4])
        row_b = sb("row_b", [B, SLOTS * BLOCK])
        row_d = sb("row_d", [B, SLOTS * BLOCK])
        far_i = sb("far_i", [P, B], I32)
        near_i = sb("near_i", [P, NG], I32)
        (mix_raw,), (h_low,) = share([("mix_raw", [B, 2, T * T], F32)], [("h_low", [P, NF, PAIR_TOK], F32R)])
        mix_w = sb("mix_w", [P, 2, NG, T])
        side_b = sb("side_b", [B, T])
        bias = sb("bias", [P, NG])
        R = range(2)
        idx = [sb(f"idx{r}", [P, GB + 1], I32) for r in R]
        far = [sb(f"far{r}", [P, GB, KV]) for r in R]
        near = [sb(f"near{r}", [P, KV]) for r in R]
        k_t = [sb(f"k_t{r}", [P, GB, SPAN]) for r in R]
        q_bd = [sb(f"q_bd{r}", [P, GB, 2, GS, T]) for r in R]
        mask = [sb(f"mask{r}", [P, GB, SPAN]) for r in R]
        prob = [sb(f"prob{r}", [P, GB, 2, SPAN]) for r in R]
        prob_near = [sb(f"prob_near{r}", [P, 2, GB, T]) for r in R]
        top = [sb(f"top{r}", [P, GB * 2]) for r in R]
        ntop = [sb(f"ntop{r}", [P, GB * 2]) for r in R]
        den = [sb(f"den{r}", [P, GB * 2]) for r in R]
        rden = [sb(f"rden{r}", [P, GB * 2]) for r in R]
        p_far = [far_probs[:, GB * r:GB * (r + 1), :] for r in R]
        p_near = [sb(f"p_near{r}", [P, GB, 2 * P]) for r in R]
        o_t = [sb(f"o_t{r}", [P, GS, GB, T]) for r in R]
        w_mix = [sb(f"w_mix{r}", [P, 2, GB, T]) for r in R]
        x1 = [sb(f"x1_{r}", [P, D]) for r in R]
        x2 = [sb(f"x2_{r}", [P, D]) for r in R]
        x3 = [sb(f"x3_{r}", [P, D]) for r in R]
        x3_t = sb("x3_t", [P, KD, 2, P])
        xf_high = sb("xf_high", [P, KD * PAIR_TOK], F32R)
        xf_low = sb("xf_low", [P, KD * PAIR_TOK], F32R)
        (low_raw,), (low_low,) = share([("low_raw", [NR, 2 * PAIR_TOK], F32)],
                                       [("low_low", [NR, 2 * PAIR_TOK], F32R)])
        low_high = sb("low_high", [NR, 2 * PAIR_TOK], F32R)
        (lowd_raw,), (lowd_low,) = share([("lowd_raw", [NR, PAIR_TOK], F32)], [("lowd_low", [NR, PAIR_TOK], F32R)])
        th, gs = (th0, th1, th2), (gs0, gs1)
        hf = [sb(f"hf{r}", [P, PAIR_TOK]) for r in R]
        m_xf = [t[:, :].rearrange("p (k t) -> p k t", k=KD) for t in (xf_high, xf_low)]
        m_low = [t[:, :].rearrange("p (g t) -> p g t", g=2) for t in (low_high, low_low)]
        m_h = [t[:, :, :] for t in (h_high, h_low)]
        m_lowd = [t[:, :] for t in (lowd_high, lowd_low)]
        bank = [ctx.enter_context(nc.psum_tensor(f"bank{n}", [P, 512], F32)) for n in range(8)]

        small_in = sem("small_in")
        k128_in = sem("k128_in")
        scale_in = sem("scale_in")
        x_in = sem("x_in")
        wvkq_in = sem("wvkq_in")
        wo_in = sem("wo_in")
        w_in = {name: sem(f"w_in_{name}") for name in ("a", "b", "gu", "d", "ad", "bd")}
        high_ready = sem("high_ready")
        split_ready = {name: sem(f"split_{name}") for name in SPLITS}
        mix_idx_in = sem("mix_idx_in")
        ones_set = sem("ones_set")
        sel_ready = sem("sel_ready")
        len_psum = sem("len_psum")
        len_ready = sem("len_ready")
        tidx_ready = sem("tidx_ready")
        blk_in = sem("blk_in")
        blk_ready = sem("blk_ready")
        k_in = sem("k_in")
        v_in = sem("v_in")
        k_moved = sem("k_moved")
        v_moved = sem("v_moved")
        blk_out = sem("blk_out")
        new_out = sem("new_out")
        xt_psum = sem("xt_psum")
        xt_ready = sem("xt_ready")
        w_psum = sem("w_psum")
        w_ready = sem("w_ready")
        arg_ready = sem("arg_ready")
        sin_ready = sem("sin_ready")
        rope_ready = sem("rope_ready")
        vk_psum = sem("vk_psum")
        vk_ready = sem("vk_ready")
        q_psum = sem("q_psum")
        q_ready = sem("q_ready")
        sq_ready = sem("sq_ready")
        ssum_ready = sem("ssum_ready")
        meansq_ready = sem("meansq_ready")
        rms_ready = sem("rms_ready")
        cos_ready = sem("cos_ready")
        job_done = sem("job_done")
        qt_psum = sem("qt_psum")
        qt_ready = sem("qt_ready")
        diag_ready = sem("diag_ready")
        wr_psum = sem("wr_psum")
        wr_ready = sem("wr_ready")
        widsel_ready = sem("widsel_ready")
        wid_psum = sem("wid_psum")
        rows_ready = sem("rows_ready")
        rows_out = sem("rows_out")
        rows_in = sem("rows_in")
        shift_ready = sem("shift_ready")
        place_psum = sem("place_psum")
        place_ready = sem("place_ready")
        mix_in = sem("mix_in")
        side_in = sem("side_in")
        mix_out = sem("mix_out")
        mix_back = sem("mix_back")
        vector_order = sem("vector_order")
        idx_ready = sem("idx_ready")
        kv_in = [sem(f"kv_in{r}") for r in R]
        qbd_ready = sem("qbd_ready")
        mask_ready = sem("mask_ready")
        wmix_ready = sem("wmix_ready")
        kt_psum = sem("kt_psum")
        far_kt_ready = sem("far_kt_ready")
        near_kt_ready = sem("near_kt_ready")
        scores_psum = sem("scores_psum")
        top_ready = sem("top_ready")
        ntop_ready = sem("ntop_ready")
        exp_ready = sem("exp_ready")
        rden_ready = sem("rden_ready")
        prob_ready = sem("prob_ready")
        pfar_psum = sem("pfar_psum")
        pnear_psum = sem("pnear_psum")
        pfar0_ready = sem("pfar0_ready")
        pfar1_ready = sem("pfar1_ready")
        pnear_ready = sem("pnear_ready")
        o_psum = sem("o_psum")
        o_ready = sem("o_ready")
        wo_psum = sem("wo_psum")
        x1_ready = sem("x1_ready")
        mix1_psum = sem("mix1_psum")
        x2_ready = sem("x2_ready")
        mix2_psum = sem("mix2_psum")
        x3_ready = sem("x3_ready")
        x3_kept = sem("x3_kept")
        x3t_psum = sem("x3t_psum")
        x3t_ready = sem("x3t_ready")
        xfhigh_ready = sem("xfhigh_ready")
        xf_ready = sem("xf_ready")
        lowraw_ready = sem("lowraw_ready")
        lowhigh_ready = sem("lowhigh_ready")
        low_psum = sem("low_psum")
        low_ready = sem("low_ready")
        gu_psum = sem("gu_psum")
        tanh_ready = sem("tanh_ready")
        gs_ready = sem("gs_ready")
        hf_ready = sem("hf_ready")
        hhigh_ready = sem("hhigh_ready")
        h_ready = sem("h_ready")
        lowd_psum = sem("lowd_psum")
        lowdraw_ready = sem("lowdraw_ready")
        lowdhigh_ready = sem("lowdhigh_ready")
        lowd_ready = sem("lowd_ready")
        down_psum = sem("down_psum")
        y_ready = sem("y_ready")
        y_out = sem("y_out")

        def xf_half(t, r):
            return t[:, :].rearrange("p (k t) -> p k t", k=KD)[:, :, r * P:(r + 1) * P]

        def over(ap, axis, n):
            ap = ap.unsqueeze(axis)
            shape = list(ap.shape)
            shape[axis] = n
            return ap.broadcast_to(shape)

        LOW_BANKS, HIGH_BANKS = bank[0:4], bank[4:8]
        FFN_BANKS = bank[4:8]
        SCORE = slice(0, 2 * SPAN)

        block = ctx.enter_context(nc.Block())

        def blocks_of(table, t0, t1):
            v = table.rearrange("(t b) (j o) -> (b j) t o", t=NT, o=BLOCK)[:, t0:t1, :]
            return v.rearrange("p t o -> p (t o)") if t1 - t0 == 1 else v

        def blocks_of_rows(t0, t1):
            v = rows[:, t0 * BLOCK:t1 * BLOCK]
            return v if t1 - t0 == 1 else v.rearrange("p (t o) -> p t o", o=BLOCK)

        @block.sync
        def _(sp):
            sp.dma_start(len_i[:, :], lens.rearrange("(b o) -> b o", o=1)).then_inc(small_in, 16)
            sp.dma_start(k32[:, :], c32).then_inc(small_in, 16)
            sp.dma_start(k96[:, :], c96).then_inc(small_in, 16)
            sp.dma_start(k128[:, :], c128).then_inc(k128_in, 16)
            sp.dma_start(xs[:, :, :], x.rearrange("(g s) t d -> (s t) g d", s=GB)).then_inc(x_in, 16)
            sp.dma_start(wv_raw[:, :], Wv).then_inc(wvkq_in, 16)
            sp.dma_start(wk_raw[:, :], Wk).then_inc(wvkq_in, 16)
            sp.dma_start(wq_raw[:, :, :], Wq.rearrange("(a p) d -> p a d", p=P)).then_inc(wvkq_in, 16)
            for a in range(2):
                for h in range(GS):
                    sp.dma_start(wo_raw[:, a, h, :].rearrange("p (g d) -> p g d", g=G),
                                 Wo[a * P:(a + 1) * P, :].rearrange("p (g h d) -> p g h d", g=G, h=GS)[:, :, h, :]
                                 ).then_inc(wo_in, 16)
            def new_rows(i):
                sp.wait_ge(vk_ready, 2 * i + 2)
                sp.wait_ge(job_done, i + 1)
                lo = TILE_ROWS + 4 * i * P
                sp.dma_start(kv_rows[lo:lo + 4 * P, :].rearrange("(g p) c -> p g c", p=P),
                             new_kv[:, 4 * i:4 * i + 4, :]).then_inc(new_out, 16)

            def block_rows(t):
                sp.wait_ge(k_moved, t + 1)
                sp.wait_ge(v_moved, t + 1)
                lo = t * TILE_ROWS + (NEW_ROWS if t else 0)
                sp.dma_start(kv_rows[lo:lo + TILE_ROWS, :].rearrange("(p o) c -> p (o c)", o=BLOCK),
                             kv_blk[:, :, :].rearrange("p o c -> p (o c)")).then_inc(blk_out, 16)

            def rows_out_to_table(t0, t1):
                sp.wait_ge(rows_ready, 1 if t0 == 0 else 2)
                sp.dma_start(blocks_of(row_table, t0, t1), blocks_of_rows(t0, t1)).then_inc(rows_out, 16)

            def rows_back(t1):
                sp.wait_ge(rows_out, 16 if t1 == 1 else 32)
                sp.dma_start(row_b[0:t1 * BT, :], row_table[0:t1 * BT, :]).then_inc(rows_in, 16)

            block_rows(0)
            new_rows(0)
            rows_out_to_table(0, 1)
            rows_back(1)
            new_rows(1)
            block_rows(1)
            sp.wait_ge(kv_in[1], 16 * (GB + 1))
            for a, src in enumerate((Ag, Au)):
                for k in range(KD):
                    at = (a * KD + k) * NR
                    sp.dma_start(a_raw[:, at:at + NR].rearrange("p (n r) -> p n r", r=RANK),
                                 src[:, k * P:(k + 1) * P, :].rearrange("n p r -> p n r")).then_inc(w_in["a"], 16)
            block_rows(2)
            sp.wait_ge(job_done, len(JOBS))
            sp.wait_ge(q_ready, NT)
            sp.wait_ge(qt_psum, NT)
            for a, src in enumerate((Bg, Bu)):
                sp.dma_start(b_raw[:, a * FF:(a + 1) * FF], src.rearrange("n r f -> (n r) f")).then_inc(w_in["b"], 16)
            for a, src in enumerate((Wg, Wu)):
                sp.dma_start(gu_raw[:, a * KD:(a + 1) * KD, :], src.rearrange("(k p) f -> p k f", p=P)
                             ).then_inc(w_in["gu"], 16)
            block_rows(3)
            rows_out_to_table(1, NT)
            sp.dma_start(d_raw[:, :].rearrange("p (k d) -> p k d", k=NF), Wd.rearrange("(k p) f -> p k f", p=P)
                         ).then_inc(w_in["d"], 16)
            rows_back(NT)
            for k in range(NF):
                sp.dma_start(ad_raw[:, k * NR:(k + 1) * NR].rearrange("p (n r) -> p n r", r=RANK),
                             Ad[:, k * P:(k + 1) * P, :].rearrange("n p r -> p n r")).then_inc(w_in["ad"], 16)
            sp.dma_start(bd_raw[:, :], Bd.rearrange("n r f -> (n r) f")).then_inc(w_in["bd"], 16)

            def store(m):
                for r in R:
                    sp.wait_ge(y_ready, 2 * m + r + 1)
                    sp.dma_start(out[bass.ds(m * 2 * GB + GB * r, GB), :, :].rearrange("s t d -> (s t) d"),
                                 xs[:, bass.ds(2 * m + r, 1), :].rearrange("p a d -> p (a d)")).then_inc(y_out, 16)

            with sp.Fori(0, NPAIR) as m:
                store(m)
            sp.wait_ge(y_out, 16 * NG)

        SPLIT_AT = {name: n + 1 for n, name in enumerate(SPLITS)}
        LOADS = {"a": 2 * KD, "b": 2, "gu0": 2, "gu1": 2, "ad": NF, "d": 1, "bd": 1}

        def take_low(eng, name):
            eng.wait_ge(high_ready, SPLIT_AT[name])
            raw, high, low = WEIGHTS[name]
            eng.tensor_tensor(low, raw, high.bitcast(F32), ALU.subtract).then_inc(split_ready[name], 1)

        @block.gpsimd
        def _(pool):
            pool.memset(ones[:, :], 1.0).then_inc(ones_set, 1)
            pool.memset(ones16[:, :], 1.0).then_inc(ones_set, 1)
            pool.wait_ge(tidx_ready, 1)
            for t in range(NT):
                pool.indirect_dma_start(
                    blk_i[:, t:t + 1], None, table.rearrange("b (n o) -> (b n) o", o=1),
                    bass.IndirectOffsetOnAxis(ap=tidx[:, t:t + 1], axis=0)).then_inc(blk_in, 16)
            pool.wait_ge(blk_in, 16 * NT)

            def load_blocks(t):
                for dst, src, seen, done in ((k_raw, kb, k_moved, k_in), (v_raw, vb, v_moved, v_in)):
                    if t:
                        pool.wait_ge(seen, t)
                    pool.indirect_dma_start(dst[:, :], None, src.rearrange("n g o d -> n (g o d)"),
                                            bass.IndirectOffsetOnAxis(ap=blk_i[:, t:t + 1], axis=0)).then_inc(done, 16)

            def cos_part(j):
                kind, g = JOBS[j]
                n, nh, ng, src = (0, G, 4, k_in_f) if kind == "k" else (1, H, 2, q_in_f)
                if j == 0:
                    pool.wait_ge(rope_ready, 1)
                else:
                    pool.wait_ge(job_done, j)
                if kind == "k":
                    pool.wait_ge(vk_ready, g // 2 + 2)
                else:
                    pool.wait_ge(q_ready, g // 2 + 1)
                pool.tensor_tensor(cos_x[:, :].rearrange("p (t h d) -> p t h d", t=ng, d=HD),
                                   src[:, g:g + ng, :].rearrange("p t (h d) -> p t h d", d=HD),
                                   over(rope_c[:, n, g:g + ng, :], 2, nh), ALU.mult).then_inc(cos_ready, 1)

            load_blocks(0)
            pool.wait_ge(mix_idx_in, 32)
            for n, (w, i) in enumerate(((w1, cond_i), (w2, subj_i))):
                pool.indirect_dma_start(mix_raw[:, n, :], None, w.rearrange("n c d -> n (c d)"),
                                        bass.IndirectOffsetOnAxis(ap=i[:, :], axis=0)).then_inc(mix_in, 16)
            pool.indirect_dma_start(side_b[:, :], None, side,
                                    bass.IndirectOffsetOnAxis(ap=subj_i[:, :], axis=0)).then_inc(side_in, 16)
            for j in range(POOL_JOBS):
                cos_part(j)
            pool.wait_ge(rows_in, 16)
            load_blocks(1)

            def prepare(n, r, pair):
                table_rows = kv_rows if pair is not None else kv_rows[0:TILE_ROWS + NEW_ROWS, :]
                if pair is not None:
                    pool.wait_ge(kv_in[r], pair * (GB + 1) * 16)
                pool.tensor_copy(idx[r][:, 0:GB], far_i[:, bass.ds(GB * n, GB)]).then_inc(idx_ready, 1)
                pool.tensor_copy(idx[r][:, GB:GB + 1], near_i[:, bass.ds(n, 1)]).then_inc(idx_ready, 1)
                pool.wait_ge(idx_ready, 2 * n + 2)
                if pair is not None:
                    pool.wait_ge(o_psum, n - 1)
                pool.nop(nofuse=True)
                for s in range(GB):
                    pool.indirect_dma_start(far[r][:, s, :], None, table_rows,
                                            bass.IndirectOffsetOnAxis(ap=idx[r][:, s:s + 1], axis=0)
                                            ).then_inc(kv_in[r], 16)
                pool.indirect_dma_start(near[r][:, :], None, table_rows,
                                        bass.IndirectOffsetOnAxis(ap=idx[r][:, GB:GB + 1], axis=0)
                                        ).then_inc(kv_in[r], 16)

            def spread_q(n, r):
                for h in range(GS):
                    src = q_t[:, bass.ds(n, 1), h, :].rearrange("p a (s t) -> p (a s) t", s=GB)
                    pool.tensor_tensor(q_bd[r][:, :, :, h, :], over(src, 2, 2),
                                       over(over(c1("pair"), 1, GB), 3, T), ALU.mult).then_inc(qbd_ready, 1)

            def spread_w(n, r):
                for w in range(2):
                    src = mix_w[:, w, bass.ds(n, 1), :].rearrange("p a d -> p (a d)")
                    pool.tensor_tensor(w_mix[r][:, w, :, :], over(src, 1, GB), over(c1("sample"), 2, T),
                                       ALU.mult).then_inc(wmix_ready, 1)

            def normalise(n, r):
                for half in range(2):
                    pool.wait_ge(rden_ready, 2 * n + half + 1)
                    s = slice(2 * half, 2 * half + 2)
                    v = prob[r][:, s, :, 0:P].rearrange("p s c i -> p (s c) i")
                    scale = rden[r][:, 4 * half:4 * half + 4]
                    pool.tensor_tensor(v, v, over(scale, 2, P), ALU.mult).then_inc(prob_ready, 1)
                    pool.tensor_tensor(prob_near[r][:, :, s, :].rearrange("p c s i -> p s c i"),
                                       prob[r][:, s, :, P:SPAN],
                                       over(scale.rearrange("p (s c) -> p s c", c=2), 3, T),
                                       ALU.mult).then_inc(prob_ready, 1)

            def keep(n, r):
                pool.wait_ge(x3_ready, n + 1)
                pool.tensor_copy(xs[:, bass.ds(n, 1), :].rearrange("p a d -> p (a d)"), x3[r][:, :]).then_inc(x3_kept, 1)

            pool.wait_ge(qt_ready, 1)
            for r in R:
                spread_q(r, r)
            pool.wait_ge(place_ready, 3)
            pool.wait_ge(blk_out, 16)
            pool.wait_ge(new_out, 32)
            for r in R:
                prepare(r, r, None)
            load_blocks(2)

            def pair_steps(order, m):
                for step in order:
                    if step[0] == "load":
                        load_blocks(step[1])
                    elif step[0] == "split" and SPLITS[step[1]] == "pool":
                        take_low(pool, step[1])
                    elif step[0] == "place":
                        pool.wait_ge(place_ready, 5)
                        pool.wait_ge(blk_out, 16 * NT)
                        pool.wait_ge(qt_ready, NT)
                        for r in R:
                            prepare(2 * m + 2 + r, r, m + 1)
                            spread_q(2 * m + 2 + r, r)
                            spread_w(2 * m + 2 + r, r)
                    elif step[0] == "scores":
                        normalise(2 * m + 2 + step[1], step[1])
                    elif step[0] == "mix2":
                        keep(2 * m + 2 + step[1], step[1])

            pool.wait_ge(mix_back, 32)
            for r in R:
                spread_w(r, r)
            pair_steps(START_ORDER, -1)
            pair_steps(FIRST_ORDER, 0)
            with pool.Fori(1, NPAIR - 1) as m:
                for r in R:
                    prepare(2 * m + 2 + r, r, m + 1)
                    spread_q(2 * m + 2 + r, r)
                    spread_w(2 * m + 2 + r, r)
                pair_steps(LOOP_ORDER, m)

        @block.scalar
        def _(act):
            act.dma_start(cond_i[:, :], cond.rearrange("(b o) -> b o", o=1)).then_inc(mix_idx_in, 16)
            act.dma_start(subj_i[:, :], subj.rearrange("(b o) -> b o", o=1)).then_inc(mix_idx_in, 16)
            for n, s in enumerate((ks, qs)):
                act.dma_start(scale_qk[:, n, :], s.partition_broadcast(P)).then_inc(scale_in, 16)
            for n in range(2):
                act.wait_ge(xt_psum, 2 * n + 1)
                act.copy(x_t[:, n, 0:4, :].rearrange("p g t -> p (g t)"), bank[1 + 2 * n][:, :]).then_inc(xt_ready, 1)
            act.wait_ge(w_psum, 1)
            act.copy(w_vkq[:, :, 0:KV], bank[5][:, :].rearrange("p (k c) -> p k c", k=KD)).then_inc(w_ready, 1)
            act.wait_ge(arg_ready, 1)
            act.activation(sincos[:, :, :, :].rearrange("p a g f -> p (a g f)"),
                           rest[:, :, :, :].rearrange("p a g f -> p (a g f)"), ACT.Sin).then_inc(sin_ready, 1)

            def square(j):
                kind, g = JOBS[j]
                ng, src = (4, k_in_f) if kind == "k" else (2, q_in_f)
                if j:
                    act.wait_ge(ssum_ready, j)
                if kind == "q":
                    act.wait_ge(q_ready, g // 2 + 1)
                act.activation(sq[:, :], src[:, g:g + ng, :].rearrange("p t c -> p (t c)"), ACT.Square
                               ).then_inc(sq_ready, 1)

            def root(j):
                act.wait_ge(meansq_ready, j + 1)
                act.activation(rms[:, :], meansq[:, :], ACT.Sqrt).then_inc(rms_ready, 1)

            def take_q(i):
                act.wait_ge(q_psum, i + 1)
                act.copy(q_in_f[:, 2 * i:2 * i + 2, :].rearrange("p t c -> p (t c)"), bank[(5, 6, 1, 2)[i]][:, :]
                         ).then_inc(q_ready, 1)

            def move_k(t):
                act.wait_ge(k_in, 16 * (t + 1))
                if t:
                    act.wait_ge(blk_out, 16 * t)
                act.copy(kv_blk[:, :, 0:G * HD].rearrange("p o (g d) -> p o g d", d=HD),
                         k_raw[:, :].rearrange("p (g o d) -> p o g d", g=G, d=HD)).then_inc(k_moved, 1)

            def take_qt(i):
                act.wait_ge(qt_psum, i + 1)
                act.copy(q_t[:, 2 * i:2 * i + 2, :, :].rearrange("p g h t -> p (g h t)"), bank[3 + i % 2][:, :]
                         ).then_inc(qt_ready, 1)

            def take_vk(i):
                act.wait_ge(vk_psum, i + 1)
                src = bank[1 + i][:, :].rearrange("p (t c) -> p t c", t=2)
                act.copy(new_kv[:, 2 * i:2 * i + 2, G * HD:KV], src[:, :, 0:G * HD])
                act.copy(k_in_f[:, 2 * i:2 * i + 2, :], src[:, :, G * HD:KV]).then_inc(vk_ready, 1)

            take_vk(0)
            take_vk(1)
            act.wait_ge(vk_ready, 2)
            square(0)
            act.wait_ge(wr_psum, 1)
            for n in range(3):
                act.copy(wr_all[:, :, :].rearrange("p o w -> p (o w)")[:, 512 * n:512 * (n + 1)],
                         bank[5 + n][0:BP, :]).then_inc(wr_ready, 1)
            root(0)
            move_k(0)
            take_vk(2)
            take_vk(3)
            act.wait_ge(vk_ready, 4)
            square(1)
            take_q(0)
            root(1)
            square(2)
            act.wait_ge(mix_in, 32)
            for n in range(2):
                act.dma_start(mix_rows[n, :, :], mix_raw[:, n, :]).then_inc(mix_out, 16)
            root(2)
            for i in range(1, 4):
                take_q(i)
            take_qt(0)
            square(3)
            root(3)
            act.wait_ge(mix_out, 32)
            for n in range(2):
                act.dma_start(mix_w[:, n, :, :],
                              mix_rows[n, :, :].rearrange("(g s) (c d) -> (s c) g d", s=GB, d=T)).then_inc(mix_back, 16)
            square(4)
            move_k(1)
            take_qt(1)
            root(4)
            square(5)
            take_qt(2)
            root(5)
            take_qt(3)

            def attention(stage, n, r, b, pair):
                first = isinstance(pair, int) and pair == 0
                if stage == "kt":
                    act.wait_ge(kt_psum, n + 1)
                    act.copy(k_t[r][:, :, 0:P], b[0][:, :].rearrange("p (s i) -> p s i", s=GB)).then_inc(far_kt_ready, 1)
                elif stage == "scores":
                    for half in range(2):
                        act.wait_ge(ntop_ready, 2 * n + half + 1)
                        for j in range(4 * half, 4 * half + 4):
                            v = prob[r][:, j // 2, j % 2, :]
                            last = act.activation(v, v, ACT.Exp, bias=ntop[r][:, j:j + 1], scale=SCALE,
                                                  accum_out=den[r][:, j:j + 1])
                        last.then_inc(exp_ready, 1)
                elif stage == "pt":
                    act.wait_ge(pfar_psum, 2 * n + 1)
                    act.copy(p_far[r][:, 0:2, :].rearrange("p s c -> p (s c)"), b[2][:, :]).then_inc(pfar0_ready, 1)
                elif stage == "pv":
                    act.wait_ge(o_psum, n + 1)
                    act.copy(o_t[r][:, :, :, :].rearrange("p h s t -> p s h t"),
                             b[1][:, 0:2 * P].rearrange("p (s h t) -> p s h t", s=GB, h=GS)).then_inc(o_ready, 1)
                elif stage == "xt":
                    act.wait_ge(x3t_psum, n + 1)
                    if not first:
                        act.wait_ge(xf_ready, n - 1)
                    act.copy(x3_t[:, :, r, :], b[0][:, 0:2 * P].rearrange("p (k t) -> p k t", k=KD)
                             ).then_inc(x3t_ready, 1)
                elif stage == "xf":
                    act.wait_ge(x3t_ready, n + 1)
                    act.copy(xf_half(xf_high, r), x3_t[:, :, r, :]).then_inc(xfhigh_ready, 1)

            def take_high(name):
                act.wait_ge(w_in[name[0:2] if name in ("gu0", "gu1") else name], 16 * LOADS[name])
                if name in ("gu0", "gu1"):
                    act.wait_ge(v_moved, NT)
                    act.wait_ge(k_moved, NT)
                if name in ("b", "d"):
                    act.wait_ge(blk_out, 16 * NT)
                act.copy(WEIGHTS[name][1], WEIGHTS[name][0]).then_inc(high_ready, 1)

            def h_high_part(m, f):
                act.wait_ge(hf_ready, NF * m + f + 1)
                act.copy(h_high[:, f, :], hf[f % 2][:, :]).then_inc(hhigh_ready, 1)

            def ffn(piece, m):
                if piece == "up0":
                    act.wait_ge(lowraw_ready, m + 1)
                    act.copy(low_high[:, :], low_raw[:, :]).then_inc(lowhigh_ready, 1)
                if piece.startswith("up"):
                    f = int(piece[2:])
                    act.wait_ge(gu_psum, NF * m + f + 1)
                    act.activation(th[f % 3][:, :], FFN_BANKS[f % 3][:, 0:PAIR_TOK], ACT.Tanh,
                                   scale=0.5).then_inc(tanh_ready, 1)
                    if f:
                        h_high_part(m, f - 1)
                elif piece == "down00":
                    h_high_part(m, NF - 1)
                elif piece == "down_lora":
                    act.wait_ge(lowdraw_ready, m + 1)
                    act.copy(lowd_high[:, :], lowd_raw[:, :]).then_inc(lowdhigh_ready, 1)

            def steps(order, m, pair):
                first_pair = order is START_ORDER
                for step in order:
                    if isinstance(step, str):
                        ffn(step, m)
                    elif step[0] == "split":
                        take_high(step[1])
                    elif step[0] == "move":
                        move_k(step[1])
                    elif step[0] in STAGES:
                        stage, r = step
                        attention(stage, 2 * m + 2 + r, r, HIGH_BANKS if first_pair and r else LOW_BANKS, pair)

            steps(START_ORDER, -1, 0)
            steps(FIRST_ORDER, 0, 1)
            with act.Fori(1, NPAIR - 1) as m:
                steps(LOOP_ORDER, m, m + 1)
            for piece in FFN_PIECES:
                ffn(piece, NPAIR - 1)

        @block.vector
        def _(dve):
            count = [0]

            def then(ins):
                count[0] += 1
                ins.then_inc(vector_order, 1)
                dve.wait_ge(vector_order, count[0])

            dve.wait_ge(small_in, 48)
            then(dve.tensor_copy(len_f[:, :], len_i[:, :]))
            then(dve.tensor_scalar(len_sel[:, :], c3("of_len"), len_f[:, 0:1], None, ALU.mult))
            dve.wait_ge(mix_idx_in, 32)
            then(dve.tensor_copy(subj_f[:, :], subj_i[:, :]))
            dve.tensor_scalar(ad_sel[:, :], c3("of_len")[:, NG + NT + 1:], subj_f[:, 0:1], None,
                              ALU.mult).then_inc(sel_ready, 1)
            dve.wait_ge(len_psum, 1)
            then(dve.tensor_copy(len_all[:, 0:NG], bank[0][:, 0:NG]))
            then(dve.tensor_copy(len_all[0:BP, NG:NG + NT + 1], bank[0][0:BP, NG:NG + NT + 1]))
            then(dve.tensor_copy(len_all[:, 16:80], bank[0][:, 16:80]))
            then(dve.tensor_copy(slot_i[:, :], len_all[0:BP, NG:NG + NT]))
            then(dve.tensor_scalar(slot_i[:, :], slot_i[:, :], 4, None, ALU.logical_shift_right))
            then(dve.tensor_scalar(slot_f[:, :], slot_i[:, :], c9("slot"), 0.0, ALU.add, ALU.max))
            dve.scalar_tensor_tensor(tidx[:, :], slot_f[:, :], float(NBLK - 1), c9("table"), ALU.min,
                                     ALU.add).then_inc(tidx_ready, 1)
            dve.wait_ge(k128_in, 16)
            then(dve.tensor_scalar(pos[:, :], len_all[:, 0:NG], c1("tok"), None, ALU.add))
            then(dve.tensor_tensor(angle[:, :, :], over(pos[:, :], 2, HALF), over(c1("freq"), 1, NG), ALU.mult))
            flat = angle[:, :, :].rearrange("p g f -> p (g f)")
            t2 = turn[:, :, :, :].rearrange("p a g f -> p a (g f)")
            r2 = rest[:, :, :, :].rearrange("p a g f -> p a (g f)")
            then(dve.tensor_scalar(t2[:, 0, :], flat, 1.0 / TWO_PI, None, ALU.mult))
            then(dve.tensor_scalar(t2[:, 1, :], flat, 1.0 / TWO_PI, 0.25, ALU.mult, ALU.add))
            then(dve.tensor_scalar(t2, t2, MAGIC, None, ALU.add))
            then(dve.tensor_scalar(t2, t2, -MAGIC, None, ALU.add))
            then(dve.scalar_tensor_tensor(r2, t2, -PI_PARTS[0], over(flat, 1, 2), ALU.mult, ALU.add))
            then(dve.scalar_tensor_tensor(r2, t2, -PI_PARTS[1], r2, ALU.mult, ALU.add))
            then(dve.scalar_tensor_tensor(r2, t2, -PI_PARTS[2], r2, ALU.mult, ALU.add))
            then(dve.tensor_scalar(r2[:, 1, :], r2[:, 1, :], float(np.pi / 2), None, ALU.add))
            dve.tensor_scalar(r2, r2, 3.1415925, -3.1415925, ALU.min, ALU.max).then_inc(arg_ready, 1)
            for n in range(2):
                dve.wait_ge(xt_psum, 2 * n + 2)
                dve.tensor_copy(x_t[:, n, 4:8, :].rearrange("p g t -> p (g t)"), bank[2 + 2 * n][:, :]
                                ).then_inc(xt_ready, 1)
            dve.wait_ge(w_psum, 2)
            dve.tensor_copy(w_vkq[:, :, KV:], bank[6][:, :].rearrange("p (k c) -> p k c", k=KD)).then_inc(w_ready, 1)
            def writers():
                then(dve.tensor_copy(wr_i[:, :], len_all[0:BP, NG + NT:NG + NT + 1]))
                then(dve.tensor_scalar(wr_i[:, :], wr_i[:, :], BLOCK - 1, None, ALU.bitwise_and))
                then(dve.tensor_copy(wr_off[:, :], wr_i[:, :]))
                then(dve.tensor_tensor(wr_off[:, :], c9("wslot"), wr_off[:, :], ALU.subtract))
                then(dve.tensor_scalar(wr_d[:, :], c9("off"), wr_off[:, 0:1], None, ALU.add))
                then(dve.tensor_scalar(wr_e[:, :], wr_d[:, :], c9("wrow"), None, ALU.add))
                then(dve.scalar_tensor_tensor(wr_f[:, :], wr_d[:, :], 0.0, wr_e[:, :], ALU.is_ge, ALU.mult))
                then(dve.scalar_tensor_tensor(wr_e[:, :], wr_d[:, :], float(T - 1), wr_f[:, :], ALU.is_le, ALU.mult))
                dve.tensor_tensor(wr_diag[:, :, :], over(ident[0:BP, 0:NW], 1, BLOCK), over(wr_e[:, :], 2, NW),
                                  ALU.mult).then_inc(diag_ready, 1)

            def writer_blocks():
                dve.wait_ge(blk_in, 16 * NT)
                then(dve.tensor_copy(blk_f[:, :], blk_i[:, :]))
                dve.tensor_tensor(wid_sel[:, :, :], over(c9("writer"), 1, NT), over(blk_f[:, :], 2, BT * WS),
                                  ALU.mult).then_inc(widsel_ready, 1)

            def take_w_o():
                dve.wait_ge(w_psum, 3)
                dve.tensor_copy(w_o[:, :, :].rearrange("p h d -> p (h d)"), bank[7][:, :]).then_inc(w_ready, 1)

            def small_tables():
                then(dve.tensor_scalar(thresh[:, :], len_all[:, 16:16 + B], -BIG, BIG * WINDOW, ALU.mult, ALU.add))
                then(dve.tensor_scalar(adapt[:, :], len_all[:, 48:48 + B], c1("adapter"), None, ALU.is_equal))
                for k in range(4):
                    then(dve.tensor_scalar(bits_i[:, k:k + 1], len_i[:, :], k, 1, ALU.logical_shift_right,
                                           ALU.bitwise_and))
                then(dve.tensor_copy(bits[:, :], bits_i[:, :]))

            def move_v(t):
                dve.wait_ge(v_in, 16 * (t + 1))
                if t:
                    dve.wait_ge(blk_out, 16 * t)
                dve.tensor_copy(kv_blk[:, :, G * HD:KV].rearrange("p o (g d) -> p o g d", d=HD),
                                v_raw[:, :].rearrange("p (g o d) -> p o g d", g=G, d=HD)).then_inc(v_moved, 1)

            def norm_rope(j):
                kind, g = JOBS[j]
                n, nh, ng, src = (0, G, 4, k_in_f) if kind == "k" else (1, H, 2, q_in_f)
                dve.wait_ge(sq_ready, j + 1)
                dve.tensor_reduce(ssum[:, :], sq[:, :].rearrange("p (a d) -> p a d", d=HD), AX.X, ALU.add
                                  ).then_inc(ssum_ready, 1)
                dve.wait_ge(ssum_ready, j + 1)
                dve.tensor_scalar(meansq[:, :], ssum[:, :], 1.0 / HD, EPS, ALU.mult, ALU.add).then_inc(meansq_ready, 1)
                if kind == "k":
                    dve.wait_ge(vk_ready, g // 2 + 2)
                else:
                    dve.wait_ge(q_ready, g // 2 + 1)
                x4 = src[:, g:g + ng, :].rearrange("p t (h d) -> p t h d", d=HD)
                s4 = sin_x[:, :].rearrange("p (t h d) -> p t h d", t=ng, d=HD)
                for a in range(2):
                    mine, other = slice(a * HALF, (a + 1) * HALF), slice((1 - a) * HALF, (2 - a) * HALF)
                    then(dve.tensor_tensor(s4[:, :, :, mine], x4[:, :, :, other],
                                           over(rope_s[:, n, g:g + ng, mine], 2, nh), ALU.mult))
                if j < POOL_JOBS:
                    dve.wait_ge(cos_ready, j + 1)
                else:
                    then(dve.tensor_tensor(cos_x[:, :].rearrange("p (t h d) -> p t h d", t=ng, d=HD), x4,
                                           over(rope_c[:, n, g:g + ng, :], 2, nh), ALU.mult))
                then(dve.tensor_tensor(sin_x[:, :], sin_x[:, :], cos_x[:, :], ALU.add))
                dve.wait_ge(rms_ready, j + 1)
                then(dve.reciprocal(rstd[:, :], rms[:, :]))
                r4 = rstd[:, :].rearrange("p (t h) -> p t h", t=ng)
                if kind == "k":
                    last = dve.tensor_tensor(new_kv[:, g:g + 4, 0:G * HD].rearrange("p t (h d) -> p t h d", d=HD),
                                             s4, over(r4, 3, HD), ALU.mult)
                else:
                    if g:
                        dve.wait_ge(qt_psum, g // 2)
                    for h in range(GS):
                        last = dve.tensor_tensor(q_rot[:, :, h, :].rearrange("p t (g d) -> p t g d", d=HD),
                                                 sin_x[:, :].rearrange("p (t g h d) -> p t g h d", t=2, h=GS, d=HD)
                                                 [:, :, :, h, :],
                                                 over(r4.rearrange("p t (g h) -> p t g h", h=GS)[:, :, :, h], 3, HD),
                                                 ALU.mult)
                last.then_inc(job_done, 1)
                dve.wait_ge(job_done, j + 1)

            def find_winners(t):
                then(dve.tensor_scalar(same[:, :], wid_all[:, :], blk_f[:, t:t + 1], None, ALU.is_equal))
                then(dve.tensor_tensor(cand[:, :, :], wr_all[:, :, :], over(same[:, :], 1, BLOCK), ALU.mult))
                then(dve.tensor_reduce(winner[:, t * BLOCK:(t + 1) * BLOCK], cand[:, :, :], AX.X, ALU.max))

            def number_rows(t0, t1):
                c = slice(t0 * BLOCK, t1 * BLOCK)
                own = c9("own")[:, c]
                then(dve.tensor_scalar(won[:, c], winner[:, c], 0.0, None, ALU.is_gt))
                then(dve.scalar_tensor_tensor(winner[:, c], winner[:, c], float(TILE_ROWS - 1), own, ALU.add,
                                              ALU.subtract))
                then(dve.tensor_tensor(winner[:, c], winner[:, c], won[:, c], ALU.mult))
                dve.tensor_tensor(rows[:, c], winner[:, c], own, ALU.add).then_inc(rows_ready, 1)

            def shift_rows(ns):
                width = SLOTS * BLOCK
                for k in (3, 2, 1, 0):
                    width -= 1 << k
                    then(dve.tensor_tensor(row_d[0:ns, 0:width], row_b[0:ns, 1 << k:width + (1 << k)],
                                           row_b[0:ns, 0:width], ALU.subtract))
                    last = dve.scalar_tensor_tensor(row_b[0:ns, 0:width], row_d[0:ns, 0:width], bits[0:ns, k:k + 1],
                                                    row_b[0:ns, 0:width], ALU.mult, ALU.add)
                    if k:
                        then(last)
                last.then_inc(shift_ready, 1)

            writers()
            dve.wait_ge(scale_in, 32)
            then(dve.tensor_scalar(scale_qk[:, :, :], scale_qk[:, :, :], 1.0, None, ALU.add))
            then(dve.tensor_scalar(scale_sw[:, :, 0:HALF], scale_qk[:, :, HALF:HD], -1.0, None, ALU.mult))
            then(dve.tensor_copy(scale_sw[:, :, HALF:HD], scale_qk[:, :, 0:HALF]))
            dve.wait_ge(sin_ready, 1)
            for n in range(2):
                for dst, trig, s in ((rope_c, 1, scale_qk), (rope_s, 0, scale_sw)):
                    last = dve.tensor_tensor(dst[:, n, :, :].rearrange("p g (a f) -> p g a f", a=2),
                                             over(sincos[:, trig, :, :], 2, 2),
                                             over(s[:, n, :].rearrange("p (a f) -> p a f", a=2), 1, NG), ALU.mult)
                    if (n, trig) != (1, 0):
                        then(last)
            last.then_inc(rope_ready, 1)
            writer_blocks()
            norm_rope(0)
            move_v(0)
            dve.wait_ge(wid_psum, 1)
            then(dve.tensor_copy(wid_all[:, :], bank[0][0:BP, 0:NW]))
            dve.wait_ge(wr_ready, 3)
            find_winners(0)
            number_rows(0, 1)
            norm_rope(1)
            take_w_o()
            small_tables()
            norm_rope(2)
            dve.wait_ge(rows_in, 16)
            shift_rows(BT)
            dve.wait_ge(place_psum, 1)
            dve.tensor_copy(far_i[:, 0:BT], bank[0][:, 0:BT]).then_inc(place_ready, 1)
            dve.tensor_copy(near_i[:, 0:2], bank[0][:, B:B + 2]).then_inc(place_ready, 1)
            dve.tensor_copy(bias[:, :], bank[0][:, B + NG:B + 2 * NG]).then_inc(place_ready, 1)
            norm_rope(3)
            norm_rope(4)
            move_v(1)
            find_winners(1)
            norm_rope(5)

            def row(ap, n):
                return ap[:, bass.ds(n, 1), :].rearrange("p a d -> p (a d)")

            def attention(stage, n, r, b, pair):
                first = isinstance(pair, int) and pair == 0
                if stage == "kt":
                    dve.wait_ge(kt_psum, n + 1)
                    dve.tensor_copy(k_t[r][:, :, P:SPAN], b[1][:, 0:P].rearrange("p (s i) -> p s i", s=GB)
                                    ).then_inc(near_kt_ready, 1)
                    for s in range(GB):
                        last = dve.scalar_tensor_tensor(mask[r][:, s, :], c1("posbig"),
                                                        thresh[:, bass.ds(GB * n + s, 1)], c1("hide"),
                                                        ALU.subtract, ALU.min)
                    last.then_inc(mask_ready, 1)
                elif stage == "scores":
                    dve.wait_ge(mask_ready, n + 1)
                    for half in range(2):
                        dve.wait_ge(scores_psum, 2 * n + half + 1)
                        dve.nop(nofuse=True)
                        for j in range(4 * half, 4 * half + 4):
                            s = (j // 2) % 2
                            last = dve.tensor_tensor_reduce(
                                prob[r][:, j // 2, j % 2, :], b[(2, 0)[half] + j % 2][:, s * SPAN:(s + 1) * SPAN],
                                mask[r][:, j // 2, :], 1.0, -3.0e38, ALU.add, ALU.max, top[r][:, j:j + 1])
                        last.then_inc(top_ready, 1)
                        dve.wait_ge(top_ready, 2 * n + half + 1)
                        q = slice(4 * half, 4 * half + 4)
                        dve.tensor_scalar(ntop[r][:, q], top[r][:, q], -SCALE, None, ALU.mult).then_inc(ntop_ready, 1)
                    for half in range(2):
                        dve.wait_ge(exp_ready, 2 * n + half + 1)
                        q = slice(4 * half, 4 * half + 4)
                        dve.reciprocal(rden[r][:, q], den[r][:, q]).then_inc(rden_ready, 1)
                elif stage == "pt":
                    dve.wait_ge(pfar_psum, 2 * n + 2)
                    dve.tensor_copy(p_far[r][:, 2:4, :].rearrange("p s c -> p (s c)"), b[3][:, :]
                                    ).then_inc(pfar1_ready, 1)
                    dve.wait_ge(pnear_psum, n + 1)
                    dve.tensor_tensor(p_near[r][:, :, :], over(b[0][:, 0:2 * P], 1, GB),
                                      over(c1("sample"), 2, 2 * P), ALU.mult).then_inc(pnear_ready, 1)
                elif stage == "wo":
                    dve.wait_ge(wo_psum, n + 1)
                    dve.tensor_tensor(x1[r][:, :], b[0][:, 0:D], row(xs, n), ALU.add).then_inc(x1_ready, 1)
                elif stage == "mix1":
                    dve.wait_ge(mix1_psum, n + 1)
                    dve.tensor_tensor(x2[r][:, :], b[2][:, 0:D], x1[r][:, :], ALU.add).then_inc(x2_ready, 1)
                elif stage == "mix2":
                    dve.wait_ge(mix2_psum, n + 1)
                    dve.wait_ge(x2_ready, n + 1)
                    if not first:
                        dve.wait_ge(x3_kept, n - 1)
                    dve.scalar_tensor_tensor(x3[r][:, :], b[3][:, 0:D], bias[:, bass.ds(n, 1)], x2[r][:, :],
                                             ALU.add, ALU.add).then_inc(x3_ready, 1)
                elif stage == "xf":
                    dve.wait_ge(xfhigh_ready, n + 1)
                    dve.tensor_tensor(xf_half(xf_low, r), x3_t[:, :, r, :], xf_half(xf_high, r).bitcast(F32),
                                      ALU.subtract).then_inc(xf_ready, 1)

            def h_low_part(m, f):
                dve.wait_ge(hhigh_ready, NF * m + f + 1)
                dve.tensor_tensor(h_low[:, f, :], hf[f % 2][:, :], h_high[:, f, :].bitcast(F32), ALU.subtract
                                  ).then_inc(h_ready, 1)

            def h_whole(m, f):
                b = FFN_BANKS[f % 3]
                at = NF * m + f + 1
                dve.wait_ge(tanh_ready, at)
                dve.scalar_tensor_tensor(gs[f % 2][:, :], th[f % 3][:, :], 1.0, b[:, 0:PAIR_TOK], ALU.add,
                                         ALU.mult).then_inc(gs_ready, 1)
                dve.wait_ge(gs_ready, at)
                dve.scalar_tensor_tensor(hf[f % 2][:, :], b[:, PAIR_TOK:], 0.5, gs[f % 2][:, :], ALU.mult,
                                         ALU.mult).then_inc(hf_ready, 1)

            def ffn(piece, m):
                if piece == "adapt":
                    dve.wait_ge(low_psum, m + 1)
                    for a in range(2):
                        last = dve.tensor_tensor(
                            low_raw[:, a * PAIR_TOK:(a + 1) * PAIR_TOK].rearrange("p (s t) -> p s t", t=T),
                            FFN_BANKS[3][:, a * PAIR_TOK:(a + 1) * PAIR_TOK].rearrange("p (s t) -> p s t", t=T),
                            over(adapt[:, bass.ds(2 * GB * m, 2 * GB)], 2, T), ALU.mult)
                    last.then_inc(lowraw_ready, 1)
                if piece == "up0":
                    dve.wait_ge(lowhigh_ready, m + 1)
                    dve.tensor_tensor(low_low[:, :], low_raw[:, :], low_high[:, :].bitcast(F32), ALU.subtract
                                      ).then_inc(low_ready, 1)
                if piece.startswith("up"):
                    f = int(piece[2:])
                    h_whole(m, f)
                    if f:
                        h_low_part(m, f - 1)
                elif piece == "down00":
                    h_low_part(m, NF - 1)
                elif piece == "down_lora":
                    dve.wait_ge(lowd_psum, m + 1)
                    dve.tensor_tensor(lowd_raw[:, :].rearrange("p (s t) -> p s t", t=T),
                                      FFN_BANKS[0][:, 0:PAIR_TOK].rearrange("p (s t) -> p s t", t=T),
                                      over(adapt[:, bass.ds(2 * GB * m, 2 * GB)], 2, T), ALU.mult
                                      ).then_inc(lowdraw_ready, 1)
                    dve.wait_ge(lowdhigh_ready, m + 1)
                    dve.tensor_tensor(lowd_low[:, :], lowd_raw[:, :], lowd_high[:, :].bitcast(F32), ALU.subtract
                                      ).then_inc(lowd_ready, 1)
                elif piece == "tail":
                    for r in R:
                        dve.wait_ge(down_psum, 2 * m + r + 1)
                        dve.wait_ge(x3_kept, 2 * m + r + 1)
                        dve.tensor_tensor(row(xs, 2 * m + r), FFN_BANKS[3 - r][:, 0:D], row(xs, 2 * m + r), ALU.add
                                          ).then_inc(y_ready, 1)

            def steps(order, m, pair):
                first_pair = order is START_ORDER
                for step in order:
                    if isinstance(step, str):
                        ffn(step, m)
                    elif step[0] == "winner":
                        find_winners(step[1])
                    elif step[0] == "rows":
                        number_rows(1, NT)
                    elif step[0] == "split" and SPLITS[step[1]] == "dve":
                        take_low(dve, step[1])
                    elif step[0] == "move":
                        move_v(step[1])
                    elif step[0] == "shift":
                        dve.wait_ge(rows_in, 32)
                        shift_rows(B)
                    elif step[0] == "place":
                        dve.wait_ge(place_psum, 2)
                        dve.tensor_copy(far_i[:, BT:B], bank[0][:, BT:B]).then_inc(place_ready, 1)
                        dve.tensor_copy(near_i[:, 2:NG], bank[0][:, B + 2:B + NG]).then_inc(place_ready, 1)
                    elif step[0] in STAGES:
                        stage, r = step
                        attention(stage, 2 * m + 2 + r, r, HIGH_BANKS if first_pair and r else LOW_BANKS, pair)

            steps(START_ORDER, -1, 0)
            steps(FIRST_ORDER, 0, 1)
            with dve.Fori(1, NPAIR - 1) as m:
                steps(LOOP_ORDER, m, m + 1)
            for piece in FFN_PIECES:
                ffn(piece, NPAIR - 1)

        @block.tensor
        def _(pe):
            pe.wait_ge(sel_ready, 1)
            pe.wait_ge(ones_set, 2)
            o = NG + NT + 1
            pe.matmul(bank[0][:, 0:NG], c3("tok_b"), len_sel[:, 0:NG], start=True, stop=True)
            pe.matmul(bank[0][0:BP, NG:NG + NT], c3("blk_b"), len_sel[:, NG:NG + NT], start=True, stop=True)
            pe.matmul(bank[0][0:BP, NG + NT:o], c3("wrt_b"), len_f[:, :], start=True, stop=True)
            pe.matmul(bank[0][:, 16:16 + B], ones[0:B, :], len_sel[:, o:o + B], start=True, stop=True)
            pe.matmul(bank[0][:, 48:48 + B], ones[0:B, :], ad_sel[:, :], start=True, stop=True).then_inc(len_psum, 1)
            pe.wait_ge(k128_in, 16)
            pe.wait_ge(x_in, 16)
            for k in range(KD):
                for hf in range(2):
                    for g in range(4):
                        last = pe.transpose(bank[1 + 2 * k + hf][:, g * P:(g + 1) * P],
                                            xs[:, 4 * hf + g, k * P:(k + 1) * P], ident)
                    last.then_inc(xt_psum, 1)
            pe.wait_ge(wvkq_in, 48)
            for at, pieces in ((5, (wv_raw, wk_raw)), (6, (wq_raw[:, 0, :], wq_raw[:, 1, :]))):
                for k in range(KD):
                    for j, w in enumerate(pieces):
                        last = pe.transpose(bank[at][:, (2 * k + j) * P:(2 * k + j + 1) * P], w[:, k * P:(k + 1) * P],
                                            ident)
                last.then_inc(w_psum, 1)

            def turn_w_o():
                pe.wait_ge(wo_in, 64)
                for h in range(GS):
                    for a in range(2):
                        last = pe.transpose(bank[7][:, h * D + a * P:h * D + (a + 1) * P], wo_raw[:, a, h, :], ident)
                last.then_inc(w_psum, 1)

            def project(i, dst, cols, done):
                for t in range(2):
                    for k in range(KD):
                        last = pe.matmul(bank[dst][:, t * D:(t + 1) * D], x_t[:, k, 2 * i + t, :], w_vkq[:, k, cols],
                                         start=(k == 0), stop=(k == KD - 1))
                last.then_inc(done, 1)

            pe.wait_ge(xt_ready, 4)
            pe.wait_ge(w_ready, 2)
            for i in range(2):
                project(i, 1 + i, slice(0, KV), vk_psum)
            pe.wait_ge(diag_ready, 1)
            for n in range(3):
                last = pe.matmul(bank[5 + n][0:BP, :], ones16[:, :],
                                 wr_diag[:, :, :].rearrange("p o w -> p (o w)")[:, 512 * n:512 * (n + 1)],
                                 start=True, stop=True)
            last.then_inc(wr_psum, 1)
            for i in range(2, 4):
                project(i, 1 + i, slice(0, KV), vk_psum)
            pe.wait_ge(widsel_ready, 1)
            pe.matmul(bank[0][0:BP, 0:NW], ones[0:BP, 0:BP], wid_sel[:, :, :].rearrange("p t w -> p (t w)"),
                      start=True, stop=True).then_inc(wid_psum, 1)
            pe.wait_ge(wr_ready, 3)
            project(0, 5, slice(KV, 512), q_psum)
            turn_w_o()
            project(1, 6, slice(KV, 512), q_psum)
            pe.wait_ge(vk_ready, 2)
            project(2, 1, slice(KV, 512), q_psum)
            project(3, 2, slice(KV, 512), q_psum)

            def turn_q(i):
                pe.wait_ge(job_done, 3 + i)
                if i >= 2:
                    pe.wait_ge(qt_ready, i - 1)
                for t in range(2):
                    for h in range(GS):
                        last = pe.transpose(bank[3 + i % 2][:, (t * GS + h) * P:(t * GS + h + 1) * P],
                                            q_rot[:, t, h, :], ident)
                last.then_inc(qt_psum, 1)

            def place(ns, with_bias):
                n = ns // GB
                pe.transpose(bank[0][:, 0:ns], row_b[0:ns, 0:P], ident[0:ns, 0:ns])
                for s in range(GB):
                    q = slice(s * T, (s + 1) * T)
                    sel = c3("group")[:, s * NG:(s + 1) * NG]
                    last = pe.matmul(bank[0][q, B:B + n], row_b[0:ns, P:SPAN], sel[0:ns, 0:n], start=True, stop=True,
                                     tile_position=(0, s * T))
                    if with_bias:
                        last = pe.matmul(bank[0][q, B + NG:B + 2 * NG], side_b[:, :], sel, start=True, stop=True,
                                         tile_position=(0, s * T))
                last.then_inc(place_psum, 1)

            pe.wait_ge(vk_ready, 4)
            turn_q(0)
            pe.wait_ge(shift_ready, 1)
            pe.wait_ge(side_in, 16)
            place(BT, True)
            for i in range(1, 4):
                turn_q(i)
            pe.wait_ge(place_ready, 3)
            pe.wait_ge(w_ready, 3)

            def attention(stage, n, r, b, pair):
                first = isinstance(pair, int) and pair == 0
                if stage == "kt":
                    pe.wait_ge(kv_in[r], (pair + 1) * (GB + 1) * 16)
                    if first:
                        pe.wait_ge(qt_ready, NT)
                    else:
                        pe.wait_ge(x3t_ready, n)
                    for s in range(GB):
                        pe.transpose(b[0][:, s * P:(s + 1) * P], far[r][:, s, 0:G * HD], ident)
                    pe.transpose(b[1][:, 0:P], near[r][:, 0:G * HD], ident).then_inc(kt_psum, 1)
                elif stage == "scores":
                    pe.wait_ge(far_kt_ready, n + 1)
                    pe.wait_ge(near_kt_ready, n + 1)
                    pe.wait_ge(qbd_ready, 2 * n + 2)
                    for half in range(2):
                        for s in range(2):
                            for c in range(2):
                                q = slice(64 * c, 64 * c + 64)
                                last = pe.matmul(b[(2, 0)[half] + c][:, s * SPAN:(s + 1) * SPAN],
                                                 q_bd[r][q, 2 * half + s, :, :, :].rearrange("p g h t -> p (g h t)"),
                                                 k_t[r][q, 2 * half + s, :], start=True, stop=True)
                        last.then_inc(scores_psum, 1)
                elif stage == "pt":
                    for half in range(2):
                        pe.wait_ge(prob_ready, 4 * n + 2 * half + 1)
                        for j in range(4):
                            last = pe.transpose(b[2 + half][:, j * P:(j + 1) * P],
                                                prob[r][:, 2 * half + j // 2, j % 2, 0:P], ident)
                        last.then_inc(pfar_psum, 1)
                    pe.wait_ge(prob_ready, 4 * n + 4)
                    for c in range(2):
                        last = pe.transpose(b[0][:, c * P:(c + 1) * P],
                                            prob_near[r][:, c, :, :].rearrange("p s i -> p (s i)"), ident)
                    last.then_inc(pnear_psum, 1)
                elif stage == "pv":
                    pe.wait_ge(pfar0_ready, n + 1)
                    pe.wait_ge(pfar1_ready, n + 1)
                    pe.wait_ge(pnear_ready, n + 1)
                    for s in range(GB):
                        for v_rows, pr, st in ((far[r][:, s, :], p_far[r], True), (near[r][:, :], p_near[r], False)):
                            for g in range(G):
                                last = pe.matmul(b[1][g * HD:(g + 1) * HD, s * 2 * T:(s + 1) * 2 * T],
                                                 v_rows[:, G * HD + g * HD:G * HD + (g + 1) * HD],
                                                 pr[:, s, g * 2 * T:(g + 1) * 2 * T], start=st, stop=not st,
                                                 tile_position=(0, g * HD))
                    last.then_inc(o_psum, 1)
                elif stage == "wo":
                    pe.wait_ge(o_ready, n + 1)
                    for h in range(GS):
                        last = pe.matmul(b[0][:, 0:D], o_t[r][:, h, :, :].rearrange("p s t -> p (s t)"), w_o[:, h, :],
                                         start=(h == 0), stop=(h == GS - 1))
                    last.then_inc(wo_psum, 1)
                elif stage == "mix1":
                    pe.wait_ge(x1_ready, n + 1)
                    pe.wait_ge(wmix_ready, 2 * n + 2)
                    pe.matmul(b[2][:, 0:D], w_mix[r][:, 0, :, :].rearrange("p s d -> p (s d)"), x1[r][:, :],
                              start=True, stop=True).then_inc(mix1_psum, 1)
                elif stage == "mix2":
                    pe.wait_ge(x2_ready, n + 1)
                    pe.matmul(b[3][:, 0:D], w_mix[r][:, 1, :, :].rearrange("p s d -> p (s d)"), x2[r][:, :],
                              start=True, stop=True).then_inc(mix2_psum, 1)
                elif stage == "xt":
                    pe.wait_ge(x3_ready, n + 1)
                    for k in range(KD):
                        last = pe.transpose(b[0][:, k * P:(k + 1) * P], x3[r][:, k * P:(k + 1) * P], ident)
                    last.then_inc(x3t_psum, 1)

            def product(dst, w, x, start, stop):
                for n, (a, b) in enumerate(((0, 0), (0, 1), (1, 0))):
                    last = pe.matmul(dst, w[a], x[b], start=start and n == 0, stop=stop and n == 2)
                return last

            def base_product(a, f):
                for k in range(KD):
                    product(FFN_BANKS[f % 3][:, a * PAIR_TOK:(a + 1) * PAIR_TOK],
                            [w[:, a, k, f * P:(f + 1) * P] for w in w_gu], [x[:, k, :] for x in m_xf], k == 0, False)

            def ffn(piece, m):
                if piece == "lora":
                    pe.wait_ge(xf_ready, 2 * m + 2)
                    if not (isinstance(m, int) and m == 0):
                        pe.wait_ge(y_ready, 2 * m - 1)
                    for a in range(2):
                        for k in range(KD):
                            last = product(FFN_BANKS[3][:, a * PAIR_TOK:(a + 1) * PAIR_TOK],
                                           [w[:, a, k, :] for w in w_a], [x[:, k, :] for x in m_xf],
                                           k == 0, k == KD - 1)
                    last.then_inc(low_psum, 1)
                elif piece.startswith("gate") or piece.startswith("up"):
                    a = int(piece.startswith("up"))
                    f = int(piece[-1])
                    if piece == "gate0":
                        for n in range(3):
                            if n == 2 and not (isinstance(m, int) and m == 0):
                                pe.wait_ge(y_ready, 2 * m)
                            base_product(0, n)
                        pe.wait_ge(low_ready, m + 1)
                    elif a == 0 and f >= 3:
                        pe.wait_ge(hf_ready, NF * m + f - 2)
                        base_product(0, f)
                    elif a:
                        base_product(1, f)
                    last = product(FFN_BANKS[f % 3][:, a * PAIR_TOK:(a + 1) * PAIR_TOK],
                                   [w[:, a, f * P:(f + 1) * P] for w in w_b], [x[:, a, :] for x in m_low], False, True)
                    if a:
                        last.then_inc(gu_psum, 1)
                elif piece == "down_lora":
                    pe.wait_ge(h_ready, NF * m + NF)
                    for k in range(NF):
                        last = product(FFN_BANKS[0][:, 0:PAIR_TOK], [w[:, k, :] for w in w_ad],
                                       [x[:, k, :] for x in m_h], k == 0, k == NF - 1)
                    last.then_inc(lowd_psum, 1)
                elif piece == "tail":
                    for r in R:
                        for k in range(NF - 2, NF):
                            down(r, k)
                    pe.wait_ge(lowd_ready, m + 1)
                    for r in R:
                        product(FFN_BANKS[3 - r][:, 0:D], [x[:, r * P:(r + 1) * P] for x in m_lowd],
                                w_bd, False, True).then_inc(down_psum, 1)
                elif piece.startswith("down"):
                    r, third = int(piece[4]), int(piece[5])
                    if r == 0:
                        pe.wait_ge(h_ready, NF * m + 3 * third + 3)
                    for k in range(3 * third, 3 * third + 3):
                        down(r, k)

            def down(r, k):
                product(FFN_BANKS[3 - r][:, 0:D], [x[:, k, r * P:(r + 1) * P] for x in m_h],
                        [w[:, k, :] for w in w_d], k == 0, False)

            def steps(order, m, pair):
                first_pair = order is START_ORDER
                for step in order:
                    if isinstance(step, str):
                        ffn(step, m)
                    elif step[0] == "use":
                        pe.wait_ge(split_ready[step[1]], 1)
                    elif step[0] == "place":
                        pe.wait_ge(shift_ready, 2)
                        pe.wait_ge(x3t_ready, 2)
                        place(B, False)
                        pe.wait_ge(place_ready, 5)
                    elif step[0] in STAGES:
                        stage, r = step
                        attention(stage, 2 * m + 2 + r, r, HIGH_BANKS if first_pair and r else LOW_BANKS, pair)

            steps(START_ORDER, -1, 0)
            steps(FIRST_ORDER, 0, 1)
            with pe.Fori(1, NPAIR - 1) as m:
                steps(LOOP_ORDER, m, m + 1)
            for piece in FFN_PIECES:
                ffn(piece, NPAIR - 1)


NAMES = [("x", "x"), ("itok_Bx257_0_4111", "table"), ("itok_B_37_3939", "lens"), ("itok_B_1_198", "cond"),
         ("itok_B_0_7", "subj"), ("fside_8xS_0", "side"), ("L0_cond_Wq", "Wq"), ("L0_cond_Wk", "Wk"),
         ("L0_cond_Wv", "Wv"), ("L0_cond_Wo", "Wo"), ("L0_cond_q_norm_scale", "qs"), ("L0_cond_k_norm_scale", "ks"),
         ("L0_cond_k_blocks", "kb"), ("L0_cond_v_blocks", "vb"), ("L1_cond_weights", "w1"), ("L2_cond_weights", "w2"),
         ("L3_cond_Wg", "Wg"), ("L3_cond_Wu", "Wu"), ("L3_cond_Wd", "Wd"), ("L3_cond_Ag", "Ag"),
         ("L3_cond_Bg", "Bg"), ("L3_cond_Au", "Au"), ("L3_cond_Bu", "Bu"), ("L3_cond_Ad", "Ad"), ("L3_cond_Bd", "Bd")]


def kernel(**inputs):
    import concourse.bacc as bacc
    from concourse.bass_utils import run_bass_kernel_spmd

    nc = bacc.Bacc("TRN2", target_bir_lowering=False, num_devices=1)
    arrays, args = {}, {}

    def give(name, a):
        a = np.ascontiguousarray(a)
        arrays[f"in_{name}"] = a
        args[name] = nc.dram_tensor(f"in_{name}", a.shape, mybir.dt.from_np(a.dtype), kind="ExternalInput").ap()

    for name, short in NAMES:
        give(short, inputs[name])
    for name, a in zip(("c128", "c96", "c32"), tables()):
        give(name, a)
    args["out"] = nc.dram_tensor("out", (B, T, D), F32, kind="ExternalOutput").ap()
    build(nc, **args)
    r = run_bass_kernel_spmd(nc, [arrays], core_ids=[0])
    return r.results[0]["out"]
```

```python
from contextlib import ExitStack

import concourse.bass as bass
import numpy as np
from concourse import mybir

F32 = mybir.dt.float32
F16 = mybir.dt.float16
F32R = mybir.dt.float32r
I32 = mybir.dt.int32
ALU = mybir.AluOpType
ACT = mybir.ActivationFunctionType
AX = mybir.AxisListType

P = 128
B, T, D = 32, 32, 256
H, G, HD = 8, 4, 32
GS = H // G
HALF = HD // 2
BLOCK, WINDOW = 16, 128
NBLK = 257
CACHE_BLOCKS = 16 * NBLK
GB = P // T
NG = B // GB
NPAIR = NG // 2
KD = D // P
SPAN = WINDOW + T
SLOTS = 12
BT = 8
NT = B // BT
BP = BT * SLOTS
BACK = WINDOW // BLOCK
WS = 3
NW = B * WS
KV = 2 * G * HD
BELEMS = G * BLOCK * HD
OLD_ROWS = B * SLOTS * BLOCK
NEW_ROWS = B * T
TILE_ROWS = BP * BLOCK
FF = 1024
NF = FF // P
NR = 128
RANK = 16
SCALE = 256.0 ** -0.5
EPS = 1e-6
THETA = 10000.0
BIG = 2.0 ** 100
TWO_PI = 2.0 * np.pi
PI_PARTS = (6.28125, 0.0019350051879882812, 3.019915981956753e-07)
MAGIC = 1.5 * 2.0 ** 23
PAIR_TOK = 2 * P


def layout(fields):
    at, where = 0, {}
    for name, n in fields:
        where[name] = (at, at + n)
        at += n
    return where, at


C128, C128_N = layout([("ident", P), ("hide", SPAN), ("posbig", SPAN), ("pair", 2), ("sample", GB),
                       ("tok", 1), ("adapter", 1), ("freq", HALF)])
C96, C96_N = layout([("slot", 1), ("table", NT), ("own", NT * BLOCK), ("writer", BT * WS), ("off", BLOCK),
                     ("wslot", 1), ("wrow", 1)])
C32, C32_N = layout([("tok_b", P), ("blk_b", BP), ("wrt_b", NW), ("of_len", NG + NT + 1 + B), ("group", GB * NG)])


def tables():
    p = np.arange(P)
    a = np.zeros((P, C128_N), np.float32)

    def put(arr, where, name, v):
        lo, hi = where[name]
        arr[:, lo:hi] = v

    i = np.arange(SPAN)[None, :]
    t = (p % T)[:, None]
    put(a, C128, "ident", np.eye(P))
    put(a, C128, "hide", np.where((i > t) & (i <= WINDOW + t), 0.0, -BIG))
    put(a, C128, "posbig", i * BIG)
    put(a, C128, "pair", (p[:, None] // HD) % 2 == np.arange(2)[None, :])
    put(a, C128, "sample", p[:, None] // T == np.arange(GB)[None, :])
    put(a, C128, "tok", t)
    put(a, C128, "adapter", p[:, None] // RANK)
    half = np.arange(HALF, dtype=np.float32) / np.float32(HALF)
    put(a, C128, "freq", (np.float32(1.0) / np.power(np.float32(THETA), half))[None, :])
    q = np.arange(BP)
    b = np.zeros((BP, C96_N), np.float32)
    tile = np.arange(NT)[None, :]
    put(b, C96, "slot", (q % SLOTS - BACK)[:, None])
    put(b, C96, "table", (tile * BT + (q // SLOTS)[:, None]) * NBLK)
    own = ((tile[:, :, None] * BT + (q // SLOTS)[:, None, None]) * SLOTS + (q % SLOTS)[:, None, None]) * BLOCK
    own += np.where(tile > 0, NEW_ROWS, 0)[:, :, None]
    put(b, C96, "own", (own + np.arange(BLOCK)[None, None, :]).reshape(BP, -1))
    w = np.arange(BT * WS)[None, :]
    put(b, C96, "writer", q[:, None] == (w // WS) * SLOTS + BACK + w % WS)
    put(b, C96, "off", np.arange(BLOCK)[None, :])
    put(b, C96, "wslot", ((q % WS) * BLOCK)[:, None])
    put(b, C96, "wrow", ((q // WS) * T + 1)[:, None])
    s = np.arange(B)[:, None]
    c = np.zeros((B, C32_N), np.float32)
    put(c, C32, "tok_b", s % GB == p[None, :] // T)
    put(c, C32, "blk_b", s % BT == q[None, :] // SLOTS)
    put(c, C32, "wrt_b", s == np.arange(NW)[None, :] // WS)
    put(c, C32, "of_len", np.concatenate([s // GB == np.arange(NG)[None, :], s // BT == np.arange(NT)[None, :],
                                          np.ones((B, 1)), np.eye(B)], axis=1))
    g = np.arange(GB * NG)[None, :]
    put(c, C32, "group", s == (g % NG) * GB + g // NG)
    return a, b, c


FFN_PIECES = (["lora", "adapt"] + [f"{k}{f}" for f in range(NF) for k in ("gate", "up")]
              + ["down00", "down01", "down10", "down11", "down_lora0", "down_lora1", "tail0", "tail1", "tail2"])
STAGES = ["kt", "scores", "den", "pt0", "pt1", "pv", "wo", "mix1", "mix2", "xt", "xf"]
LOOP_ORDER = (
    [("spread", 0), ("kt", 0), "lora", "adapt", ("scores", 0), "gate0", ("den", 0), "up0", "gate1", "up1",
     ("pt0", 0), "gate2", ("pt1", 0), ("fetch", 1), ("spread", 1), "up2", "gate3", ("pv", 0), "up3",
     ("wo", 0), "gate4", ("mix1", 0), "up4", ("mix2", 0), ("ahead", 0), "gate5", ("xt", 0), "up5", ("kt", 1),
     "gate6", "up6", ("scores", 1), "gate7", ("den", 1), "up7", ("xf", 0), "down00", "down01", ("pt0", 1),
     "down10", ("pt1", 1), ("next_mask", 0), ("next_mask", 1), "down11", "down_lora0", ("pv", 1),
     "down_lora1", ("wo", 1), "tail0", ("mix1", 1), "tail1", ("mix2", 1), "tail2", ("xt", 1), ("xf", 1)])

START_ORDER = (
    [("mask", 0), ("kt", 0), ("scores", 0), ("rotate", 2), ("move_k", 2), ("den", 0), ("pt0", 0),
     ("normalise", 2), ("move_v", 2), ("load", 3), ("winner", 1), ("pt1", 0), ("kt", 1), ("mask", 1),
     ("scores", 1), ("winner", 2), ("pv", 0), ("den", 1), ("move_k", 3), ("move_v", 3), ("wo", 0),
     ("winner", 3), ("rows", 1), ("pt0", 1), ("pt1", 1), ("split", "a"), ("mix1", 0), ("split", "gu0"),
     ("split", "gu1"), ("mix2", 0), ("next_mask", 0), ("pv", 1), ("xt", 0), ("shift", 1), ("wo", 1),
     ("place", 1), ("ahead", 0), ("mix1", 1), ("xf", 0), ("mix2", 1), ("split", "b"), ("xt", 1), ("xf", 1),
     ("next_mask", 1)])
FIRST_ORDER = (
    [("spread", 0), ("warm", 16, 1), ("kt", 0), ("use", "a"), "lora", "adapt", ("scores", 0), ("use", "b"),
     ("use", "gu0"), ("use", "gu1"), "gate0", ("den", 0), ("split", "ad"), "up0", ("pt0", 0), "gate1", "up1",
     ("pt1", 0), ("split", "d"), ("fetch", 1), ("spread", 1), "gate2", "up2", "gate3", ("pv", 0), "up3",
     ("wo", 0), "gate4", ("mix1", 0), "up4", ("mix2", 0), ("ahead", 0), ("split", "bd"), "gate5", ("xt", 0),
     "up5", ("kt", 1), "gate6", "up6", ("scores", 1), "gate7", ("den", 1), "up7", ("xf", 0), ("use", "d"),
     "down00", "down01", ("pt0", 1), "down10", ("pt1", 1), ("next_mask", 0), ("next_mask", 1), "down11",
     ("use", "ad"), "down_lora0", ("pv", 1), "down_lora1", ("wo", 1), "tail0", ("mix1", 1), "tail1",
     ("mix2", 1), ("use", "bd"), "tail2", ("xt", 1), ("xf", 1)])
SPLITS = {"a": "pool", "gu0": "pool", "gu1": "pool", "b": "dve", "ad": "pool", "d": "dve", "bd": "pool"}
JOBS = [("k", 0, NG), ("q", 0, 2), ("q", 2, NG - 2)]
JOB_COLS = [n * (G if kind == "k" else H) * HD for kind, _, n in JOBS]
JOB_AT = [sum(JOB_COLS[:j]) for j in range(len(JOBS) + 1)]
SQ_AT = [0, JOB_COLS[0], 0]


def build(nc, x, table, lens, cond, subj, side, Wq, Wk, Wv, Wo, qs, ks, kb, vb, w1, w2,
          Wg, Wu, Wd, Ag, Bg, Au, Bu, Ad, Bd, c128, c96, c32, out):
    ctx = ExitStack()
    with ctx:
        def sb(name, shape, dt=F32):
            return ctx.enter_context(nc.sbuf_tensor(name, shape, dt))

        def share(*layers):
            sizes, made = [], []
            for layer in layers:
                with ExitStack() as inner:
                    made.append([inner.enter_context(nc.sbuf_tensor(name, shape, dt)) for name, shape, dt in layer])
                sizes.append(sum(-(-int(np.prod(shape[1:])) * (2 if dt == F16 else 4) // 32) * 8
                                 for _, shape, dt in layer))
            sb(f"place_of_{layers[0][0][0]}", [P, max(sizes)])
            return made

        def sem(name):
            return ctx.enter_context(nc.semaphore(name))

        kv_rows = nc.dram_tensor("kv_rows", (OLD_ROWS + NEW_ROWS, KV), F32, kind="Internal").ap()
        row_table = nc.dram_tensor("row_table", (B, SLOTS * BLOCK), F32, kind="Internal").ap()
        mix_rows = nc.dram_tensor("mix_rows", (2, B, T * T), F32, kind="Internal").ap()

        k128 = sb("k128", [P, C128_N])
        k96 = sb("k96", [BP, C96_N])
        k32 = sb("k32", [B, C32_N])
        ones = sb("ones", [P, P])
        ones16 = sb("ones16", [BP, BP], F16)

        def c1(name):
            return k128[:, C128[name][0]:C128[name][1]]

        def c9(name):
            return k96[:, C96[name][0]:C96[name][1]]

        def c3(name):
            return k32[:, C32[name][0]:C32[name][1]]

        ident = c1("ident")

        ((q_in_f, k_in_f, sin_x, wq_raw, wk_raw, wv_raw, w_vkq), (gu_raw, b_raw, ad_raw),
         (gu_low, b_low, ad_low)) = share(
            [("q_in_f", [P, NG, H * HD], F32), ("k_in_f", [P, NG, G * HD], F32),
             ("sin_x", [P, max(JOB_COLS)], F32), ("wq_raw", [P, 2, D], F32), ("wk_raw", [P, D], F32),
             ("wv_raw", [P, D], F32), ("w_vkq", [P, KD, 512], F32)],
            [("gu_raw", [P, 2 * KD, FF], F32), ("b_raw", [NR, 2 * FF], F32), ("ad_raw", [P, NF * NR], F32)],
            [("gu_low", [P, 2 * KD, FF], F32R), ("b_low", [NR, 2 * FF], F32R), ("ad_low", [P, NF * NR], F32R)])
        (wo_raw,), (a_high,) = share([("wo_raw", [P, 2, GS, G * HD], F32)],
                                     [("a_high", [P, 2 * KD * NR], F32R)])
        w_o = sb("w_o", [P, GS, D])
        (early,), (gu_high,) = share([("early", [P, 2 * BELEMS], F32)],
                                     [("gu_high", [P, 2 * KD, FF], F32R)])
        (angle, turn, rest, sincos), (moved,), (d_high, b_high) = share(
            [("angle", [P, NG, HALF], F32), ("turn", [P, 2, NG, HALF], F32), ("rest", [P, 2, NG, HALF], F32),
             ("sincos", [P, 2, NG, HALF], F32)],
            [("moved", [P, BLOCK * KV], F32)],
            [("d_high", [P, NF * D], F32R), ("b_high", [NR, 2 * FF], F32R)])
        (rope_c, rope_s), (ad_high,) = share(
            [("rope_c", [P, 2, NG, HD], F32), ("rope_s", [P, 2, NG, HD], F32)],
            [("ad_high", [P, NF * NR], F32R)])
        (a_raw,), (a_low,) = share([("a_raw", [P, 2 * KD * NR], F32)], [("a_low", [P, 2 * KD * NR], F32R)])
        (d_raw,), (d_low,) = share([("d_raw", [P, NF * D], F32)], [("d_low", [P, NF * D], F32R)])
        (bd_raw,), (bd_low,) = share([("bd_raw", [NR, D], F32)], [("bd_low", [NR, D], F32R)])
        bd_high = sb("bd_high", [NR, D], F32R)
        lower, upper = slice(0, FF // 2), slice(FF // 2, FF)
        WEIGHTS = {"a": (a_raw[:, :], a_high[:, :], a_low[:, :]), "b": (b_raw[:, :], b_high[:, :], b_low[:, :]),
                   "gu0": (gu_raw[:, :, lower], gu_high[:, :, lower], gu_low[:, :, lower]),
                   "gu1": (gu_raw[:, :, upper], gu_high[:, :, upper], gu_low[:, :, upper]),
                   "ad": (ad_raw[:, :], ad_high[:, :], ad_low[:, :]), "d": (d_raw[:, :], d_high[:, :], d_low[:, :]),
                   "bd": (bd_raw[:, :], bd_high[:, :], bd_low[:, :])}
        w_gu = [t[:, :, :].rearrange("p (g k) f -> p g k f", g=2) for t in (gu_high, gu_low)]
        w_b = [t[:, :].rearrange("p (g f) -> p g f", g=2) for t in (b_high, b_low)]
        w_ad = [t[:, :].rearrange("p (k n) -> p k n", k=NF) for t in (ad_high, ad_low)]
        w_a = [t[:, :].rearrange("p (g k n) -> p g k n", g=2, k=KD) for t in (a_high, a_low)]
        w_d = [t[:, :].rearrange("p (k d) -> p k d", k=NF) for t in (d_high, d_low)]
        w_bd = [t[:, :] for t in (bd_high, bd_low)]
        len_i = sb("len_i", [B, 1], I32)
        cond_i = sb("cond_i", [B, 1], I32)
        subj_i = sb("subj_i", [B, 1], I32)
        len_f = sb("len_f", [B, 1])
        subj_f = sb("subj_f", [B, 1])
        scale_qk = sb("scale_qk", [P, 2, HD])
        scale_sw = sb("scale_sw", [P, 2, HD])
        len_sel = sb("len_sel", [B, NG + NT + 1 + B])
        ad_sel = sb("ad_sel", [B, B])
        len_all = sb("len_all", [P, 80])
        adapt = sb("adapt", [NR, B])
        thresh = sb("thresh", [P, B + 2 * GB])
        xs = sb("xs", [P, NG, D])
        (x_t,), (h_high,) = share([("x_t", [P, KD, NG, P], F32)], [("h_high", [P, NF, PAIR_TOK], F32R)])
        pos = sb("pos", [P, NG])
        ssum = sb("ssum", [P, JOB_AT[-1] // HD])
        meansq = sb("meansq", [P, JOB_AT[-1] // HD])
        rms = sb("rms", [P, JOB_AT[-1] // HD])
        rstd = sb("rstd", [P, JOB_AT[-1] // HD])
        far_probs = sb("far_probs", [P, 2 * GB, 2 * P])
        new_kv = far_probs[:, :, :]
        q_t = sb("q_t", [P, NG, GS, P])
        slot_i = sb("slot_i", [BP, NT], I32)
        slot_f = sb("slot_f", [BP, NT])
        tidx = sb("tidx", [BP, NT], I32)
        blk_i = sb("blk_i", [BP, NT], I32)
        blk_f = sb("blk_f", [BP, NT])
        k_raw = early[0:BP, 0:BELEMS]
        v_raw = early[0:BP, BELEMS:2 * BELEMS]
        kv_blk = moved[0:BP, :].rearrange("p (o c) -> p o c", c=KV)
        wr_i = sb("wr_i", [BP, 1], I32)
        wr_off = sb("wr_off", [BP, 1])
        wr_d = sb("wr_d", [BP, BLOCK])
        wr_e = sb("wr_e", [BP, BLOCK])
        wr_f = sb("wr_f", [BP, BLOCK])
        (wr_diag, wr_all), (th0, th1, th2, gs0, gs1, lowd_high) = share(
            [("wr_diag", [BP, BLOCK, NW], F16), ("wr_all", [BP, BLOCK, NW], F16)],
            [(f"th{n}", [P, PAIR_TOK], F32) for n in range(3)]
            + [(f"gs{n}", [P, PAIR_TOK], F32) for n in range(2)] + [("lowd_high", [NR, PAIR_TOK], F32R)])
        wid_sel = sb("wid_sel", [BP, NT, BT * WS])
        wid_all = sb("wid_all", [BP, NW])
        same = sb("same", [BP, NW], F16)
        cand = wr_diag
        winner = sb("winner", [BP, NT * BLOCK])
        won = sb("won", [BP, NT * BLOCK])
        rows = sb("rows", [BP, NT * BLOCK])
        bits_i = sb("bits_i", [B, 4], I32)
        bits = sb("bits", [B, 4])
        row_b = sb("row_b", [B, SLOTS * BLOCK])
        row_d = sb("row_d", [B, SLOTS * BLOCK])
        far_i = sb("far_i", [P, B + GB], I32)
        near_i = sb("near_i", [P, NG + 1], I32)
        (mix_raw,), (h_low,) = share([("mix_raw", [B, 2, T * T], F32)], [("h_low", [P, NF, PAIR_TOK], F32R)])
        mix_w = sb("mix_w", [P, 2, NG, T])
        side_b = sb("side_b", [B, T])
        bias = sb("bias", [P, NG])
        R = range(2)
        idx = [sb(f"idx{r}", [P, GB + 1], I32) for r in R]
        far = [sb(f"far{r}", [P, GB, KV]) for r in R]
        near = [sb(f"near{r}", [P, KV]) for r in R]
        ((cos_first, q_rot_first, _, sq, cos_last, q_rot_last),
         (k_t0, mask0, prob0, k_t1, mask1, prob1, p_near0, p_near1)) = share(
            [("cos_first", [P, JOB_AT[2]], F32), ("q_rot_first", [P, 2, GS, G * HD], F32),
             ("place_between", [P, 512], F32),
             ("sq", [P, max(JOB_COLS)], F32), ("cos_last", [P, JOB_COLS[2]], F32),
             ("q_rot_last", [P, NG - 2, GS, G * HD], F32)],
            [(name, shape, F32) for r in R for name, shape in (
                (f"k_t{r}", [P, GB, SPAN]), (f"mask{r}", [P, GB, SPAN]), (f"prob{r}", [P, GB, 2, SPAN]))]
            + [(f"p_near{r}", [P, GB, 2 * P], F32) for r in R])
        cos_of = (cos_first[:, 0:JOB_AT[1]], cos_first[:, JOB_AT[1]:], cos_last[:, :])
        q_rot_of = (None, q_rot_first, q_rot_last)
        k_t, mask, prob, p_near = (k_t0, k_t1), (mask0, mask1), (prob0, prob1), (p_near0, p_near1)
        q_bd = [sb(f"q_bd{r}", [P, GB, 2, GS, T]) for r in R]
        prob_near = [sb(f"prob_near{r}", [P, 2, GB, T]) for r in R]
        top = [sb(f"top{r}", [P, GB * 2]) for r in R]
        ntop = [sb(f"ntop{r}", [P, GB * 2]) for r in R]
        den = [sb(f"den{r}", [P, GB * 2]) for r in R]
        rden = [sb(f"rden{r}", [P, GB * 2]) for r in R]
        p_far = [far_probs[:, GB * r:GB * (r + 1), :] for r in R]
        o_t = [sb(f"o_t{r}", [P, GS, GB, T]) for r in R]
        w_mix = [sb(f"w_mix{r}", [P, 2, GB, T]) for r in R]
        x1 = [sb(f"x1_{r}", [P, D]) for r in R]
        x2 = [sb(f"x2_{r}", [P, D]) for r in R]
        x3 = [sb(f"x3_{r}", [P, D]) for r in R]
        x3_t = sb("x3_t", [P, KD, 2, P])
        xf_high = sb("xf_high", [P, KD * PAIR_TOK], F32R)
        xf_low = sb("xf_low", [P, KD * PAIR_TOK], F32R)
        (low_raw,), (low_low,) = share([("low_raw", [NR, 2 * PAIR_TOK], F32)],
                                       [("low_low", [NR, 2 * PAIR_TOK], F32R)])
        low_high = sb("low_high", [NR, 2 * PAIR_TOK], F32R)
        (lowd_raw,), (lowd_low,) = share([("lowd_raw", [NR, PAIR_TOK], F32)], [("lowd_low", [NR, PAIR_TOK], F32R)])
        th, gs = (th0, th1, th2), (gs0, gs1)
        hf = [sb(f"hf{r}", [P, PAIR_TOK]) for r in R]
        m_xf = [t[:, :].rearrange("p (k t) -> p k t", k=KD) for t in (xf_high, xf_low)]
        m_low = [t[:, :].rearrange("p (g t) -> p g t", g=2) for t in (low_high, low_low)]
        m_h = [t[:, :, :] for t in (h_high, h_low)]
        m_lowd = [t[:, :] for t in (lowd_high, lowd_low)]
        bank = [ctx.enter_context(nc.psum_tensor(f"bank{n}", [P, 512], F32)) for n in range(8)]

        small_in = sem("small_in")
        k128_in = sem("k128_in")
        scale_in = sem("scale_in")
        x_in = sem("x_in")
        wvkq_in = sem("wvkq_in")
        wo_in = sem("wo_in")
        w_in = {name: sem(f"w_in_{name}") for name in ("a", "b", "gu", "d", "ad", "bd")}
        high_ready = sem("high_ready")
        split_ready = {name: sem(f"split_{name}") for name in SPLITS}
        mix_idx_in = sem("mix_idx_in")
        ones_set = sem("ones_set")
        sel_ready = sem("sel_ready")
        len_psum = sem("len_psum")
        tidx_ready = sem("tidx_ready")
        blk_in = sem("blk_in")
        k_in = sem("k_in")
        v_in = sem("v_in")
        k_moved = sem("k_moved")
        v_moved = sem("v_moved")
        blk_out = sem("blk_out")
        new_out = sem("new_out")
        xt_psum = sem("xt_psum")
        xt_ready = sem("xt_ready")
        w_psum = sem("w_psum")
        w_ready = sem("w_ready")
        arg_ready = sem("arg_ready")
        sin_ready = sem("sin_ready")
        rope_ready = sem("rope_ready")
        vk_psum = sem("vk_psum")
        vk_ready = sem("vk_ready")
        q_psum = sem("q_psum")
        q_ready = sem("q_ready")
        sq_ready = sem("sq_ready")
        ssum_ready = sem("ssum_ready")
        meansq_ready = sem("meansq_ready")
        rms_ready = sem("rms_ready")
        cos_ready = sem("cos_ready")
        job_done = sem("job_done")
        qt_psum = sem("qt_psum")
        qt_ready = sem("qt_ready")
        diag_ready = sem("diag_ready")
        wr_psum = sem("wr_psum")
        wr_ready = sem("wr_ready")
        widsel_ready = sem("widsel_ready")
        wid_psum = sem("wid_psum")
        rows_ready = sem("rows_ready")
        rows_out = sem("rows_out")
        rows_in = sem("rows_in")
        shift_ready = sem("shift_ready")
        place_psum = sem("place_psum")
        place_ready = sem("place_ready")
        mix_in = sem("mix_in")
        side_in = sem("side_in")
        mix_out = sem("mix_out")
        mix_back = sem("mix_back")
        vector_order = sem("vector_order")
        idx_ready = sem("idx_ready")
        kv_in = [sem(f"kv_in{r}") for r in R]
        qbd_ready = sem("qbd_ready")
        mask_ready = sem("mask_ready")
        wmix_ready = sem("wmix_ready")
        kt_psum = sem("kt_psum")
        far_kt_ready = sem("far_kt_ready")
        near_kt_ready = sem("near_kt_ready")
        scores_psum = sem("scores_psum")
        top_ready = sem("top_ready")
        ntop_ready = sem("ntop_ready")
        exp_ready = sem("exp_ready")
        rden_ready = sem("rden_ready")
        prob_ready = sem("prob_ready")
        pfar_psum = sem("pfar_psum")
        pnear_psum = sem("pnear_psum")
        pfar0_ready = sem("pfar0_ready")
        pfar1_ready = sem("pfar1_ready")
        pnear_ready = sem("pnear_ready")
        o_psum = sem("o_psum")
        o_ready = sem("o_ready")
        wo_psum = sem("wo_psum")
        x1_ready = sem("x1_ready")
        mix1_psum = sem("mix1_psum")
        x2_ready = sem("x2_ready")
        mix2_psum = sem("mix2_psum")
        x3_ready = sem("x3_ready")
        x3_kept = sem("x3_kept")
        x3t_psum = sem("x3t_psum")
        x3t_ready = sem("x3t_ready")
        xfhigh_ready = sem("xfhigh_ready")
        xf_ready = sem("xf_ready")
        lowraw_ready = sem("lowraw_ready")
        lowhigh_ready = sem("lowhigh_ready")
        low_psum = sem("low_psum")
        low_ready = sem("low_ready")
        gu_psum = sem("gu_psum")
        tanh_ready = sem("tanh_ready")
        gs_ready = sem("gs_ready")
        hf_ready = sem("hf_ready")
        hhigh_ready = sem("hhigh_ready")
        h_ready = sem("h_ready")
        lowd_psum = sem("lowd_psum")
        lowdraw_ready = sem("lowdraw_ready")
        lowdhigh_ready = sem("lowdhigh_ready")
        lowd_ready = sem("lowd_ready")
        down_psum = sem("down_psum")
        y_ready = sem("y_ready")
        y_out = sem("y_out")

        def xf_half(t, r):
            return t[:, :].rearrange("p (k t) -> p k t", k=KD)[:, :, r * P:(r + 1) * P]

        def over(ap, axis, n):
            ap = ap.unsqueeze(axis)
            shape = list(ap.shape)
            shape[axis] = n
            return ap.broadcast_to(shape)

        LOW_BANKS, HIGH_BANKS = bank[0:4], bank[4:8]
        FFN_BANKS = bank[4:8]
        SCORE = slice(0, 2 * SPAN)

        block = ctx.enter_context(nc.Block())

        def blocks_of(table, t0, t1):
            v = table.rearrange("(t b) (j o) -> (b j) t o", t=NT, o=BLOCK)[:, t0:t1, :]
            return v.rearrange("p t o -> p (t o)") if t1 - t0 == 1 else v

        def blocks_of_rows(t0, t1):
            v = rows[:, t0 * BLOCK:t1 * BLOCK]
            return v if t1 - t0 == 1 else v.rearrange("p (t o) -> p t o", o=BLOCK)

        @block.sync
        def _(sp):
            sp.dma_start(len_i[:, :], lens.rearrange("(b o) -> b o", o=1)).then_inc(small_in, 16)
            sp.dma_start(k32[:, :], c32).then_inc(small_in, 16)
            sp.dma_start(k96[:, :], c96).then_inc(small_in, 16)
            sp.dma_start(k128[:, :], c128).then_inc(k128_in, 16)
            sp.dma_start(xs[:, :, :], x.rearrange("(g s) t d -> (s t) g d", s=GB)).then_inc(x_in, 16)
            sp.dma_start(wv_raw[:, :], Wv).then_inc(wvkq_in, 16)
            sp.dma_start(wk_raw[:, :], Wk).then_inc(wvkq_in, 16)
            sp.dma_start(wq_raw[:, :, :], Wq.rearrange("(a p) d -> p a d", p=P)).then_inc(wvkq_in, 16)
            for a in range(2):
                for h in range(GS):
                    sp.dma_start(wo_raw[:, a, h, :].rearrange("p (g d) -> p g d", g=G),
                                 Wo[a * P:(a + 1) * P, :].rearrange("p (g h d) -> p g h d", g=G, h=GS)[:, :, h, :]
                                 ).then_inc(wo_in, 16)
            def new_rows():
                sp.wait_ge(vk_ready, NPAIR)
                sp.wait_ge(job_done, 1)
                sp.dma_start(kv_rows[TILE_ROWS:TILE_ROWS + NEW_ROWS, :].rearrange("(g p) c -> p g c", p=P),
                             new_kv[:, :, :]).then_inc(new_out, 16)

            def block_rows(t):
                sp.wait_ge(k_moved, t + 1)
                sp.wait_ge(v_moved, t + 1)
                lo = t * TILE_ROWS + (NEW_ROWS if t else 0)
                sp.dma_start(kv_rows[lo:lo + TILE_ROWS, :].rearrange("(p o) c -> p (o c)", o=BLOCK),
                             kv_blk[:, :, :].rearrange("p o c -> p (o c)")).then_inc(blk_out, 16)

            def rows_out_to_table(t0, t1):
                sp.wait_ge(rows_ready, 1 if t0 == 0 else 2)
                sp.dma_start(blocks_of(row_table, t0, t1), blocks_of_rows(t0, t1)).then_inc(rows_out, 16)

            def rows_back(t1):
                sp.wait_ge(rows_out, 16 if t1 == 1 else 32)
                sp.dma_start(row_b[0:t1 * BT, :], row_table[0:t1 * BT, :]).then_inc(rows_in, 16)

            block_rows(0)
            rows_out_to_table(0, 1)
            rows_back(1)
            new_rows()
            sp.wait_ge(kv_in[0], 16 * (GB + 1))
            block_rows(1)
            sp.wait_ge(kv_in[1], 16 * (GB + 1))
            for a, src in enumerate((Ag, Au)):
                for k in range(KD):
                    at = (a * KD + k) * NR
                    sp.dma_start(a_raw[:, at:at + NR].rearrange("p (n r) -> p n r", r=RANK),
                                 src[:, k * P:(k + 1) * P, :].rearrange("n p r -> p n r")).then_inc(w_in["a"], 16)
            block_rows(2)
            sp.wait_ge(job_done, len(JOBS))
            sp.wait_ge(q_ready, NT)
            for a, src in enumerate((Bg, Bu)):
                sp.dma_start(b_raw[:, a * FF:(a + 1) * FF], src.rearrange("n r f -> (n r) f")).then_inc(w_in["b"], 16)
            for a, src in enumerate((Wg, Wu)):
                sp.dma_start(gu_raw[:, a * KD:(a + 1) * KD, :], src.rearrange("(k p) f -> p k f", p=P)
                             ).then_inc(w_in["gu"], 16)
            block_rows(3)
            rows_out_to_table(1, NT)
            sp.dma_start(d_raw[:, :].rearrange("p (k d) -> p k d", k=NF), Wd.rearrange("(k p) f -> p k f", p=P)
                         ).then_inc(w_in["d"], 16)
            rows_back(NT)
            for k in range(NF):
                sp.dma_start(ad_raw[:, k * NR:(k + 1) * NR].rearrange("p (n r) -> p n r", r=RANK),
                             Ad[:, k * P:(k + 1) * P, :].rearrange("n p r -> p n r")).then_inc(w_in["ad"], 16)
            sp.dma_start(bd_raw[:, :], Bd.rearrange("n r f -> (n r) f")).then_inc(w_in["bd"], 16)

            def store(m):
                for r in R:
                    sp.wait_ge(y_ready, 2 * m + r + 1)
                    sp.dma_start(out[bass.ds(m * 2 * GB + GB * r, GB), :, :].rearrange("s t d -> (s t) d"),
                                 xs[:, bass.ds(2 * m + r, 1), :].rearrange("p a d -> p (a d)")).then_inc(y_out, 16)

            with sp.Fori(0, NPAIR) as m:
                store(m)
            sp.wait_ge(y_out, 16 * NG)

        SPLIT_AT = {name: n + 1 for n, name in enumerate(SPLITS)}
        LOADS = {"a": 2 * KD, "b": 2, "gu0": 2, "gu1": 2, "ad": NF, "d": 1, "bd": 1}

        def take_low(eng, name):
            eng.wait_ge(high_ready, SPLIT_AT[name])
            raw, high, low = WEIGHTS[name]
            eng.tensor_tensor(low, raw, high.bitcast(F32), ALU.subtract).then_inc(split_ready[name], 1)

        @block.gpsimd
        def _(pool):
            pool.memset(ones[:, :], 1.0).then_inc(ones_set, 1)
            pool.memset(ones16[:, :], 1.0).then_inc(ones_set, 1)
            pool.wait_ge(tidx_ready, 1)
            for t in range(NT):
                pool.indirect_dma_start(
                    blk_i[:, t:t + 1], None, table.rearrange("b (n o) -> (b n) o", o=1),
                    bass.IndirectOffsetOnAxis(ap=tidx[:, t:t + 1], axis=0)).then_inc(blk_in, 16)
            pool.wait_ge(blk_in, 16 * NT)

            def load_blocks(t):
                for dst, src, seen, done in ((k_raw, kb, k_moved, k_in), (v_raw, vb, v_moved, v_in)):
                    if t:
                        pool.wait_ge(seen, t)
                    pool.indirect_dma_start(dst[:, :], None, src.rearrange("n g o d -> n (g o d)"),
                                            bass.IndirectOffsetOnAxis(ap=blk_i[:, t:t + 1], axis=0)).then_inc(done, 16)

            def cos_part(j):
                kind, g, ng = JOBS[j]
                n, nh, src = (0, G, k_in_f) if kind == "k" else (1, H, q_in_f)
                pool.wait_ge(rope_ready, 1)
                pool.wait_ge(vk_ready if kind == "k" else q_ready, (g + ng) // 2)
                pool.tensor_tensor(cos_of[j].rearrange("p (t h d) -> p t h d", t=ng, d=HD),
                                   src[:, g:g + ng, :].rearrange("p t (h d) -> p t h d", d=HD),
                                   over(rope_c[:, n, g:g + ng, :], 2, nh), ALU.mult).then_inc(cos_ready, 1)

            load_blocks(0)
            pool.wait_ge(mix_idx_in, 32)
            for n, (w, i) in enumerate(((w1, cond_i), (w2, subj_i))):
                pool.indirect_dma_start(mix_raw[:, n, :], None, w.rearrange("n c d -> n (c d)"),
                                        bass.IndirectOffsetOnAxis(ap=i[:, :], axis=0)).then_inc(mix_in, 16)
            pool.indirect_dma_start(side_b[:, :], None, side,
                                    bass.IndirectOffsetOnAxis(ap=subj_i[:, :], axis=0)).then_inc(side_in, 16)
            for j in range(len(JOBS)):
                cos_part(j)
            pool.wait_ge(rows_in, 16)
            load_blocks(1)

            def prepare(n, r, pair):
                table_rows = kv_rows if pair is not None else kv_rows[0:TILE_ROWS + NEW_ROWS, :]
                if pair is not None:
                    pool.wait_ge(kv_in[r], pair * (GB + 1) * 16)
                pool.tensor_copy(idx[r][:, 0:GB], far_i[:, bass.ds(GB * n, GB)]).then_inc(idx_ready, 1)
                pool.tensor_copy(idx[r][:, GB:GB + 1], near_i[:, bass.ds(n, 1)]).then_inc(idx_ready, 1)
                pool.wait_ge(idx_ready, 2 * n + 2)
                if pair is not None:
                    pool.wait_ge(o_psum, n - 1)
                pool.nop(nofuse=True)
                for s in range(GB):
                    pool.indirect_dma_start(far[r][:, s, :], None, table_rows,
                                            bass.IndirectOffsetOnAxis(ap=idx[r][:, s:s + 1], axis=0)
                                            ).then_inc(kv_in[r], 16)
                pool.indirect_dma_start(near[r][:, :], None, table_rows,
                                        bass.IndirectOffsetOnAxis(ap=idx[r][:, GB:GB + 1], axis=0)
                                        ).then_inc(kv_in[r], 16)

            def spread_q(n, r):
                for h in range(GS):
                    src = q_t[:, bass.ds(n, 1), h, :].rearrange("p a (s t) -> p (a s) t", s=GB)
                    pool.tensor_tensor(q_bd[r][:, :, :, h, :], over(src, 2, 2),
                                       over(over(c1("pair"), 1, GB), 3, T), ALU.mult).then_inc(qbd_ready, 1)

            def spread_w(n, r):
                for w in range(2):
                    src = mix_w[:, w, bass.ds(n, 1), :].rearrange("p a d -> p (a d)")
                    pool.tensor_tensor(w_mix[r][:, w, :, :], over(src, 1, GB), over(c1("sample"), 2, T),
                                       ALU.mult).then_inc(wmix_ready, 1)

            def normalise(n, r):
                for half in range(2):
                    pool.wait_ge(rden_ready, 2 * n + half + 1)
                    s = slice(2 * half, 2 * half + 2)
                    v = prob[r][:, s, :, 0:P].rearrange("p s c i -> p (s c) i")
                    scale = rden[r][:, 4 * half:4 * half + 4]
                    pool.tensor_tensor(v, v, over(scale, 2, P), ALU.mult).then_inc(prob_ready, 1)
                    pool.tensor_tensor(prob_near[r][:, :, s, :].rearrange("p c s i -> p s c i"),
                                       prob[r][:, s, :, P:SPAN],
                                       over(scale.rearrange("p (s c) -> p s c", c=2), 3, T),
                                       ALU.mult).then_inc(prob_ready, 1)

            def keep(n, r):
                pool.wait_ge(x3_ready, n + 1)
                pool.tensor_copy(xs[:, bass.ds(n, 1), :].rearrange("p a d -> p (a d)"), x3[r][:, :]).then_inc(x3_kept, 1)

            pool.wait_ge(place_ready, 3)
            pool.wait_ge(blk_out, 16)
            pool.wait_ge(new_out, 16)
            for r in R:
                prepare(r, r, None)
                pool.wait_ge(qt_ready, 1)
                spread_q(r, r)
            load_blocks(2)

            def pair_steps(order, m):
                for step in order:
                    if step[0] == "load":
                        load_blocks(step[1])
                    elif step[0] == "split" and SPLITS[step[1]] == "pool":
                        take_low(pool, step[1])
                    elif step[0] == "place":
                        pool.wait_ge(place_ready, 5)
                        pool.wait_ge(blk_out, 16 * NT)
                        pool.wait_ge(qt_ready, NT)
                    elif step[0] == "fetch":
                        prepare(2 * m + 3, 1, m + 1)
                    elif step[0] == "ahead":
                        prepare(2 * m + 4, 0, m + 2)
                    elif step[0] == "spread":
                        spread_q(2 * m + 2 + step[1], step[1])
                        spread_w(2 * m + 2 + step[1], step[1])
                    elif step[0] == "den":
                        normalise(2 * m + 2 + step[1], step[1])
                    elif step[0] == "mix2":
                        keep(2 * m + 2 + step[1], step[1])

            pool.wait_ge(mix_back, 32)
            for r in R:
                spread_w(r, r)
            pair_steps(START_ORDER, -1)
            pair_steps(FIRST_ORDER, 0)
            with pool.Fori(1, NPAIR - 1) as m:
                pair_steps(LOOP_ORDER, m)
            pool.wait_ge(kv_in[0], (NPAIR + 1) * (GB + 1) * 16)

        @block.scalar
        def _(act):
            act.dma_start(cond_i[:, :], cond.rearrange("(b o) -> b o", o=1)).then_inc(mix_idx_in, 16)
            act.dma_start(subj_i[:, :], subj.rearrange("(b o) -> b o", o=1)).then_inc(mix_idx_in, 16)
            for n, s in enumerate((ks, qs)):
                act.dma_start(scale_qk[:, n, :], s.partition_broadcast(P)).then_inc(scale_in, 16)
            for n in range(2):
                act.wait_ge(xt_psum, 2 * n + 1)
                act.copy(x_t[:, n, 0:4, :].rearrange("p g t -> p (g t)"), bank[1 + 2 * n][:, :]).then_inc(xt_ready, 1)
            act.wait_ge(w_psum, 1)
            act.copy(w_vkq[:, :, 0:KV], bank[5][:, :].rearrange("p (k c) -> p k c", k=KD)).then_inc(w_ready, 1)
            act.wait_ge(arg_ready, 1)
            act.activation(sincos[:, :, :, :].rearrange("p a g f -> p (a g f)"),
                           rest[:, :, :, :].rearrange("p a g f -> p (a g f)"), ACT.Sin).then_inc(sin_ready, 1)

            def square(j):
                kind, g, ng = JOBS[j]
                src = k_in_f if kind == "k" else q_in_f
                act.wait_ge(vk_ready if kind == "k" else q_ready, (g + ng) // 2)
                if j == 2:
                    act.wait_ge(ssum_ready, 2)
                act.activation(sq[:, SQ_AT[j]:SQ_AT[j] + JOB_COLS[j]],
                               src[:, g:g + ng, :].rearrange("p t c -> p (t c)"), ACT.Square).then_inc(sq_ready, 1)

            def root(j):
                act.wait_ge(meansq_ready, j + 1)
                c = slice(JOB_AT[j] // HD, JOB_AT[j + 1] // HD)
                act.activation(rms[:, c], meansq[:, c], ACT.Sqrt).then_inc(rms_ready, 1)

            def take_q(i):
                act.wait_ge(q_psum, i + 1)
                act.copy(q_in_f[:, 2 * i:2 * i + 2, :].rearrange("p t c -> p (t c)"), bank[(5, 6, 1, 2)[i]][:, :]
                         ).then_inc(q_ready, 1)

            def move_k(t):
                act.wait_ge(k_in, 16 * (t + 1))
                if t:
                    act.wait_ge(blk_out, 16 * t)
                else:
                    act.wait_ge(rope_ready, 1)
                act.copy(kv_blk[:, :, 0:G * HD].rearrange("p o (g d) -> p o g d", d=HD),
                         k_raw[:, :].rearrange("p (g o d) -> p o g d", g=G, d=HD)).then_inc(k_moved, 1)

            def take_qt(i):
                act.wait_ge(qt_psum, i + 1)
                act.copy(q_t[:, 2 * i:2 * i + 2, :, :].rearrange("p g h t -> p (g h t)"), bank[3 + i][:, :]
                         ).then_inc(qt_ready, 1)

            def take_vk(i):
                act.wait_ge(vk_psum, i + 1)
                src = bank[1 + i][:, :].rearrange("p (t c) -> p t c", t=2)
                act.copy(new_kv[:, 2 * i:2 * i + 2, G * HD:KV], src[:, :, 0:G * HD])
                act.copy(k_in_f[:, 2 * i:2 * i + 2, :], src[:, :, G * HD:KV]).then_inc(vk_ready, 1)

            take_vk(0)
            take_vk(1)
            act.wait_ge(wr_psum, 1)
            for n in range(3):
                act.copy(wr_all[:, :, :].rearrange("p o w -> p (o w)")[:, 512 * n:512 * (n + 1)],
                         bank[5 + n][0:BP, :]).then_inc(wr_ready, 1)
            take_vk(2)
            take_vk(3)
            move_k(0)
            square(0)
            for i in range(4):
                take_q(i)
            square(1)
            root(0)
            root(1)
            act.wait_ge(mix_in, 32)
            for n in range(2):
                act.dma_start(mix_rows[n, :, :], mix_raw[:, n, :]).then_inc(mix_out, 16)
            square(2)
            take_qt(0)
            act.wait_ge(mix_out, 32)
            for n in range(2):
                act.dma_start(mix_w[:, n, :, :],
                              mix_rows[n, :, :].rearrange("(g s) (c d) -> (s c) g d", s=GB, d=T)).then_inc(mix_back, 16)
            move_k(1)
            root(2)

            def attention(stage, n, r, b, pair):
                first = isinstance(pair, int) and pair == 0
                if stage == "kt":
                    act.wait_ge(kt_psum, n + 1)
                    act.copy(k_t[r][:, :, 0:P], b[0][:, :].rearrange("p (s i) -> p s i", s=GB)).then_inc(far_kt_ready, 1)
                elif stage == "scores":
                    for half in range(2):
                        act.wait_ge(ntop_ready, 2 * n + half + 1)
                        for j in range(4 * half, 4 * half + 4):
                            v = prob[r][:, j // 2, j % 2, :]
                            last = act.activation(v, v, ACT.Exp, bias=ntop[r][:, j:j + 1], scale=SCALE,
                                                  accum_out=den[r][:, j:j + 1])
                        last.then_inc(exp_ready, 1)
                elif stage == "pt0":
                    act.wait_ge(pfar_psum, 2 * n + 1)
                    act.copy(p_far[r][:, 0:2, :].rearrange("p s c -> p (s c)"), b[2][:, :]).then_inc(pfar0_ready, 1)
                elif stage == "pv":
                    act.wait_ge(o_psum, n + 1)
                    act.copy(o_t[r][:, :, :, :].rearrange("p h s t -> p s h t"),
                             b[1][:, 0:2 * P].rearrange("p (s h t) -> p s h t", s=GB, h=GS)).then_inc(o_ready, 1)
                elif stage == "xt":
                    act.wait_ge(x3t_psum, n + 1)
                    if not first:
                        act.wait_ge(xf_ready, n - 1)
                    act.copy(x3_t[:, :, r, :], b[0][:, 0:2 * P].rearrange("p (k t) -> p k t", k=KD)
                             ).then_inc(x3t_ready, 1)
                elif stage == "xf":
                    act.wait_ge(x3t_ready, n + 1)
                    act.copy(xf_half(xf_high, r), x3_t[:, :, r, :]).then_inc(xfhigh_ready, 1)

            def take_high(name):
                act.wait_ge(w_in[name[0:2] if name in ("gu0", "gu1") else name], 16 * LOADS[name])
                if name in ("gu0", "gu1"):
                    act.wait_ge(v_moved, NT)
                    act.wait_ge(k_moved, NT)
                if name in ("b", "d"):
                    act.wait_ge(blk_out, 16 * NT)
                act.copy(WEIGHTS[name][1], WEIGHTS[name][0]).then_inc(high_ready, 1)

            def h_high_part(m, f):
                act.wait_ge(hf_ready, NF * m + f + 1)
                act.copy(h_high[:, f, :], hf[f % 2][:, :]).then_inc(hhigh_ready, 1)

            def ffn(piece, m):
                if piece == "adapt":
                    act.wait_ge(lowraw_ready, m + 1)
                    act.copy(low_high[:, :], low_raw[:, :]).then_inc(lowhigh_ready, 1)
                if piece.startswith("up"):
                    f = int(piece[2:])
                    act.wait_ge(gu_psum, NF * m + f + 1)
                    act.activation(th[f % 3][:, :], FFN_BANKS[f % 3][:, 0:PAIR_TOK], ACT.Tanh,
                                   scale=0.5).then_inc(tanh_ready, 1)
                    if f:
                        h_high_part(m, f - 1)
                elif piece == "down00":
                    h_high_part(m, NF - 1)
                elif piece == "down_lora1":
                    act.wait_ge(lowdraw_ready, m + 1)
                    act.copy(lowd_high[:, :], lowd_raw[:, :]).then_inc(lowdhigh_ready, 1)

            def steps(order, m, pair):
                first_pair = order is START_ORDER
                for step in order:
                    if isinstance(step, str):
                        ffn(step, m)
                    elif step[0] == "split":
                        take_high(step[1])
                    elif step == ("normalise", 2):
                        for i in range(1, NPAIR):
                            take_qt(i)
                    elif step[0] == "move_k":
                        move_k(step[1])
                    elif step[0] in STAGES:
                        stage, r = step
                        attention(stage, 2 * m + 2 + r, r, HIGH_BANKS if first_pair and r else LOW_BANKS, pair)

            steps(START_ORDER, -1, 0)
            steps(FIRST_ORDER, 0, 1)
            with act.Fori(1, NPAIR - 1) as m:
                steps(LOOP_ORDER, m, m + 1)
            for piece in FFN_PIECES:
                ffn(piece, NPAIR - 1)

        @block.vector
        def _(dve):
            count = [0]

            def then(ins):
                count[0] += 1
                ins.then_inc(vector_order, 1)
                dve.wait_ge(vector_order, count[0])

            dve.wait_ge(small_in, 48)
            then(dve.tensor_copy(len_f[:, :], len_i[:, :]))
            then(dve.tensor_scalar(len_sel[:, :], c3("of_len"), len_f[:, 0:1], None, ALU.mult))
            dve.wait_ge(mix_idx_in, 32)
            then(dve.tensor_copy(subj_f[:, :], subj_i[:, :]))
            dve.tensor_scalar(ad_sel[:, :], c3("of_len")[:, NG + NT + 1:], subj_f[:, 0:1], None,
                              ALU.mult).then_inc(sel_ready, 1)
            dve.wait_ge(len_psum, 1)
            then(dve.tensor_copy(len_all[:, 0:NG], bank[0][:, 0:NG]))
            then(dve.tensor_copy(len_all[0:BP, NG:NG + NT + 1], bank[0][0:BP, NG:NG + NT + 1]))
            then(dve.tensor_copy(len_all[:, 16:80], bank[0][:, 16:80]))
            then(dve.tensor_copy(slot_i[:, :], len_all[0:BP, NG:NG + NT]))
            then(dve.tensor_scalar(slot_i[:, :], slot_i[:, :], 4, None, ALU.logical_shift_right))
            then(dve.tensor_scalar(slot_f[:, :], slot_i[:, :], c9("slot"), 0.0, ALU.add, ALU.max))
            dve.scalar_tensor_tensor(tidx[:, :], slot_f[:, :], float(NBLK - 1), c9("table"), ALU.min,
                                     ALU.add).then_inc(tidx_ready, 1)
            dve.wait_ge(k128_in, 16)
            then(dve.tensor_scalar(pos[:, :], len_all[:, 0:NG], c1("tok"), None, ALU.add))
            then(dve.tensor_tensor(angle[:, :, :], over(pos[:, :], 2, HALF), over(c1("freq"), 1, NG), ALU.mult))
            flat = angle[:, :, :].rearrange("p g f -> p (g f)")
            t2 = turn[:, :, :, :].rearrange("p a g f -> p a (g f)")
            r2 = rest[:, :, :, :].rearrange("p a g f -> p a (g f)")
            then(dve.tensor_scalar(t2[:, 0, :], flat, 1.0 / TWO_PI, None, ALU.mult))
            then(dve.tensor_scalar(t2[:, 1, :], flat, 1.0 / TWO_PI, 0.25, ALU.mult, ALU.add))
            then(dve.tensor_scalar(t2, t2, MAGIC, None, ALU.add))
            then(dve.tensor_scalar(t2, t2, -MAGIC, None, ALU.add))
            then(dve.scalar_tensor_tensor(r2, t2, -PI_PARTS[0], over(flat, 1, 2), ALU.mult, ALU.add))
            then(dve.scalar_tensor_tensor(r2, t2, -PI_PARTS[1], r2, ALU.mult, ALU.add))
            then(dve.scalar_tensor_tensor(r2, t2, -PI_PARTS[2], r2, ALU.mult, ALU.add))
            then(dve.tensor_scalar(r2[:, 1, :], r2[:, 1, :], float(np.pi / 2), None, ALU.add))
            dve.tensor_scalar(r2, r2, 3.1415925, -3.1415925, ALU.min, ALU.max).then_inc(arg_ready, 1)
            for n in range(2):
                dve.wait_ge(xt_psum, 2 * n + 2)
                dve.tensor_copy(x_t[:, n, 4:8, :].rearrange("p g t -> p (g t)"), bank[2 + 2 * n][:, :]
                                ).then_inc(xt_ready, 1)
            dve.wait_ge(w_psum, 2)
            dve.tensor_copy(w_vkq[:, :, KV:], bank[6][:, :].rearrange("p (k c) -> p k c", k=KD)).then_inc(w_ready, 1)
            def writers():
                then(dve.tensor_copy(wr_i[:, :], len_all[0:BP, NG + NT:NG + NT + 1]))
                then(dve.tensor_scalar(wr_i[:, :], wr_i[:, :], BLOCK - 1, None, ALU.bitwise_and))
                then(dve.tensor_copy(wr_off[:, :], wr_i[:, :]))
                then(dve.tensor_tensor(wr_off[:, :], c9("wslot"), wr_off[:, :], ALU.subtract))
                then(dve.tensor_scalar(wr_d[:, :], c9("off"), wr_off[:, 0:1], None, ALU.add))
                then(dve.tensor_scalar(wr_e[:, :], wr_d[:, :], c9("wrow"), None, ALU.add))
                then(dve.scalar_tensor_tensor(wr_f[:, :], wr_d[:, :], 0.0, wr_e[:, :], ALU.is_ge, ALU.mult))
                then(dve.scalar_tensor_tensor(wr_e[:, :], wr_d[:, :], float(T - 1), wr_f[:, :], ALU.is_le, ALU.mult))
                dve.tensor_tensor(wr_diag[:, :, :], over(ident[0:BP, 0:NW], 1, BLOCK), over(wr_e[:, :], 2, NW),
                                  ALU.mult).then_inc(diag_ready, 1)

            def writer_blocks():
                dve.wait_ge(blk_in, 16 * NT)
                then(dve.tensor_copy(blk_f[:, :], blk_i[:, :]))
                dve.tensor_tensor(wid_sel[:, :, :], over(c9("writer"), 1, NT), over(blk_f[:, :], 2, BT * WS),
                                  ALU.mult).then_inc(widsel_ready, 1)

            def take_w_o():
                dve.wait_ge(w_psum, 3)
                dve.tensor_copy(w_o[:, :, :].rearrange("p h d -> p (h d)"), bank[7][:, :]).then_inc(w_ready, 1)

            def small_tables():
                then(dve.tensor_scalar(thresh[:, 0:B], len_all[:, 16:16 + B], -BIG, BIG * WINDOW, ALU.mult, ALU.add))
                then(dve.tensor_scalar(thresh[:, B:], len_all[:, 16:16 + 2 * GB], -BIG, BIG * WINDOW, ALU.mult,
                                       ALU.add))
                then(dve.tensor_scalar(adapt[:, :], len_all[:, 48:48 + B], c1("adapter"), None, ALU.is_equal))

            def length_bits():
                for k in range(4):
                    then(dve.tensor_scalar(bits_i[:, k:k + 1], len_i[:, :], k, 1, ALU.logical_shift_right,
                                           ALU.bitwise_and))
                then(dve.tensor_copy(bits[:, :], bits_i[:, :]))

            def move_v(t):
                dve.wait_ge(v_in, 16 * (t + 1))
                if t:
                    dve.wait_ge(blk_out, 16 * t)
                dve.tensor_copy(kv_blk[:, :, G * HD:KV].rearrange("p o (g d) -> p o g d", d=HD),
                                v_raw[:, :].rearrange("p (g o d) -> p o g d", g=G, d=HD)).then_inc(v_moved, 1)

            def mean_square(j):
                c = slice(JOB_AT[j] // HD, JOB_AT[j + 1] // HD)
                dve.wait_ge(sq_ready, j + 1)
                dve.tensor_reduce(ssum[:, c], sq[:, SQ_AT[j]:SQ_AT[j] + JOB_COLS[j]].rearrange("p (a d) -> p a d", d=HD),
                                  AX.X, ALU.add).then_inc(ssum_ready, 1)
                dve.wait_ge(ssum_ready, j + 1)
                dve.tensor_scalar(meansq[:, c], ssum[:, c], 1.0 / HD, EPS, ALU.mult, ALU.add).then_inc(meansq_ready, 1)

            def rotate(j):
                kind, g, ng = JOBS[j]
                n, nh, src = (0, G, k_in_f) if kind == "k" else (1, H, q_in_f)
                cols = JOB_COLS[j]
                dve.wait_ge(vk_ready if kind == "k" else q_ready, (g + ng) // 2)
                x4 = src[:, g:g + ng, :].rearrange("p t (h d) -> p t h d", d=HD)
                s4 = sin_x[:, 0:cols].rearrange("p (t h d) -> p t h d", t=ng, d=HD)
                for a in range(2):
                    mine, other = slice(a * HALF, (a + 1) * HALF), slice((1 - a) * HALF, (2 - a) * HALF)
                    then(dve.tensor_tensor(s4[:, :, :, mine], x4[:, :, :, other],
                                           over(rope_s[:, n, g:g + ng, mine], 2, nh), ALU.mult))

            def normalise(j):
                kind, g, ng = JOBS[j]
                cols = JOB_COLS[j]
                c = slice(JOB_AT[j] // HD, JOB_AT[j + 1] // HD)
                s4 = sin_x[:, 0:cols].rearrange("p (t h d) -> p t h d", t=ng, d=HD)
                dve.wait_ge(cos_ready, j + 1)
                then(dve.tensor_tensor(sin_x[:, 0:cols], sin_x[:, 0:cols], cos_of[j], ALU.add))
                dve.wait_ge(rms_ready, j + 1)
                then(dve.reciprocal(rstd[:, c], rms[:, c]))
                r4 = rstd[:, c].rearrange("p (t h) -> p t h", t=ng)
                if kind == "k":
                    last = dve.tensor_tensor(new_kv[:, :, 0:G * HD].rearrange("p t (h d) -> p t h d", d=HD),
                                             s4, over(r4, 3, HD), ALU.mult)
                else:
                    for h in range(GS):
                        last = dve.tensor_tensor(q_rot_of[j][:, :, h, :].rearrange("p t (g d) -> p t g d", d=HD),
                                                 sin_x[:, 0:cols].rearrange("p (t g h d) -> p t g h d", t=ng, h=GS,
                                                                            d=HD)[:, :, :, h, :],
                                                 over(r4.rearrange("p t (g h) -> p t g h", h=GS)[:, :, :, h], 3, HD),
                                                 ALU.mult)
                last.then_inc(job_done, 1)
                dve.wait_ge(job_done, j + 1)

            def norm_rope(j):
                mean_square(j)
                rotate(j)
                normalise(j)

            def find_winners(t):
                then(dve.tensor_scalar(same[:, :], wid_all[:, :], blk_f[:, t:t + 1], None, ALU.is_equal))
                then(dve.tensor_tensor(cand[:, :, :], wr_all[:, :, :], over(same[:, :], 1, BLOCK), ALU.mult))
                then(dve.tensor_reduce(winner[:, t * BLOCK:(t + 1) * BLOCK], cand[:, :, :], AX.X, ALU.max))

            def number_rows(t0, t1):
                c = slice(t0 * BLOCK, t1 * BLOCK)
                own = c9("own")[:, c]
                then(dve.tensor_scalar(won[:, c], winner[:, c], 0.0, None, ALU.is_gt))
                then(dve.scalar_tensor_tensor(winner[:, c], winner[:, c], float(TILE_ROWS - 1), own, ALU.add,
                                              ALU.subtract))
                then(dve.tensor_tensor(winner[:, c], winner[:, c], won[:, c], ALU.mult))
                dve.tensor_tensor(rows[:, c], winner[:, c], own, ALU.add).then_inc(rows_ready, 1)

            def shift_rows(ns):
                width = SLOTS * BLOCK
                for k in (3, 2, 1, 0):
                    width -= 1 << k
                    then(dve.tensor_tensor(row_d[0:ns, 0:width], row_b[0:ns, 1 << k:width + (1 << k)],
                                           row_b[0:ns, 0:width], ALU.subtract))
                    last = dve.scalar_tensor_tensor(row_b[0:ns, 0:width], row_d[0:ns, 0:width], bits[0:ns, k:k + 1],
                                                    row_b[0:ns, 0:width], ALU.mult, ALU.add)
                    if k:
                        then(last)
                last.then_inc(shift_ready, 1)

            writers()
            dve.wait_ge(scale_in, 32)
            then(dve.tensor_scalar(scale_qk[:, :, :], scale_qk[:, :, :], 1.0, None, ALU.add))
            then(dve.tensor_scalar(scale_sw[:, :, 0:HALF], scale_qk[:, :, HALF:HD], -1.0, None, ALU.mult))
            then(dve.tensor_copy(scale_sw[:, :, HALF:HD], scale_qk[:, :, 0:HALF]))
            dve.wait_ge(sin_ready, 1)
            for n in range(2):
                for dst, trig, s in ((rope_c, 1, scale_qk), (rope_s, 0, scale_sw)):
                    last = dve.tensor_tensor(dst[:, n, :, :].rearrange("p g (a f) -> p g a f", a=2),
                                             over(sincos[:, trig, :, :], 2, 2),
                                             over(s[:, n, :].rearrange("p (a f) -> p a f", a=2), 1, NG), ALU.mult)
                    if (n, trig) != (1, 0):
                        then(last)
            last.then_inc(rope_ready, 1)
            writer_blocks()
            length_bits()
            dve.wait_ge(wid_psum, 1)
            then(dve.tensor_copy(wid_all[:, :], bank[0][0:BP, 0:NW]))
            move_v(0)
            dve.wait_ge(wr_ready, 3)
            find_winners(0)
            number_rows(0, 1)
            norm_rope(0)
            dve.wait_ge(rows_in, 16)
            shift_rows(BT)
            dve.wait_ge(place_psum, 1)
            dve.tensor_copy(far_i[:, 0:BT], bank[0][:, 0:BT]).then_inc(place_ready, 1)
            dve.tensor_copy(near_i[:, 0:2], bank[0][:, B:B + 2]).then_inc(place_ready, 1)
            dve.tensor_copy(bias[:, :], bank[0][:, B + NG:B + 2 * NG]).then_inc(place_ready, 1)
            norm_rope(1)
            take_w_o()
            small_tables()
            move_v(1)
            mean_square(2)

            def row(ap, n):
                return ap[:, bass.ds(n, 1), :].rearrange("p a d -> p (a d)")

            def make_mask(n, r):
                for s in range(GB):
                    last = dve.scalar_tensor_tensor(mask[r][:, s, :], c1("posbig"), thresh[:, bass.ds(GB * n + s, 1)],
                                                    c1("hide"), ALU.subtract, ALU.min)
                last.then_inc(mask_ready, 1)

            def attention(stage, n, r, b, pair):
                first = isinstance(pair, int) and pair == 0
                if stage == "kt":
                    dve.wait_ge(kt_psum, n + 1)
                    dve.tensor_copy(k_t[r][:, :, P:SPAN], b[1][:, 0:P].rearrange("p (s i) -> p s i", s=GB)
                                    ).then_inc(near_kt_ready, 1)
                elif stage == "scores":
                    dve.wait_ge(mask_ready, n + 1)
                    for half in range(2):
                        dve.wait_ge(scores_psum, 2 * n + half + 1)
                        dve.nop(nofuse=True)
                        for j in range(4 * half, 4 * half + 4):
                            s = (j // 2) % 2
                            last = dve.tensor_tensor_reduce(
                                prob[r][:, j // 2, j % 2, :], b[(2, 0)[half] + j % 2][:, s * SPAN:(s + 1) * SPAN],
                                mask[r][:, j // 2, :], 1.0, -3.0e38, ALU.add, ALU.max, top[r][:, j:j + 1])
                        last.then_inc(top_ready, 1)
                        dve.wait_ge(top_ready, 2 * n + half + 1)
                        q = slice(4 * half, 4 * half + 4)
                        dve.tensor_scalar(ntop[r][:, q], top[r][:, q], -SCALE, None, ALU.mult).then_inc(ntop_ready, 1)
                elif stage == "den":
                    for half in range(2):
                        dve.wait_ge(exp_ready, 2 * n + half + 1)
                        q = slice(4 * half, 4 * half + 4)
                        dve.reciprocal(rden[r][:, q], den[r][:, q]).then_inc(rden_ready, 1)
                elif stage == "pt1":
                    dve.wait_ge(pfar_psum, 2 * n + 2)
                    dve.tensor_copy(p_far[r][:, 2:4, :].rearrange("p s c -> p (s c)"), b[3][:, :]
                                    ).then_inc(pfar1_ready, 1)
                    dve.wait_ge(pnear_psum, n + 1)
                    dve.tensor_tensor(p_near[r][:, :, :], over(b[0][:, 0:2 * P], 1, GB),
                                      over(c1("sample"), 2, 2 * P), ALU.mult).then_inc(pnear_ready, 1)
                elif stage == "wo":
                    dve.wait_ge(wo_psum, n + 1)
                    dve.tensor_tensor(x1[r][:, :], b[0][:, 0:D], row(xs, n), ALU.add).then_inc(x1_ready, 1)
                elif stage == "mix1":
                    dve.wait_ge(mix1_psum, n + 1)
                    dve.tensor_tensor(x2[r][:, :], b[2][:, 0:D], x1[r][:, :], ALU.add).then_inc(x2_ready, 1)
                elif stage == "mix2":
                    dve.wait_ge(mix2_psum, n + 1)
                    dve.wait_ge(x2_ready, n + 1)
                    if not first:
                        dve.wait_ge(x3_kept, n - 1)
                    dve.scalar_tensor_tensor(x3[r][:, :], b[3][:, 0:D], bias[:, bass.ds(n, 1)], x2[r][:, :],
                                             ALU.add, ALU.add).then_inc(x3_ready, 1)
                elif stage == "xf":
                    dve.wait_ge(xfhigh_ready, n + 1)
                    dve.tensor_tensor(xf_half(xf_low, r), x3_t[:, :, r, :], xf_half(xf_high, r).bitcast(F32),
                                      ALU.subtract).then_inc(xf_ready, 1)

            def h_low_part(m, f):
                dve.wait_ge(hhigh_ready, NF * m + f + 1)
                dve.tensor_tensor(h_low[:, f, :], hf[f % 2][:, :], h_high[:, f, :].bitcast(F32), ALU.subtract
                                  ).then_inc(h_ready, 1)

            def h_whole(m, f):
                b = FFN_BANKS[f % 3]
                at = NF * m + f + 1
                dve.wait_ge(tanh_ready, at)
                dve.scalar_tensor_tensor(gs[f % 2][:, :], th[f % 3][:, :], 1.0, b[:, 0:PAIR_TOK], ALU.add,
                                         ALU.mult).then_inc(gs_ready, 1)
                dve.wait_ge(gs_ready, at)
                dve.scalar_tensor_tensor(hf[f % 2][:, :], b[:, PAIR_TOK:], 0.5, gs[f % 2][:, :], ALU.mult,
                                         ALU.mult).then_inc(hf_ready, 1)

            def ffn(piece, m):
                if piece == "adapt":
                    dve.wait_ge(low_psum, m + 1)
                    for a in range(2):
                        last = dve.tensor_tensor(
                            low_raw[:, a * PAIR_TOK:(a + 1) * PAIR_TOK].rearrange("p (s t) -> p s t", t=T),
                            FFN_BANKS[3][:, a * PAIR_TOK:(a + 1) * PAIR_TOK].rearrange("p (s t) -> p s t", t=T),
                            over(adapt[:, bass.ds(2 * GB * m, 2 * GB)], 2, T), ALU.mult)
                    last.then_inc(lowraw_ready, 1)
                    dve.wait_ge(lowhigh_ready, m + 1)
                    dve.tensor_tensor(low_low[:, :], low_raw[:, :], low_high[:, :].bitcast(F32), ALU.subtract
                                      ).then_inc(low_ready, 1)
                if piece.startswith("up"):
                    f = int(piece[2:])
                    h_whole(m, f)
                    if f:
                        h_low_part(m, f - 1)
                elif piece == "down00":
                    h_low_part(m, NF - 1)
                elif piece == "down_lora1":
                    dve.wait_ge(lowd_psum, m + 1)
                    dve.tensor_tensor(lowd_raw[:, :].rearrange("p (s t) -> p s t", t=T),
                                      FFN_BANKS[0][:, 0:PAIR_TOK].rearrange("p (s t) -> p s t", t=T),
                                      over(adapt[:, bass.ds(2 * GB * m, 2 * GB)], 2, T), ALU.mult
                                      ).then_inc(lowdraw_ready, 1)
                    dve.wait_ge(lowdhigh_ready, m + 1)
                    dve.tensor_tensor(lowd_low[:, :], lowd_raw[:, :], lowd_high[:, :].bitcast(F32), ALU.subtract
                                      ).then_inc(lowd_ready, 1)
                elif piece == "tail2":
                    for r in R:
                        dve.wait_ge(down_psum, 2 * m + r + 1)
                        dve.wait_ge(x3_kept, 2 * m + r + 1)
                        dve.tensor_tensor(row(xs, 2 * m + r), FFN_BANKS[3 - r][:, 0:D], row(xs, 2 * m + r), ALU.add
                                          ).then_inc(y_ready, 1)

            def steps(order, m, pair):
                first_pair = order is START_ORDER
                for step in order:
                    if isinstance(step, str):
                        ffn(step, m)
                    elif step[0] == "mask":
                        make_mask(step[1], step[1])
                    elif step[0] == "next_mask":
                        make_mask(2 * m + 4 + step[1], step[1])
                    elif step[0] == "winner":
                        find_winners(step[1])
                    elif step[0] == "rows":
                        number_rows(1, NT)
                    elif step[0] == "split" and SPLITS[step[1]] == "dve":
                        take_low(dve, step[1])
                    elif step == ("rotate", 2):
                        rotate(2)
                    elif step == ("normalise", 2):
                        normalise(2)
                    elif step[0] == "move_v":
                        move_v(step[1])
                    elif step[0] == "shift":
                        dve.wait_ge(rows_in, 32)
                        shift_rows(B)
                    elif step[0] == "place":
                        dve.wait_ge(place_psum, 2)
                        dve.tensor_copy(far_i[:, B:], bank[0][:, 0:GB])
                        dve.tensor_copy(near_i[:, NG:], bank[0][:, B:B + 1])
                        dve.tensor_copy(far_i[:, BT:B], bank[0][:, BT:B]).then_inc(place_ready, 1)
                        dve.tensor_copy(near_i[:, 2:NG], bank[0][:, B + 2:B + NG]).then_inc(place_ready, 1)
                    elif step[0] in STAGES:
                        stage, r = step
                        attention(stage, 2 * m + 2 + r, r, HIGH_BANKS if first_pair and r else LOW_BANKS, pair)

            steps(START_ORDER, -1, 0)
            steps(FIRST_ORDER, 0, 1)
            with dve.Fori(1, NPAIR - 1) as m:
                steps(LOOP_ORDER, m, m + 1)
            for piece in FFN_PIECES:
                ffn(piece, NPAIR - 1)

        @block.tensor
        def _(pe):
            pe.wait_ge(sel_ready, 1)
            pe.wait_ge(ones_set, 2)
            o = NG + NT + 1
            pe.matmul(bank[0][:, 0:NG], c3("tok_b"), len_sel[:, 0:NG], start=True, stop=True)
            pe.matmul(bank[0][0:BP, NG:NG + NT], c3("blk_b"), len_sel[:, NG:NG + NT], start=True, stop=True)
            pe.matmul(bank[0][0:BP, NG + NT:o], c3("wrt_b"), len_f[:, :], start=True, stop=True)
            pe.matmul(bank[0][:, 16:16 + B], ones[0:B, :], len_sel[:, o:o + B], start=True, stop=True)
            pe.matmul(bank[0][:, 48:48 + B], ones[0:B, :], ad_sel[:, :], start=True, stop=True).then_inc(len_psum, 1)
            pe.wait_ge(k128_in, 16)
            pe.wait_ge(x_in, 16)
            for k in range(KD):
                for hf in range(2):
                    for g in range(4):
                        last = pe.transpose(bank[1 + 2 * k + hf][:, g * P:(g + 1) * P],
                                            xs[:, 4 * hf + g, k * P:(k + 1) * P], ident)
                    last.then_inc(xt_psum, 1)
            pe.wait_ge(wvkq_in, 48)
            for at, pieces in ((5, (wv_raw, wk_raw)), (6, (wq_raw[:, 0, :], wq_raw[:, 1, :]))):
                for k in range(KD):
                    for j, w in enumerate(pieces):
                        last = pe.transpose(bank[at][:, (2 * k + j) * P:(2 * k + j + 1) * P], w[:, k * P:(k + 1) * P],
                                            ident)
                last.then_inc(w_psum, 1)

            def turn_w_o():
                pe.wait_ge(wo_in, 64)
                for h in range(GS):
                    for a in range(2):
                        last = pe.transpose(bank[7][:, h * D + a * P:h * D + (a + 1) * P], wo_raw[:, a, h, :], ident)
                last.then_inc(w_psum, 1)

            def project(i, dst, cols, done):
                for t in range(2):
                    for k in range(KD):
                        last = pe.matmul(bank[dst][:, t * D:(t + 1) * D], x_t[:, k, 2 * i + t, :], w_vkq[:, k, cols],
                                         start=(k == 0), stop=(k == KD - 1))
                last.then_inc(done, 1)

            pe.wait_ge(xt_ready, 4)
            pe.wait_ge(w_ready, 2)
            for i in range(2):
                project(i, 1 + i, slice(0, KV), vk_psum)
            pe.wait_ge(diag_ready, 1)
            for n in range(3):
                last = pe.matmul(bank[5 + n][0:BP, :], ones16[:, :],
                                 wr_diag[:, :, :].rearrange("p o w -> p (o w)")[:, 512 * n:512 * (n + 1)],
                                 start=True, stop=True)
            last.then_inc(wr_psum, 1)
            for i in range(2, 4):
                project(i, 1 + i, slice(0, KV), vk_psum)
            pe.wait_ge(widsel_ready, 1)
            pe.matmul(bank[0][0:BP, 0:NW], ones[0:BP, 0:BP], wid_sel[:, :, :].rearrange("p t w -> p (t w)"),
                      start=True, stop=True).then_inc(wid_psum, 1)
            pe.wait_ge(wr_ready, 3)
            project(0, 5, slice(KV, 512), q_psum)
            turn_w_o()
            project(1, 6, slice(KV, 512), q_psum)
            pe.wait_ge(vk_ready, 2)
            project(2, 1, slice(KV, 512), q_psum)
            project(3, 2, slice(KV, 512), q_psum)

            def turn_q(i):
                for t in range(2):
                    for h in range(GS):
                        last = pe.transpose(bank[3 + i][:, (t * GS + h) * P:(t * GS + h + 1) * P],
                                            (q_rot_last[:, 2 * i - 2 + t, h, :] if i else q_rot_first[:, t, h, :]), ident)
                last.then_inc(qt_psum, 1)

            def place(ns, with_bias):
                n = ns // GB
                pe.transpose(bank[0][:, 0:ns], row_b[0:ns, 0:P], ident[0:ns, 0:ns])
                for s in range(GB):
                    q = slice(s * T, (s + 1) * T)
                    sel = c3("group")[:, s * NG:(s + 1) * NG]
                    last = pe.matmul(bank[0][q, B:B + n], row_b[0:ns, P:SPAN], sel[0:ns, 0:n], start=True, stop=True,
                                     tile_position=(0, s * T))
                    if with_bias:
                        last = pe.matmul(bank[0][q, B + NG:B + 2 * NG], side_b[:, :], sel, start=True, stop=True,
                                         tile_position=(0, s * T))
                last.then_inc(place_psum, 1)

            pe.wait_ge(shift_ready, 1)
            pe.wait_ge(side_in, 16)
            place(BT, True)
            pe.wait_ge(vk_ready, 4)
            pe.wait_ge(job_done, 2)
            turn_q(0)
            pe.wait_ge(q_ready, 4)
            pe.wait_ge(place_ready, 3)
            pe.wait_ge(w_ready, 3)

            def attention(stage, n, r, b, pair):
                first = isinstance(pair, int) and pair == 0
                if stage == "kt":
                    pe.wait_ge(kv_in[r], (pair + 1) * (GB + 1) * 16)
                    if first:
                        pe.wait_ge(qt_ready, NPAIR if r else 1)
                    else:
                        pe.wait_ge(x3t_ready, n)
                    for s in range(GB):
                        pe.transpose(b[0][:, s * P:(s + 1) * P], far[r][:, s, 0:G * HD], ident)
                    pe.transpose(b[1][:, 0:P], near[r][:, 0:G * HD], ident).then_inc(kt_psum, 1)
                elif stage == "scores":
                    pe.wait_ge(far_kt_ready, n + 1)
                    pe.wait_ge(near_kt_ready, n + 1)
                    pe.wait_ge(qbd_ready, 2 * n + 2)
                    for half in range(2):
                        for s in range(2):
                            for c in range(2):
                                q = slice(64 * c, 64 * c + 64)
                                last = pe.matmul(b[(2, 0)[half] + c][:, s * SPAN:(s + 1) * SPAN],
                                                 q_bd[r][q, 2 * half + s, :, :, :].rearrange("p g h t -> p (g h t)"),
                                                 k_t[r][q, 2 * half + s, :], start=True, stop=True)
                        last.then_inc(scores_psum, 1)
                elif stage in ("pt0", "pt1"):
                    half = int(stage[2])
                    pe.wait_ge(prob_ready, 4 * n + 2 * half + 1)
                    for j in range(4):
                        last = pe.transpose(b[2 + half][:, j * P:(j + 1) * P],
                                            prob[r][:, 2 * half + j // 2, j % 2, 0:P], ident)
                    last.then_inc(pfar_psum, 1)
                    if half:
                        pe.wait_ge(prob_ready, 4 * n + 4)
                        for c in range(2):
                            last = pe.transpose(b[0][:, c * P:(c + 1) * P],
                                                prob_near[r][:, c, :, :].rearrange("p s i -> p (s i)"), ident)
                        last.then_inc(pnear_psum, 1)
                elif stage == "pv":
                    pe.wait_ge(pfar0_ready, n + 1)
                    pe.wait_ge(pfar1_ready, n + 1)
                    pe.wait_ge(pnear_ready, n + 1)
                    for s in range(GB):
                        for v_rows, pr, st in ((far[r][:, s, :], p_far[r], True), (near[r][:, :], p_near[r], False)):
                            for g in range(G):
                                last = pe.matmul(b[1][g * HD:(g + 1) * HD, s * 2 * T:(s + 1) * 2 * T],
                                                 v_rows[:, G * HD + g * HD:G * HD + (g + 1) * HD],
                                                 pr[:, s, g * 2 * T:(g + 1) * 2 * T], start=st, stop=not st,
                                                 tile_position=(0, g * HD))
                    last.then_inc(o_psum, 1)
                elif stage == "wo":
                    pe.wait_ge(o_ready, n + 1)
                    for h in range(GS):
                        last = pe.matmul(b[0][:, 0:D], o_t[r][:, h, :, :].rearrange("p s t -> p (s t)"), w_o[:, h, :],
                                         start=(h == 0), stop=(h == GS - 1))
                    last.then_inc(wo_psum, 1)
                elif stage == "mix1":
                    pe.wait_ge(x1_ready, n + 1)
                    pe.wait_ge(wmix_ready, 2 * n + 2)
                    pe.matmul(b[2][:, 0:D], w_mix[r][:, 0, :, :].rearrange("p s d -> p (s d)"), x1[r][:, :],
                              start=True, stop=True).then_inc(mix1_psum, 1)
                elif stage == "mix2":
                    pe.wait_ge(x2_ready, n + 1)
                    pe.matmul(b[3][:, 0:D], w_mix[r][:, 1, :, :].rearrange("p s d -> p (s d)"), x2[r][:, :],
                              start=True, stop=True).then_inc(mix2_psum, 1)
                elif stage == "xt":
                    pe.wait_ge(x3_ready, n + 1)
                    for k in range(KD):
                        last = pe.transpose(b[0][:, k * P:(k + 1) * P], x3[r][:, k * P:(k + 1) * P], ident)
                    last.then_inc(x3t_psum, 1)

            def product(dst, w, x, start, stop):
                for n, (a, b) in enumerate(((0, 0), (0, 1), (1, 0))):
                    last = pe.matmul(dst, w[a], x[b], start=start and n == 0, stop=stop and n == 2)
                return last

            def base_product(a, f):
                for k in range(KD):
                    product(FFN_BANKS[f % 3][:, a * PAIR_TOK:(a + 1) * PAIR_TOK],
                            [w[:, a, k, f * P:(f + 1) * P] for w in w_gu], [x[:, k, :] for x in m_xf], k == 0, False)

            def ffn(piece, m):
                if piece == "lora":
                    pe.wait_ge(xf_ready, 2 * m + 2)
                    if not (isinstance(m, int) and m == 0):
                        pe.wait_ge(y_ready, 2 * m - 1)
                    for a in range(2):
                        for k in range(KD):
                            last = product(FFN_BANKS[3][:, a * PAIR_TOK:(a + 1) * PAIR_TOK],
                                           [w[:, a, k, :] for w in w_a], [x[:, k, :] for x in m_xf],
                                           k == 0, k == KD - 1)
                    last.then_inc(low_psum, 1)
                elif piece.startswith("gate") or piece.startswith("up"):
                    a = int(piece.startswith("up"))
                    f = int(piece[-1])
                    if piece == "gate0":
                        for n in range(3):
                            if n == 2 and not (isinstance(m, int) and m == 0):
                                pe.wait_ge(y_ready, 2 * m)
                            base_product(0, n)
                        pe.wait_ge(low_ready, m + 1)
                    elif a == 0 and f >= 3:
                        pe.wait_ge(hf_ready, NF * m + f - 2)
                        base_product(0, f)
                    elif a:
                        base_product(1, f)
                    last = product(FFN_BANKS[f % 3][:, a * PAIR_TOK:(a + 1) * PAIR_TOK],
                                   [w[:, a, f * P:(f + 1) * P] for w in w_b], [x[:, a, :] for x in m_low], False, True)
                    if a:
                        last.then_inc(gu_psum, 1)
                elif piece.startswith("down_lora"):
                    if piece[-1] == "0":
                        pe.wait_ge(h_ready, NF * m + NF)
                    half = int(piece[-1])
                    for k in range(half * NF // 2, (half + 1) * NF // 2):
                        last = product(FFN_BANKS[0][:, 0:PAIR_TOK], [w[:, k, :] for w in w_ad],
                                       [x[:, k, :] for x in m_h], k == 0, k == NF - 1)
                    if half:
                        last.then_inc(lowd_psum, 1)
                elif piece in ("tail0", "tail1"):
                    for k in range(NF - 2, NF):
                        down(int(piece[4]), k)
                elif piece == "tail2":
                    pe.wait_ge(lowd_ready, m + 1)
                    for r in R:
                        product(FFN_BANKS[3 - r][:, 0:D], [x[:, r * P:(r + 1) * P] for x in m_lowd],
                                w_bd, False, True).then_inc(down_psum, 1)
                elif piece.startswith("down"):
                    r, third = int(piece[4]), int(piece[5])
                    if r == 0:
                        pe.wait_ge(h_ready, NF * m + 3 * third + 3)
                    for k in range(3 * third, 3 * third + 3):
                        down(r, k)

            def down(r, k):
                product(FFN_BANKS[3 - r][:, 0:D], [x[:, k, r * P:(r + 1) * P] for x in m_h],
                        [w[:, k, :] for w in w_d], k == 0, False)

            def steps(order, m, pair):
                first_pair = order is START_ORDER
                for step in order:
                    if isinstance(step, str):
                        ffn(step, m)
                    elif step == ("normalise", 2):
                        pe.wait_ge(job_done, 3)
                        for i in range(1, NPAIR):
                            turn_q(i)
                    elif step[0] == "use":
                        pe.wait_ge(split_ready[step[1]], 1)
                    elif step[0] == "warm":
                        for n in range(step[1]):
                            pe.transpose(bank[step[2]][:, 0:P], ident, ident)
                    elif step[0] == "place":
                        pe.wait_ge(shift_ready, 2)
                        pe.wait_ge(x3t_ready, 1)
                        place(B, False)
                        pe.wait_ge(place_ready, 5)
                    elif step[0] in STAGES:
                        stage, r = step
                        attention(stage, 2 * m + 2 + r, r, HIGH_BANKS if first_pair and r else LOW_BANKS, pair)

            steps(START_ORDER, -1, 0)
            steps(FIRST_ORDER, 0, 1)
            with pe.Fori(1, NPAIR - 1) as m:
                steps(LOOP_ORDER, m, m + 1)
            for piece in FFN_PIECES:
                ffn(piece, NPAIR - 1)


NAMES = [("x", "x"), ("itok_Bx257_0_4111", "table"), ("itok_B_37_3939", "lens"), ("itok_B_1_198", "cond"),
         ("itok_B_0_7", "subj"), ("fside_8xS_0", "side"), ("L0_cond_Wq", "Wq"), ("L0_cond_Wk", "Wk"),
         ("L0_cond_Wv", "Wv"), ("L0_cond_Wo", "Wo"), ("L0_cond_q_norm_scale", "qs"), ("L0_cond_k_norm_scale", "ks"),
         ("L0_cond_k_blocks", "kb"), ("L0_cond_v_blocks", "vb"), ("L1_cond_weights", "w1"), ("L2_cond_weights", "w2"),
         ("L3_cond_Wg", "Wg"), ("L3_cond_Wu", "Wu"), ("L3_cond_Wd", "Wd"), ("L3_cond_Ag", "Ag"),
         ("L3_cond_Bg", "Bg"), ("L3_cond_Au", "Au"), ("L3_cond_Bu", "Bu"), ("L3_cond_Ad", "Ad"), ("L3_cond_Bd", "Bd")]


def kernel(**inputs):
    import concourse.bacc as bacc
    from concourse.bass_utils import run_bass_kernel_spmd

    nc = bacc.Bacc("TRN2", target_bir_lowering=False, num_devices=1)
    arrays, args = {}, {}

    def give(name, a):
        a = np.ascontiguousarray(a)
        arrays[f"in_{name}"] = a
        args[name] = nc.dram_tensor(f"in_{name}", a.shape, mybir.dt.from_np(a.dtype), kind="ExternalInput").ap()

    for name, short in NAMES:
        give(short, inputs[name])
    for name, a in zip(("c128", "c96", "c32"), tables()):
        give(name, a)
    args["out"] = nc.dram_tensor("out", (B, T, D), F32, kind="ExternalOutput").ap()
    build(nc, **args)
    r = run_bass_kernel_spmd(nc, [arrays], core_ids=[0])
    return r.results[0]["out"]
```
